# Optimizing a Trainium2 kernel written in Bass

```python
import numpy as np
import jax
import jax.numpy as jnp

def _softmax(x, axis=-1):
    return jax.nn.softmax(x, axis=axis)

def _gelu(x):
    return jax.nn.gelu(x, approximate=True)

def _silu(x):
    return jax.nn.silu(x)

def _sigmoid(x):
    return jax.nn.sigmoid(x)

def _layernorm(x, axis=-1, eps=1e-05):
    m = jnp.mean(x, axis=axis, keepdims=True)
    v = jnp.var(x, axis=axis, keepdims=True)
    return (x - m) / jnp.sqrt(v + eps)

def _scatter_add(tgt, idx, src, axis=0):
    return tgt.at[idx].add(src)

def _segment_sum(src, seg, n):
    return jax.ops.segment_sum(src, seg, n)
kernel_name = 'mk_flamingo_gated_d1_seqx_r8_020953'

def setup_inputs(seed: int=0):
    np.random.seed(seed)
    _w = jnp.asarray

    def _rec_inputs():
        import jax
        import jax.numpy as jnp
        _rk = jax.random.key(seed)
        x = -0.0005146 + 1 * jax.random.normal(jax.random.fold_in(_rk, 1), (2, 512, 128), jnp.float32)
        _lenS = 512 - jax.random.randint(jax.random.fold_in(_rk, 7), (2,), 0, max(1, 512 // 4) + 1, jnp.int32)
        _lenS2 = 32 - jax.random.randint(jax.random.fold_in(_rk, 8), (2,), 0, max(1, 32 // 4) + 1, jnp.int32)
        _ctx_1024P = jax.random.normal(jax.random.fold_in(_rk, 11), (2, 16, 128), jnp.float32)
        _ctx_1024c = jax.random.dirichlet(jax.random.fold_in(_rk, 511), 0.3 * jnp.ones((16,), jnp.float32), (2, 32))
        _ctx_1024t = jnp.einsum('bsk,bkd->bsd', _ctx_1024c, _ctx_1024P)
        _ctx_1024t = _ctx_1024t * jax.lax.rsqrt(jnp.mean(jnp.square(_ctx_1024t)) + 1e-12) * 0.953939
        ctx_1024 = -0.000392918 + 0.999932 * (_ctx_1024t + 0.3 * jax.random.normal(jax.random.fold_in(_rk, 611), (2, 32, 128), jnp.float32))
        _validS = jnp.arange(512)[None, :] < _lenS[:, None]
        _validS2 = jnp.arange(32)[None, :] < _lenS2[:, None]
        _causal = jnp.tril(jnp.ones((512, 512), dtype=bool))
        mask_BxS2_bf1 = jnp.ones((2, 32), dtype=bool)
        _g = jax.random.normal(jax.random.fold_in(_rk, 9001), (2, 1), jnp.float32)
        _g = jnp.sign(_g) * jnp.maximum(jnp.abs(_g), 1.0) + (_g == 0) * 1.0
        g_xattn = _g[0]
        g_ffn = _g[1]
        return (x, ctx_1024, mask_BxS2_bf1, g_xattn, g_ffn)
    x, ctx_1024, mask_BxS2_bf1, g_xattn, g_ffn = _rec_inputs()

    def _L0_xattn_setup():
        import jax, jax.numpy as jnp
        import numpy as np
        DIM = 128
        DIM_LATENT = 128
        DIM_HEAD = 64
        HEADS = 16
        INNER = HEADS * DIM_HEAD

        def layernorm(x, g, b, eps=1e-05):
            m = jnp.mean(x, axis=-1, keepdims=True)
            v = jnp.mean((x - m) ** 2, axis=-1, keepdims=True)
            return (x - m) / jnp.sqrt(v + eps) * g + b

        def rmsnorm(x, gamma, eps=1e-08):
            n = jnp.linalg.norm(x, axis=-1, keepdims=True) * x.shape[-1] ** (-0.5)
            return x / jnp.maximum(n, eps) * gamma
        key = jax.random.key(seed)
        ks = jax.random.split(key, 8)
        b, n, m = (4, 512, 64)
        x = jax.random.normal(ks[0], (b, n, DIM), dtype=jnp.float32)
        latents = jax.random.normal(ks[1], (b, m, DIM_LATENT), dtype=jnp.float32)
        mask = jnp.ones((b, n), dtype=bool)
        s = 0.02
        return {'x': x, 'latents': latents, 'mask': mask, 'ln_x_g': jnp.ones((DIM,), jnp.float32), 'ln_x_b': jnp.zeros((DIM,), jnp.float32), 'ln_l_g': jnp.ones((DIM_LATENT,), jnp.float32), 'ln_l_b': jnp.zeros((DIM_LATENT,), jnp.float32), 'qn_g': jnp.ones((DIM_HEAD,), jnp.float32), 'kn_g': jnp.ones((DIM_HEAD,), jnp.float32), 'Wq': jax.random.normal(ks[2], (DIM_LATENT, INNER), jnp.float32) * s, 'Wkv': jax.random.normal(ks[3], (DIM, 2 * INNER), jnp.float32) * s, 'Wout': jax.random.normal(ks[4], (INNER, DIM_LATENT), jnp.float32) * s, 'bout': jnp.zeros((DIM_LATENT,), jnp.float32)}
    _L0_xattn_all = _L0_xattn_setup()
    _L0_xattn_in = {k: v for k, v in _L0_xattn_all.items() if k in ('ln_x_g', 'ln_x_b', 'ln_l_g', 'ln_l_b', 'qn_g', 'kn_g', 'Wq', 'Wkv', 'Wout', 'bout')}
    del _L0_xattn_all

    def _L0_ffn_setup():
        import jax, jax.numpy as jnp
        import numpy as np
        TOP_K = 2
        key = jax.random.key(seed)
        ks = jax.random.split(key, 5)
        B, T, D, E, F = (2, 256, 128, 8, 256)
        scale_d = 1.0 / np.sqrt(D)
        scale_f = 1.0 / np.sqrt(F)
        return {'x': jax.random.normal(ks[0], (B, T, D), jnp.float32), 'kernel_router_DE': jax.random.normal(ks[1], (D, E), jnp.float32) * scale_d, 'kernel_gating_EDF': jax.random.normal(ks[2], (E, D, F), jnp.float32) * scale_d, 'kernel_up_EDF': jax.random.normal(ks[3], (E, D, F), jnp.float32) * scale_d, 'kernel_down_EFD': jax.random.normal(ks[4], (E, F, D), jnp.float32) * scale_f}
    _L0_ffn_all = _L0_ffn_setup()
    _L0_ffn_in = {k: v for k, v in _L0_ffn_all.items() if k in ('kernel_router_DE', 'kernel_gating_EDF', 'kernel_up_EDF', 'kernel_down_EFD')}
    del _L0_ffn_all
    return {'x': x, 'ctx_1024': ctx_1024, 'mask_BxS2_bf1': mask_BxS2_bf1, 'g_xattn': g_xattn, 'g_ffn': g_ffn, 'L0_xattn_ln_x_g': _L0_xattn_in['ln_x_g'], 'L0_xattn_ln_x_b': _L0_xattn_in['ln_x_b'], 'L0_xattn_ln_l_g': _L0_xattn_in['ln_l_g'], 'L0_xattn_ln_l_b': _L0_xattn_in['ln_l_b'], 'L0_xattn_qn_g': _L0_xattn_in['qn_g'], 'L0_xattn_kn_g': _L0_xattn_in['kn_g'], 'L0_xattn_Wq': _L0_xattn_in['Wq'], 'L0_xattn_Wkv': _L0_xattn_in['Wkv'], 'L0_xattn_Wout': _L0_xattn_in['Wout'], 'L0_xattn_bout': _L0_xattn_in['bout'], 'L0_ffn_kernel_router_DE': _L0_ffn_in['kernel_router_DE'], 'L0_ffn_kernel_gating_EDF': _L0_ffn_in['kernel_gating_EDF'], 'L0_ffn_kernel_up_EDF': _L0_ffn_in['kernel_up_EDF'], 'L0_ffn_kernel_down_EFD': _L0_ffn_in['kernel_down_EFD']}

def reference(x, ctx_1024, mask_BxS2_bf1, g_xattn, g_ffn, L0_xattn_ln_x_g, L0_xattn_ln_x_b, L0_xattn_ln_l_g, L0_xattn_ln_l_b, L0_xattn_qn_g, L0_xattn_kn_g, L0_xattn_Wq, L0_xattn_Wkv, L0_xattn_Wout, L0_xattn_bout, L0_ffn_kernel_router_DE, L0_ffn_kernel_gating_EDF, L0_ffn_kernel_up_EDF, L0_ffn_kernel_down_EFD):
    import jax
    import jax.numpy as jnp

    def _L0_xattn_ref(x, latents, mask, ln_x_g, ln_x_b, ln_l_g, ln_l_b, qn_g, kn_g, Wq, Wkv, Wout, bout):
        import jax, jax.numpy as jnp
        import numpy as np
        DIM = 128
        DIM_LATENT = 128
        DIM_HEAD = 64
        HEADS = 16
        INNER = HEADS * DIM_HEAD

        def layernorm(x, g, b, eps=1e-05):
            m = jnp.mean(x, axis=-1, keepdims=True)
            v = jnp.mean((x - m) ** 2, axis=-1, keepdims=True)
            return (x - m) / jnp.sqrt(v + eps) * g + b

        def rmsnorm(x, gamma, eps=1e-08):
            n = jnp.linalg.norm(x, axis=-1, keepdims=True) * x.shape[-1] ** (-0.5)
            return x / jnp.maximum(n, eps) * gamma
        b, n, _ = x.shape
        m = latents.shape[1]
        h, d = (HEADS, DIM_HEAD)
        scale = d ** (-0.5)
        xn = layernorm(x, ln_x_g, ln_x_b)
        ln = layernorm(latents, ln_l_g, ln_l_b)
        q = (ln @ Wq).reshape(b, m, h, d).transpose(0, 2, 1, 3)
        kv = jnp.concatenate([xn @ Wkv, ln @ Wkv], axis=1)
        kv = kv.reshape(b, n + m, 2, h, d)
        k = kv[:, :, 0].transpose(0, 2, 1, 3)
        v = kv[:, :, 1].transpose(0, 2, 1, 3)
        qn = rmsnorm(q, qn_g) * scale
        kn = rmsnorm(k, kn_g)
        sim = jnp.einsum('bhid,bhjd->bhij', qn, kn)
        max_neg = -jnp.finfo(sim.dtype).max
        padded_mask = jnp.concatenate([mask, jnp.ones((b, m), bool)], axis=1)
        sim = jnp.where(padded_mask[:, None, None, :], sim, max_neg)
        attn = jax.nn.softmax(sim.astype(jnp.float32), axis=-1).astype(sim.dtype)
        out = jnp.einsum('bhij,bhjd->bhid', attn, v)
        out = out.transpose(0, 2, 1, 3).reshape(b, m, h * d)
        return out @ Wout + bout

    def _L0_ffn_ref(x, kernel_router_DE, kernel_gating_EDF, kernel_up_EDF, kernel_down_EFD):
        import jax, jax.numpy as jnp
        import numpy as np
        TOP_K = 2
        E = kernel_router_DE.shape[-1]
        x = x.astype(jnp.float32)
        router_logits_BTE = jnp.einsum('BTD,DE->BTE', x, kernel_router_DE)
        probs_BTE = jax.nn.softmax(router_logits_BTE.astype(jnp.float32), axis=-1)
        weights_BTX, indices_BTX = jax.lax.top_k(probs_BTE, TOP_K)
        norm_weights_BTX = jax.nn.softmax(weights_BTX, axis=-1)
        one_hot_BTXE = jax.nn.one_hot(indices_BTX, num_classes=E, dtype=jnp.float32)
        full_weights_BTE = jnp.sum(one_hot_BTXE * norm_weights_BTX[..., None], axis=2)
        gating_BTEF = jnp.einsum('BTD,EDF->BTEF', x, kernel_gating_EDF)
        fuse_BTEF = jax.nn.silu(gating_BTEF) * jnp.einsum('BTD,EDF->BTEF', x, kernel_up_EDF)
        down_BTED = jnp.einsum('BTEF,EFD->BTED', fuse_BTEF, kernel_down_EFD)
        out_BTD = jnp.einsum('BTED,BTE->BTD', down_BTED, full_weights_BTE)
        return out_BTD.astype(jnp.float32)
    x = x + jnp.tanh(g_xattn[0]) * _L0_xattn_ref(ctx_1024, _layernorm(x, axis=-1), mask_BxS2_bf1, L0_xattn_ln_x_g, L0_xattn_ln_x_b, L0_xattn_ln_l_g, L0_xattn_ln_l_b, L0_xattn_qn_g, L0_xattn_kn_g, L0_xattn_Wq, L0_xattn_Wkv, L0_xattn_Wout, L0_xattn_bout)
    x = x + jnp.tanh(g_ffn[0]) * _L0_ffn_ref(_layernorm(x, axis=-1), L0_ffn_kernel_router_DE, L0_ffn_kernel_gating_EDF, L0_ffn_kernel_up_EDF, L0_ffn_kernel_down_EFD)
    return x

_drawn_inputs = setup_inputs


def setup_inputs(seed=0):
    import zlib

    import numpy as np

    out = dict(_drawn_inputs(seed))
    spreads = {'L0_xattn_ln_x_g': (1.0, 0.6),
     'L0_xattn_ln_x_b': (0.0, 0.631),
     'L0_xattn_ln_l_g': (1.0, 0.2),
     'L0_xattn_ln_l_b': (0.0, 0.1),
     'L0_xattn_qn_g': (1.0, 0.6),
     'L0_xattn_kn_g': (1.0, 0.6),
     'L0_xattn_bout': (0.0, 0.1)}
    factors = {'ctx_1024': 2.868}
    for name, (base, spread) in spreads.items():
        noise = np.random.default_rng([zlib.crc32(name.encode()), seed]).standard_normal(out[name].shape)
        drawn = base * np.exp(spread * noise) if base else spread * noise
        out[name] = jnp.asarray(drawn.astype(out[name].dtype))
    for name, factor in factors.items():
        out[name] = (out[name] * factor).astype(out[name].dtype)
    return out
```

```python
from contextlib import ExitStack

import concourse.bass as bass
from concourse import mybir

P = 128
F32 = mybir.dt.float32
F32R = mybir.dt.float32r
F16 = mybir.dt.float16
BF16 = mybir.dt.bfloat16
U8 = mybir.dt.uint8
ALU = mybir.AluOpType
ACT = mybir.ActivationFunctionType
AX_X = mybir.AxisListType.X

LN_EPS = 1e-5
RMS_EPS = 1e-8
V_SCALE = 32.0
MASKED = 1e30


def flamingo_gated_block(nc, x, ctx_in, mask, g_xattn, g_ffn, ln_x_g, ln_x_b, ln_l_g, ln_l_b, qn_g, kn_g,
                         Wq, Wkv, Wout, bout, router, w_gate, w_up, w_down, out):
    B, N, D = x.shape
    C = ctx_in.shape[1]
    DH = qn_g.shape[0]
    INNER = Wq.shape[1]
    H = INNER // DH
    HG = 4
    NG = H // HG
    GC = HG * DH
    QT = N // P
    T = B * QT
    KEYS = N + C
    UNIT = QT * HG
    UNITS = B * NG
    ITEMS = UNITS * UNIT
    PER = B * UNIT
    KSTEPS = HG + 1
    TILES = QT + 1
    E, _, F = w_gate.shape
    FC = F // P
    W3 = 3 * GC

    with ExitStack() as ctx:
        def sb(name, shape, dt):
            return ctx.enter_context(nc.sbuf_tensor(name, shape, dt))

        def ps(name, shape, dt):
            return ctx.enter_context(nc.psum_tensor(name, shape, dt))

        def sem(name):
            return ctx.enter_context(nc.semaphore(name))

        scores = [ps(f"scores{k}", [P, 1024], F32) for k in range(2)]
        turned = ps("turned", [P, 512], F32)
        attn_o = ps("attn_o", [P, 512], F32)
        proj_qk = ps("proj_qk", [P, 512], F32)
        proj_v = ps("proj_v", [P, 512], F32)

        x_sb = sb("x_sb", [P, T, D], F32)
        ctx_sb = sb("ctx_sb", [B * C, D], F32)
        gains = sb("gains", [P, 4], F32)
        head_gains = sb("head_gains", [P, 2, DH], F32)
        head_gain = sb("head_gain", [P, DH], F32)
        bout_b = sb("bout_b", [P, D], F32)
        gates = sb("gates", [P, 2], F32)
        gates_t = sb("gates_t", [P, 2], F32)
        mask_u8 = sb("mask_u8", [1, B * C], U8)
        mask_row = sb("mask_row", [1, B * C], BF16)
        ones_row = sb("ones_row", [1, P], BF16)
        ident = sb("ident", [P, P], F32)
        ident_h = sb("ident_h", [P, P], F16)
        falling = sb("falling", [P, E], F32)
        wqkv = sb("wqkv", [P, NG * W3], F32)
        wqkv_hi = sb("wqkv_hi", [P, NG * W3], F32R)
        wqkv_lo = sb("wqkv_lo", [P, NG * W3], F32R)
        wout = sb("wout", [P, H // 2, D], F32)
        wr = sb("wr", [P, E], F32)
        wr_hl = sb("wr_hl", [P, 2, E], F32R)
        wg = sb("wg", [P, E * F], F32)
        wu = sb("wu", [P, E * F], F32)
        wd = sb("wd", [P, E * FC * D], F32)

        stats = sb("stats", [P, T + 1, 6], F32)
        moments = sb("moments", [P, T + 1, 2], F32)
        ln_v = sb("ln_v", [P, 8, QT], F32)
        ln_l = sb("ln_l", [P, 8, QT], F32)
        ln_e = sb("ln_e", [P, 8, QT], F32)
        ln_t = sb("ln_t", [P, 8, 3, QT], F32)
        ln_r = sb("ln_r", [P, 8, QT], F32)
        ln_s = sb("ln_s", [P, T], F32)
        z = sb("z", [P, T + 1, D], F32)
        lnT = sb("lnT", [P, B * N + B * C], F32)
        LNW = B * N + (B - 1) * C + P
        lnT_hi = sb("lnT_hi", [P, LNW], F32R)
        lnT_lo = sb("lnT_lo", [P, LNW], F32R)

        squares = [sb(f"squares{k}", [P, 512], F32) for k in range(2)]
        sumsq = sb("sumsq", [P, 2, 8], F32)
        meansq = sb("meansq", [P, 2, 8], F32)
        rms_l = sb("rms_l", [P, 2, 8], F32)
        rms_e = sb("rms_e", [P, 2, 8], F32)
        rms_t = sb("rms_t", [P, 2, 3, 8], F32)
        rms_r = sb("rms_r", [P, 2, 8], F32)
        qk = [sb(f"qk{k}", [P, 512], F32) for k in range(2)]
        qk_hl = [sb(f"qk_hl{k}", [P, 8, 2, DH], F16) for k in range(2)]
        v_ctx = [sb(f"v_ctx{k}", [C, HG, 2, DH], F16) for k in range(B)]
        q_st = [sb(f"q_st{k}", [P, HG, N], F16) for k in range(B)]
        k_st = [sb(f"k_st{k}", [P, HG, KEYS], F16) for k in range(B)]
        k_sw = [sb(f"k_sw{k}", [P, HG, KEYS], F16) for k in range(B)]
        v_hl = [sb(f"v_hl{k}", [P, 2, QT, GC], F16) for k in range(B)]
        v_bd = [sb(f"v_bd{k}", [P, 2, GC], F16) for k in range(B)]

        NM, SUMS, RAW, SPLIT = 4, 4, 4, 4
        neg_max = sb("neg_max", [P, NM], F32)
        sums = sb("sums", [P, SUMS, HG], F32)
        sums_s = sb("sums_s", [P, 2, HG], F32)
        inv_sums = sb("inv_sums", [P, 2, HG], F32)
        probs = [sb(f"probs{k}", [P, HG, KEYS], F32) for k in range(2)]
        probs_c = [sb(f"probs_c{k}", [P, HG * C], F32) for k in range(2)]
        p_raw = [sb(f"p_raw{k}", [P, 512], F32) for k in range(RAW)]
        p_hi = [sb(f"p_hi{k}", [P, 512], F16) for k in range(SPLIT)]
        p_lo = [sb(f"p_lo{k}", [P, 512], F16) for k in range(SPLIT)]
        o_sb = sb("o_sb", [P, T * INNER], F32)

        oT = [q_st[k][:, :, :].rearrange("p h n -> p (h n)").bitcast(F32) for k in range(2)]
        spare = [probs[k][:, :, :].rearrange("p h n -> p (h n)") for k in range(2)]
        x1 = spare[0][:, 0:T * D].rearrange("p (t d) -> p t d", t=T)
        x1_t = spare[0][:, T * D:(T + 2) * D].rearrange("p (t d) -> p t d", t=2)
        x2T_hi = lnT_hi
        x2T_lo = lnT_lo
        x2T = lnT
        rt = k_st[0][:, :, :].rearrange("p h n -> p (h n)").bitcast(F32)[:, 0:16 * T * E].rearrange(
            "p (s t e) -> p s t e", s=16, t=T)
        rs = sb("rs", [P, 8, T], F32)
        w_tok = sb("w_tok", [P, T, E], F32)
        wgu_hi = [wqkv_hi[:, 2 * F * k:2 * F * (k + 1)] for k in range(2)]
        wgu_lo = [wqkv_lo[:, 2 * F * k:2 * F * (k + 1)] for k in range(2)]
        th = [p_raw[k] for k in range(2)]
        gt = [p_raw[2 + k] for k in range(2)]
        hid = [spare[1][:, 512 * k:512 * (k + 1)] for k in range(2)]

        x_in, ctx_inn, gains_in = sem("x_in"), sem("ctx_inn"), sem("gains_in")
        x_in2 = sem("x_in2")
        w0_in, w_in, rest_in, moe_in = sem("w0_in"), sem("w_in"), sem("rest_in"), sem("moe_in")
        const_z, const_ok, ident_h_ok = sem("const_z"), sem("const_ok"), sem("ident_h_ok")
        mask_ok, mask_f = sem("mask_ok"), sem("mask_f")
        head_gain_ok = sem("head_gain_ok")
        whi_ok, wlo_ok = sem("whi_ok"), sem("wlo_ok")
        bn_ok, var_ok, lnl_ok, lne_ok, newton = sem("bn_ok"), sem("var_ok"), sem("lnl_ok"), sem("lne_ok"), sem("newton")
        z_ok, zT_ok, lnT_ok, lnhi_ok, lnlo_ok = sem("z_ok"), sem("zT_ok"), sem("lnT_ok"), sem("lnhi_ok"), sem("lnlo_ok")
        qk_mm, sq_ok, ss_ok, ms_ok, rl_ok, re_ok = (sem(n) for n in
                                                   ("qk_mm", "sq_ok", "ss_ok", "ms_ok", "rl_ok", "re_ok"))
        rms_step, norm_ok, gain_ok, qkhi_ok, qklo_ok = (sem(n) for n in
                                                        ("rms_step", "norm_ok", "gain_ok", "qkhi_ok", "qklo_ok"))
        qkT_ok, qkst_ok, v_mm, vhi_ok, vlo_ok = (sem(n) for n in ("qkT_ok", "qkst_ok", "v_mm", "vhi_ok", "vlo_ok"))
        ksw_ok, vbd_ok = sem("ksw_ok"), sem("vbd_ok")
        s_ok, max_ok, exp_ok, pT_ok, raw_ok, phi_ok, plo_ok, pv_ok = (sem(n) for n in (
            "s_ok", "max_ok", "exp_ok", "pT_ok", "raw_ok", "phi_ok", "plo_ok", "pv_ok"))
        pack_ok, den_ok, o_ok = sem("pack_ok"), sem("den_ok"), sem("o_ok")
        oT_mm, oTa_ok, oTv_ok, y_mm, x1t_ok, x1_ok = (sem(n) for n in
                                                      ("oT_mm", "oTa_ok", "oTv_ok", "y_mm", "x1t_ok", "x1_ok"))
        gate_ok, wr_ok = sem("gate_ok"), sem("wr_ok")
        z2_ok, z2T_ok, x2T_ok, x2hi_ok, x2lo_ok, logit_ok = (sem(n) for n in (
            "z2_ok", "z2T_ok", "x2T_ok", "x2hi_ok", "x2lo_ok", "logit_ok"))
        rt_step, rt_exp_in, rt_exp, w_ok = sem("rt_step"), sem("rt_exp_in"), sem("rt_exp"), sem("w_ok")
        wsp_hi, wsp_lo, g_mm, u_mm, th_ok, gt_ok, hid_ok, d_mm, y_ok = (sem(n) for n in (
            "wsp_hi", "wsp_lo", "g_mm", "u_mm", "th_ok", "gt_ok", "hid_ok", "d_mm", "y_ok"))
        out_ok = sem("out_ok")

        def need(eng, s, i, per, c):
            if isinstance(i, int):
                if per * i + c > 0:
                    eng.wait_ge(s, per * i + c)
            else:
                eng.wait_ge(s, i * per + max(c, 1))

        FIRST = 12
        QK_SLOT = [-4, -1, 2, 5, 8]
        V_SLOT = [5, 6, 8, 9, 11]
        T_SLOT = [s + 5 for s in QK_SLOT]

        def is_item(i, n):
            return not isinstance(i, int) or 0 <= PER * i + n < ITEMS

        def units_at(i, n):
            for u, s in ((n // UNIT + 1, n % UNIT), (n // UNIT + 2, n % UNIT - UNIT)):
                if s >= QK_SLOT[0] and (not isinstance(i, int) or 0 <= B * i + u < UNITS):
                    yield u, s

        def tiles_at(i, n, slots, lag):
            for u, s in units_at(i, n):
                for t, at in enumerate(slots):
                    if at + lag == s:
                        yield u, t, TILES * u + t

        def run_slots(eng, slot):
            for n in range(QK_SLOT[0] - UNIT, FIRST):
                slot(0, n)
            with eng.Fori(0, NG - 1) as i:
                for n in range(FIRST, FIRST + PER):
                    slot(i, n)
            for n in range(FIRST, PER + 8):
                slot(NG - 1, n)

        def rows_cols(t):
            return (C, GC) if t == 0 else (P, 0)

        def steps_of(i, n):
            k = KSTEPS * (n // HG) + n % HG
            if n % HG == 0 and is_item(i, n - 1):
                yield k - 1, True
            if is_item(i, n):
                yield k, False

        KP = KSTEPS * PER // HG
        TP = TILES * B
        GP = PER // HG

        CH_B0A, CH_CTX, CH_B0B, CH_B1A, CH_B1B, CH_2A, CH_2B = range(7)
        CHAIN_ROWS = [P, B * C, P, P, P, P, P]
        CHAIN_COLS = [QT, 1, QT, QT, QT, QT, QT]

        XPER = 2 * B * FC
        XFIRST = 6
        XSLOTS = E * B * FC

        def is_slot(i, n):
            return not isinstance(i, int) or 0 <= XPER * i + n < XSLOTS

        def run_expert_slots(eng, slot):
            for n in range(-2, XFIRST):
                slot(0, n)
            with eng.Fori(0, E // 2 - 1) as i:
                for n in range(XFIRST, XFIRST + XPER):
                    slot(i, n)
            for n in range(XFIRST, XPER + 4):
                slot(E // 2 - 1, n)

        def expert_of(n):
            return n // 4, (n % 4) // FC, n % FC

        block = ctx.enter_context(nc.Block())

        @block.sync
        def _(sp):
            x_v = x.rearrange("b (t p) d -> p (b t) d", p=P)
            sp.dma_start(x_sb[:, 0:QT, :], x_v[:, 0:QT, :]).then_inc(x_in, 16)
            wq_v = Wq.rearrange("d (g c) -> d g c", g=NG)
            wkv_v = Wkv.rearrange("d (k g c) -> d k g c", k=2, g=NG)
            w_v = wqkv[:, :].rearrange("p (g k c) -> p g k c", g=NG, k=3)
            sp.dma_start(w_v[:, 0, 0, :], wq_v[:, 0, :]).then_inc(w0_in, 16)
            sp.dma_start(w_v[:, 0, 1:3, :], wkv_v[:, :, 0, :]).then_inc(w0_in, 16)
            sp.dma_start(x_sb[:, QT:T, :], x_v[:, QT:T, :]).then_inc(x_in2, 16)
            sp.dma_start(w_v[:, 1:NG, 0, :], wq_v[:, 1:NG, :]).then_inc(w_in, 16)
            sp.dma_start(w_v[:, 1:NG, 1, :], wkv_v[:, 0, 1:NG, :]).then_inc(w_in, 16)
            sp.dma_start(w_v[:, 1:NG, 2, :], wkv_v[:, 1, 1:NG, :]).then_inc(w_in, 16)
            sp.dma_start(bout_b[:, :], bout.partition_broadcast(P)).then_inc(rest_in, 16)
            sp.dma_start(gates[:, 0:1], g_xattn.partition_broadcast(P)).then_inc(rest_in, 16)
            sp.dma_start(gates[:, 1:2], g_ffn.partition_broadcast(P)).then_inc(rest_in, 16)
            sp.dma_start(wr[:, :], router).then_inc(rest_in, 16)
            sp.dma_start(wout[:, :, :], Wout.rearrange("(c p) d -> p c d", p=P)).then_inc(rest_in, 16)
            sp.dma_start(wg[:, :].rearrange("p (e f) -> p e f", e=E), w_gate.rearrange("e d f -> d e f")).then_inc(moe_in, 16)
            sp.dma_start(wu[:, :].rearrange("p (e f) -> p e f", e=E), w_up.rearrange("e d f -> d e f")).then_inc(moe_in, 16)
            sp.dma_start(wd[:, :].rearrange("p (e c d) -> p e c d", e=E, c=FC),
                         w_down.rearrange("e (c p) d -> p e c d", p=P)).then_inc(moe_in, 16)

            def slot(i, n):
                for u, t, tau in tiles_at(i, n, V_SLOT, 2):
                    if t == 0:
                        need(sp, vlo_ok, i, TP, tau + 1)
                        for h in range(HG):
                            sp.dma_start(
                                v_bd[u % B][C * h:C * (h + 1), :, DH * h:DH * (h + 1)],
                                v_ctx[u % B][:, h, :, :]).then_inc(vbd_ok, 16)
                for u, t, tau in tiles_at(i, n, T_SLOT, 1):
                    if t == TILES - 1:
                        need(sp, qkst_ok, i, TP, tau + 1)
                        sp.dma_start(k_sw[u % B][0:DH, :, :], k_st[u % B][DH:P, :, :]).then_inc(ksw_ok, 16)
                        sp.dma_start(k_sw[u % B][DH:P, :, :], k_st[u % B][0:DH, :, :]).then_inc(ksw_ok, 16)

            sp.wait_ge(const_ok, 1)
            run_slots(sp, slot)
            out_v = out.rearrange("b (t p) d -> p (b t) d", p=P)
            for half in range(B):
                sp.wait_ge(y_ok, (E - 1) * B * QT + (half + 1) * QT)
                sp.dma_start(out_v[:, half * QT:(half + 1) * QT, :], x1[:, half * QT:(half + 1) * QT, :]).then_inc(out_ok, 16)
            sp.wait_ge(out_ok, 16 * B)

        @block.gpsimd
        def _(pool):
            nc.gpsimd.memset(ident[:, :], 0.0).then_inc(const_z, 1)
            nc.gpsimd.memset(ones_row[:, :], 1.0)
            for e in range(E):
                nc.gpsimd.memset(falling[:, e:e + 1], float(E - e))
            pool.wait_ge(const_z, 1)
            nc.gpsimd.affine_select(out=ident[:, :], in_=ident[:, :], compare_op=ALU.not_equal, fill=1.0, base=0,
                                    pattern=[[-1, P]], channel_multiplier=1).then_inc(ident_h_ok, 1)
            for part in (lnT_hi, lnT_lo):
                nc.gpsimd.memset(part[:, B * (N + C):LNW].bitcast(F32), 0.0)
            for k in range(2):
                nc.gpsimd.memset(qk_hl[k][:, :, :, :], 0.0)
            for k in range(B):
                last = nc.gpsimd.memset(v_bd[k][:, :, :], 0.0)
            last.then_inc(const_ok, 1)
            for g in range(NG):
                pool.wait_ge(whi_ok, g + 1)
                cols = slice(g * W3, (g + 1) * W3)
                nc.gpsimd.tensor_tensor(wqkv_lo[:, cols], wqkv[:, cols], wqkv_hi[:, cols].bitcast(F32),
                                        ALU.subtract).then_inc(wlo_ok, 1)
                if g == 0:
                    pool.wait_ge(head_gain_ok, 1)

            def slot(i, n):
                for u, t, tau in tiles_at(i, n, QK_SLOT, 3):
                    if t:
                        need(pool, norm_ok, i, TP, tau + 1)
                        q = qk[tau % 2][:, 0:GC].rearrange("p (h d) -> p h d", d=DH)
                        nc.gpsimd.tensor_tensor(q, q, head_gain[:, :].unsqueeze(1).broadcast_to([P, HG, DH]),
                                                ALU.mult).then_inc(gain_ok, 1)
                for u, t, tau in tiles_at(i, n, QK_SLOT, 4):
                    rows, c0 = rows_cols(t)
                    need(pool, qkhi_ok, i, TP, tau + 1)
                    hl = qk_hl[tau % 2]
                    nc.gpsimd.tensor_tensor(
                        hl[0:rows, c0 // DH:8, 1, :], qk[tau % 2][0:rows, c0:512].rearrange("p (h d) -> p h d", d=DH),
                        hl[0:rows, c0 // DH:8, 0, :], ALU.subtract).then_inc(qklo_ok, 1)
                for k, is_ctx in steps_of(i, n - 2):
                    w = P if is_ctx else 512
                    need(pool, phi_ok, i, KP, k + 1)
                    need(pool, pv_ok, i, KP, k + 1 - SPLIT)
                    nc.gpsimd.tensor_tensor(p_lo[k % SPLIT][:, 0:w], p_raw[k % RAW][:, 0:w], p_hi[k % SPLIT][:, 0:w],
                                            ALU.subtract).then_inc(plo_ok, 1)

            run_slots(pool, slot)

            def expert_slot(i, n):
                e, half, c = expert_of(n + 2)
                if (n + 2) % 4 == 0 and is_slot(i, n + 2):
                    need(pool, wsp_hi, i, 4, 2 * e + 2)
                    need(pool, u_mm, i, XPER, 4 * (e - 1))
                    for k, w in enumerate((wg, wu)):
                        nc.gpsimd.tensor_tensor(wgu_lo[e % 2][:, k * F:(k + 1) * F], w[:, bass.ds(i * (2 * F) + e * F, F)],
                                                wgu_hi[e % 2][:, k * F:(k + 1) * F].bitcast(F32),
                                                ALU.subtract).then_inc(wsp_lo, 1)

            run_expert_slots(pool, expert_slot)

        @block.scalar
        def _(act):
            act.dma_start(ctx_sb[:, :], ctx_in.rearrange("b c d -> (b c) d")).then_inc(ctx_inn, 16)
            for k, g in enumerate((ln_l_g, ln_l_b, ln_x_g, ln_x_b)):
                act.dma_start(gains[:, k:k + 1], g.unsqueeze(1)).then_inc(gains_in, 16)
            act.dma_start(head_gains[:, 0, :], qn_g.partition_broadcast(P)).then_inc(gains_in, 16)
            act.dma_start(head_gains[:, 1, :], kn_g.partition_broadcast(P)).then_inc(gains_in, 16)
            act.dma_start(mask_u8[:, :], mask.rearrange("b c -> (b c)").unsqueeze(0)).then_inc(gains_in, 16)

            def rsqrt_start(c):
                r, n = CHAIN_ROWS[c], CHAIN_COLS[c]
                act.wait_ge(var_ok, c + 1)
                nc.scalar.activation(ln_l[0:r, c, 0:n], ln_v[0:r, c, 0:n], ACT.Ln).then_inc(lnl_ok, 1)
                act.wait_ge(lnl_ok, c + 1)
                nc.scalar.activation(ln_e[0:r, c, 0:n], ln_l[0:r, c, 0:n], ACT.Exp, scale=-0.5).then_inc(lne_ok, 1)

            def weights_hi(g):
                act.wait_ge(w0_in if g == 0 else w_in, 32 if g == 0 else 48)
                nc.scalar.copy(wqkv_hi[:, g * W3:(g + 1) * W3], wqkv[:, g * W3:(g + 1) * W3]).then_inc(whi_ok, 1)

            rsqrt_start(CH_B0A)
            rsqrt_start(CH_CTX)
            weights_hi(0)
            rsqrt_start(CH_B0B)
            rsqrt_start(CH_B1A)
            act.wait_ge(gains_in, 16 * 7)

            def with_gain(k, bank, cols, g):
                act.wait_ge(zT_ok, k + 1)
                w = cols.stop - cols.start
                nc.scalar.activation(lnT[:, cols], bank[:, 0:w], ACT.Identity, scale=gains[:, g:g + 1],
                                     bias=gains[:, g + 1:g + 2]).then_inc(lnT_ok, 1)

            with_gain(0, turned, slice(B * N, B * N + B * C), 2)
            with_gain(1, proj_qk, slice(0, N), 0)
            rsqrt_start(CH_B1B)
            weights_hi(1)
            with_gain(2, proj_v, slice(N, B * N), 0)
            weights_hi(2)
            weights_hi(3)

            def slot(i, n):
                for u, t, tau in tiles_at(i, n, QK_SLOT, 2):
                    rows, c0 = rows_cols(t)
                    h0 = c0 // DH
                    need(act, ms_ok, i, TP, tau + 1)
                    nc.scalar.activation(rms_l[0:rows, tau % 2, h0:8], meansq[0:rows, tau % 2, h0:8],
                                         ACT.Ln).then_inc(rl_ok, 1)
                    need(act, rl_ok, i, TP, tau + 1)
                    nc.scalar.activation(rms_e[0:rows, tau % 2, h0:8], rms_l[0:rows, tau % 2, h0:8], ACT.Exp,
                                         scale=-0.5).then_inc(re_ok, 1)
                for k, is_ctx in steps_of(i, n - 1):
                    w = P if is_ctx else 512
                    need(act, pT_ok, i, KP, k + 1)
                    need(act, plo_ok, i, KP, k + 1 - RAW)
                    nc.scalar.copy(p_raw[k % RAW][:, 0:w], turned[:, 0:w]).then_inc(raw_ok, 1)
                if is_item(i, n):
                    g = n // HG
                    need(act, max_ok, i, PER, n + 1)
                    need(act, pT_ok, i, KP, KSTEPS * (g - 1))
                    need(act, o_ok, i, GP, g - SUMS + 1)
                    nc.scalar.activation(probs[g % 2][:, n % HG, :], scores[n % 2][:, 0:KEYS], ACT.Exp,
                                         bias=neg_max[:, n % NM:n % NM + 1],
                                         accum_out=sums[:, g % SUMS, n % HG:n % HG + 1]).then_inc(exp_ok, 1)
                for u, t, tau in tiles_at(i, n, V_SLOT, 1):
                    rows, _ = rows_cols(t)
                    need(act, v_mm, i, TP, tau + 1)
                    need(act, pv_ok, i, KP, KSTEPS * QT * (u - 1))
                    if t == 0:
                        o = v_ctx[u % B][:, :, 0, :]
                        p = proj_v[0:C, 0:GC].rearrange("p (h d) -> p h d", d=DH)
                    else:
                        o = v_hl[u % B][:, 0, t - 1, :]
                        p = proj_v[:, 0:GC]
                    nc.scalar.activation(o, p, ACT.Copy, scale=V_SCALE).then_inc(vhi_ok, 1)
                for u, t, tau in tiles_at(i, n, QK_SLOT, 1):
                    rows, c0 = rows_cols(t)
                    need(act, qk_mm, i, TP, tau + 1)
                    need(act, ss_ok, i, TP, tau - 1)
                    nc.scalar.activation(squares[tau % 2][0:rows, c0:512], proj_qk[0:rows, c0:512],
                                         ACT.Square).then_inc(sq_ok, 1)
                for u, t, tau in tiles_at(i, n, T_SLOT, 1):
                    need(act, qkT_ok, i, TP, tau + 1)
                    need(act, s_ok, i, PER, UNIT * (u - 1))
                    tr = proj_v[:, :].bitcast(F16)
                    if t == 0:
                        nc.scalar.copy(k_st[u % B][:, :, N:KEYS],
                                       tr[:, 512:1024].rearrange("p (h c) -> p h c", c=P)[:, :, 0:C]).then_inc(qkst_ok, 1)
                    else:
                        cols = slice((t - 1) * P, t * P)
                        nc.scalar.copy(q_st[u % B][:, :, cols], tr[:, 0:512].rearrange("p (h c) -> p h c", c=P))
                        nc.scalar.copy(k_st[u % B][:, :, cols],
                                       tr[:, 512:1024].rearrange("p (h c) -> p h c", c=P)).then_inc(qkst_ok, 1)

            run_slots(act, slot)

            act.wait_ge(rest_in, 16 * 5)
            nc.scalar.activation(gates_t[:, :], gates[:, :], ACT.Tanh).then_inc(gate_ok, 1)
            for t in range(T):
                act.wait_ge(oT_mm, t + 1)
                if t >= 2:
                    act.wait_ge(y_mm, t - 1)
                nc.scalar.copy(oT[t % 2][:, 0:512], scores[t % 2][:, 0:512]).then_inc(oTa_ok, 1)
            rsqrt_start(CH_2A)
            rsqrt_start(CH_2B)
            for b in range(B):
                act.wait_ge(z2T_ok, b + 1)
                nc.scalar.copy(x2T[:, b * N:(b + 1) * N], (turned, attn_o)[b][:, :]).then_inc(x2T_ok, 1)
                act.wait_ge(x2T_ok, b + 1)
                nc.scalar.copy(x2T_hi[:, b * N:(b + 1) * N], x2T[:, b * N:(b + 1) * N]).then_inc(x2hi_ok, 1)
            act.wait_ge(rt_exp_in, 1)
            nc.scalar.activation(rt[:, 1, :, :], rt[:, 0, :, :], ACT.Exp).then_inc(rt_exp, 1)
            act.wait_ge(rt_exp_in, 2)
            nc.scalar.activation(rs[:, 5, :], rs[:, 4, :], ACT.Exp).then_inc(rt_exp, 1)
            act.wait_ge(moe_in, 48)

            def expert_slot(i, n):
                e, half, c = expert_of(n + 2)
                if (n + 2) % 4 == 0 and is_slot(i, n + 2):
                    need(act, u_mm, i, XPER, 4 * (e - 1))
                    for k, w in enumerate((wg, wu)):
                        nc.scalar.copy(wgu_hi[e % 2][:, k * F:(k + 1) * F],
                                       w[:, bass.ds(i * (2 * F) + e * F, F)]).then_inc(wsp_hi, 1)
                if is_slot(i, n):
                    need(act, g_mm, i, XPER, n + 1)
                    need(act, gt_ok, i, XPER, n - 1)
                    nc.scalar.activation(th[n % 2][:, :], scores[n % 2][:, 0:512], ACT.Tanh, scale=0.5).then_inc(th_ok, 1)

            run_expert_slots(act, expert_slot)

        @block.vector
        def _(dve):
            def norm_stats(k, rows, src):
                nc.vector.bn_stats(stats[0:rows, k, :], src).then_inc(bn_ok, 1)

            def norm_moments(k, rows, done):
                dve.wait_ge(bn_ok, done)
                return nc.vector.bn_aggr(moments[0:rows, k, :], stats[0:rows, k, :])

            step = [0]

            def link(ins):
                step[0] += 1
                ins.then_inc(newton, 1)
                dve.wait_ge(newton, step[0])

            def rsqrt_finish(c):
                r, n = CHAIN_ROWS[c], CHAIN_COLS[c]
                v, e = ln_v[0:r, c, 0:n], ln_e[0:r, c, 0:n]
                a = [ln_t[0:r, c, k, 0:n] for k in range(3)]
                dve.wait_ge(lne_ok, c + 1)
                link(nc.vector.tensor_tensor(a[0], e, e, ALU.mult))
                link(nc.vector.tensor_tensor(a[1], a[0], v, ALU.mult))
                link(nc.vector.tensor_scalar(a[2], a[1], -0.5, 1.5, ALU.mult, ALU.add))
                link(nc.vector.tensor_tensor(ln_r[0:r, c, 0:n], a[2], e, ALU.mult))

            def first_norm(b, c):
                tiles = range(b * QT, (b + 1) * QT)
                dve.wait_ge(x_in if b == 0 else x_in2, 16)
                done = bn[0]
                for t in tiles:
                    norm_stats(t, P, x_sb[:, t, :])
                    bn[0] += 1
                for k, t in enumerate(tiles):
                    last = norm_moments(t, P, done + k + 1)
                link(last)
                nc.vector.tensor_scalar(ln_v[:, c, :], moments[:, b * QT:(b + 1) * QT, 1], LN_EPS, None,
                                        ALU.add).then_inc(var_ok, 1)

            def second_norm(b, c1, c2):
                var = moments[:, b * QT:(b + 1) * QT, 1]
                link(nc.vector.tensor_tensor(ln_t[:, c2, 0, :], ln_r[:, c1, :], ln_r[:, c1, :], ALU.mult))
                link(nc.vector.tensor_tensor(ln_t[:, c2, 1, :], ln_t[:, c2, 0, :], var, ALU.mult))
                nc.vector.tensor_scalar(ln_v[:, c2, :], ln_t[:, c2, 1, :], LN_EPS, None, ALU.add).then_inc(var_ok, 1)

            def normalise(b, c1, c2):
                link(nc.vector.tensor_tensor(ln_s[:, b * QT:(b + 1) * QT], ln_r[:, c1, :], ln_r[:, c2, :], ALU.mult))
                for t in range(b * QT, (b + 1) * QT):
                    nc.vector.tensor_scalar(z[:, t, :], x_sb[:, t, :], moments[:, t, 0:1], ln_s[:, t:t + 1],
                                            ALU.subtract, ALU.mult).then_inc(z_ok, 1)

            def split_ln(k, cols):
                dve.wait_ge(lnT_ok, k + 1)
                nc.vector.tensor_copy(lnT_hi[:, cols], lnT[:, cols]).then_inc(lnhi_ok, 1)
                dve.wait_ge(lnhi_ok, k + 1)
                nc.vector.tensor_tensor(lnT_lo[:, cols], lnT[:, cols], lnT_hi[:, cols].bitcast(F32),
                                        ALU.subtract).then_inc(lnlo_ok, 1)

            bn = [0]
            first_norm(0, CH_B0A)
            dve.wait_ge(ctx_inn, 16)
            norm_stats(T, B * C, ctx_sb[:, :])
            bn[0] += 1
            link(norm_moments(T, B * C, bn[0]))
            nc.vector.tensor_scalar(ln_v[0:B * C, CH_CTX, 0:1], moments[0:B * C, T, 1:2], LN_EPS, None,
                                    ALU.add).then_inc(var_ok, 1)
            rsqrt_finish(CH_B0A)
            second_norm(0, CH_B0A, CH_B0B)
            rsqrt_finish(CH_CTX)
            nc.vector.tensor_scalar(z[0:B * C, T, :], ctx_sb[:, :], moments[0:B * C, T, 0:1], ln_r[0:B * C, CH_CTX, 0:1],
                                    ALU.subtract, ALU.mult).then_inc(z_ok, 1)
            first_norm(1, CH_B1A)
            rsqrt_finish(CH_B0B)
            normalise(0, CH_B0A, CH_B0B)
            rsqrt_finish(CH_B1A)
            second_norm(1, CH_B1A, CH_B1B)
            dve.wait_ge(ident_h_ok, 1)
            nc.vector.tensor_copy(ident_h[:, :], ident[:, :]).then_inc(ident_h_ok, 1)
            dve.wait_ge(gains_in, 16 * 7)
            nc.vector.scalar_tensor_tensor(out=head_gain[:, :], in0=head_gains[:, 0, :], scalar=DH ** -0.5,
                                           in1=head_gains[:, 1, :], op0=ALU.mult, op1=ALU.mult).then_inc(head_gain_ok, 1)
            nc.vector.tensor_scalar(mask_row[:, :], mask_u8[:, :], 1.0, MASKED, ALU.subtract, ALU.mult).then_inc(mask_ok, 1)
            dve.wait_ge(const_ok, 1)
            split_ln(0, slice(B * N, B * N + B * C))
            split_ln(1, slice(0, N))
            rsqrt_finish(CH_B1B)
            normalise(1, CH_B1A, CH_B1B)
            split_ln(2, slice(N, B * N))

            def slot(i, n):
                if is_item(i, n):
                    need(dve, s_ok, i, PER, n + 1)
                    need(dve, exp_ok, i, PER, n + 1 - NM)
                    nc.vector.tensor_reduce(neg_max[:, n % NM:n % NM + 1], scores[n % 2][:, 0:KEYS], AX_X, ALU.max,
                                            negate=True).then_inc(max_ok, 1)
                if n % HG == HG - 1 and is_item(i, n - 7):
                    g = (n - 7) // HG
                    need(dve, pv_ok, i, KP, KSTEPS * (g + 1))
                    nc.vector.tensor_scalar(sums_s[:, g % 2, :], sums[:, g % SUMS, :], V_SCALE, None,
                                            ALU.mult).then_inc(den_ok, 1)
                    need(dve, den_ok, i, 2 * GP, 2 * g + 1)
                    nc.vector.reciprocal(inv_sums[:, g % 2, :], sums_s[:, g % 2, :]).then_inc(den_ok, 1)
                    need(dve, den_ok, i, 2 * GP, 2 * g + 2)
                    u, qt = g // QT, g % QT
                    t = (u % B) * QT + qt
                    o = o_sb[:, bass.ds(i * GC + (t * INNER + (u // B) * GC), GC)].rearrange("p (h d) -> p h d", d=DH)
                    nc.vector.tensor_tensor(o, attn_o[:, 0:GC].rearrange("p (h d) -> p h d", d=DH),
                                            inv_sums[:, g % 2, :].unsqueeze(2).broadcast_to([P, HG, DH]),
                                            ALU.mult).then_inc(o_ok, 1)
                if n % HG == 0 and is_item(i, n - 1):
                    g = (n - 1) // HG
                    need(dve, exp_ok, i, PER, n)
                    need(dve, pT_ok, i, KP, KSTEPS * (g - 1))
                    nc.vector.tensor_copy(probs_c[g % 2][:, :].rearrange("p (h c) -> p h c", c=C),
                                          probs[g % 2][:, :, N:KEYS]).then_inc(pack_ok, 1)
                for k, is_ctx in steps_of(i, n - 2):
                    w = P if is_ctx else 512
                    need(dve, raw_ok, i, KP, k + 1)
                    need(dve, pv_ok, i, KP, k + 1 - SPLIT)
                    nc.vector.tensor_copy(p_hi[k % SPLIT][:, 0:w], p_raw[k % RAW][:, 0:w]).then_inc(phi_ok, 1)
                for u, t, tau in tiles_at(i, n, V_SLOT, 1):
                    need(dve, vhi_ok, i, TP, tau + 1)
                    if t == 0:
                        hi, lo = v_ctx[u % B][:, :, 0, :], v_ctx[u % B][:, :, 1, :]
                        p = proj_v[0:C, 0:GC].rearrange("p (h d) -> p h d", d=DH)
                    else:
                        hi, lo = v_hl[u % B][:, 0, t - 1, :], v_hl[u % B][:, 1, t - 1, :]
                        p = proj_v[:, 0:GC]
                    nc.vector.scalar_tensor_tensor(out=lo, in0=p, scalar=V_SCALE, in1=hi, op0=ALU.mult,
                                                   op1=ALU.subtract).then_inc(vlo_ok, 1)
                for u, t, tau in tiles_at(i, n, QK_SLOT, 1):
                    rows, c0 = rows_cols(t)
                    h0 = c0 // DH
                    need(dve, sq_ok, i, TP, tau + 1)
                    need(dve, norm_ok, i, TP, tau - 1)
                    nc.vector.tensor_reduce(sumsq[0:rows, tau % 2, h0:8],
                                            squares[tau % 2][0:rows, c0:512].rearrange("p (h d) -> p h d", d=DH),
                                            AX_X, ALU.add).then_inc(ss_ok, 1)
                    need(dve, ss_ok, i, TP, tau + 1)
                    nc.vector.tensor_scalar(meansq[0:rows, tau % 2, h0:8], sumsq[0:rows, tau % 2, h0:8], 1.0 / DH,
                                            RMS_EPS ** 2, ALU.mult, ALU.max).then_inc(ms_ok, 1)
                for u, t, tau in tiles_at(i, n, QK_SLOT, 2):
                    rows, c0 = rows_cols(t)
                    h0 = c0 // DH
                    e = rms_e[0:rows, tau % 2, h0:8]
                    a = [rms_t[0:rows, tau % 2, k, h0:8] for k in range(3)]
                    r = rms_r[0:rows, tau % 2, h0:8]
                    need(dve, re_ok, i, TP, tau + 1)
                    nc.vector.tensor_tensor(a[0], e, e, ALU.mult).then_inc(rms_step, 1)
                    need(dve, rms_step, i, 4 * TP, 4 * tau + 1)
                    nc.vector.tensor_tensor(a[1], a[0], meansq[0:rows, tau % 2, h0:8], ALU.mult).then_inc(rms_step, 1)
                    need(dve, rms_step, i, 4 * TP, 4 * tau + 2)
                    nc.vector.tensor_scalar(a[2], a[1], -0.5, 1.5, ALU.mult, ALU.add).then_inc(rms_step, 1)
                    need(dve, rms_step, i, 4 * TP, 4 * tau + 3)
                    nc.vector.tensor_tensor(r, a[2], e, ALU.mult).then_inc(rms_step, 1)
                    need(dve, rms_step, i, 4 * TP, 4 * tau + 4)
                    need(dve, qklo_ok, i, TP, tau - 1)
                    nc.vector.tensor_tensor(qk[tau % 2][0:rows, c0:512].rearrange("p (h d) -> p h d", d=DH),
                                            proj_qk[0:rows, c0:512].rearrange("p (h d) -> p h d", d=DH),
                                            r.unsqueeze(2).broadcast_to([rows, 8 - h0, DH]),
                                            ALU.mult).then_inc(norm_ok, 1)
                for u, t, tau in tiles_at(i, n, QK_SLOT, 3):
                    rows, c0 = rows_cols(t)
                    if t:
                        need(dve, gain_ok, i, B * QT, QT * u + t)
                    else:
                        need(dve, norm_ok, i, TP, tau + 1)
                    need(dve, qkT_ok, i, TP, tau - 1)
                    nc.vector.tensor_copy(qk_hl[tau % 2][0:rows, c0 // DH:8, 0, :],
                                          qk[tau % 2][0:rows, c0:512].rearrange("p (h d) -> p h d", d=DH)).then_inc(qkhi_ok, 1)

            run_slots(dve, slot)

            def oT_half(t):
                dve.wait_ge(oT_mm, t + 1)
                if t >= 2:
                    dve.wait_ge(y_mm, t - 1)
                nc.vector.tensor_copy(oT[t % 2][:, 512:1024], scores[t % 2][:, 512:1024]).then_inc(oTv_ok, 1)

            dve.wait_ge(rest_in, 16 * 5)
            nc.vector.tensor_copy(wr_hl[:, 0, :], wr[:, :]).then_inc(wr_ok, 1)
            dve.wait_ge(wr_ok, 1)
            nc.vector.tensor_tensor(wr_hl[:, 1, :], wr[:, :], wr_hl[:, 0, :].bitcast(F32), ALU.subtract).then_inc(wr_ok, 1)
            dve.wait_ge(gate_ok, 1)
            oT_half(0)
            for t in range(T):
                if t + 1 < T:
                    oT_half(t + 1)
                dve.wait_ge(y_mm, t + 1)
                y = (proj_qk, proj_v)[t % 2][:, 0:D]
                link(nc.vector.tensor_tensor(x1_t[:, t % 2, :], y, bout_b[:, :], ALU.add))
                nc.vector.scalar_tensor_tensor(out=x1[:, t, :], in0=x1_t[:, t % 2, :], scalar=gates_t[:, 0:1],
                                               in1=x_sb[:, t, :], op0=ALU.mult, op1=ALU.add).then_inc(x1_ok, 1)
                dve.wait_ge(x1_ok, t + 1)
                norm_stats(t, P, x1[:, t, :])
                bn[0] += 1
                link(norm_moments(t, P, bn[0]))
                if t % QT == QT - 1:
                    b = t // QT
                    nc.vector.tensor_scalar(ln_v[:, CH_2A + b, :], moments[:, b * QT:(b + 1) * QT, 1], LN_EPS, None,
                                            ALU.add).then_inc(var_ok, 1)
            for b in range(B):
                rsqrt_finish(CH_2A + b)
                for t in range(b * QT, (b + 1) * QT):
                    nc.vector.tensor_scalar(z[:, t, :], x1[:, t, :], moments[:, t, 0:1],
                                            ln_r[:, CH_2A + b, t % QT:t % QT + 1], ALU.subtract,
                                            ALU.mult).then_inc(z2_ok, 1)
            for b in range(B):
                cols = slice(b * N, (b + 1) * N)
                dve.wait_ge(x2hi_ok, b + 1)
                nc.vector.tensor_tensor(x2T_lo[:, cols], x2T[:, cols], x2T_hi[:, cols].bitcast(F32),
                                        ALU.subtract).then_inc(x2lo_ok, 1)

            def over(v):
                return v.unsqueeze(2).broadcast_to([P, T, E])

            fall = falling[:, :].unsqueeze(1).broadcast_to([P, T, E])
            rstep = [0]

            def rlink(ins):
                rstep[0] += 1
                ins.then_inc(rt_step, 1)
                dve.wait_ge(rt_step, rstep[0])

            dve.wait_ge(logit_ok, T)
            lg = turned[:, 0:T * 2 * E].rearrange("p (t k e) -> p t k e", t=T, k=2)
            rlink(nc.vector.tensor_copy(rt[:, 2, :, :], lg[:, :, 0, :]))
            rlink(nc.vector.tensor_tensor(rt[:, 3, :, :], rt[:, 2, :, :], lg[:, :, 1, :], ALU.add))
            rlink(nc.vector.tensor_reduce(rs[:, 0, :], rt[:, 3, :, :], AX_X, ALU.max))
            nc.vector.tensor_tensor(rt[:, 0, :, :], rt[:, 3, :, :], over(rs[:, 0, :]), ALU.subtract).then_inc(rt_exp_in, 1)
            dve.wait_ge(rt_exp, 1)
            rlink(nc.vector.tensor_reduce(rs[:, 1, :], rt[:, 1, :, :], AX_X, ALU.add))
            rlink(nc.vector.reciprocal(rs[:, 2, :], rs[:, 1, :]))
            rlink(nc.vector.tensor_tensor(rt[:, 4, :, :], rt[:, 1, :, :], over(rs[:, 2, :]), ALU.mult))
            best = [rs[:, 3, :], rs[:, 6, :]]
            hot = []
            prob = rt[:, 4, :, :]
            for k in range(2):
                a = [rt[:, 5 + 4 * k + j, :, :] for j in range(4)]
                pos = rs[:, 7, :] if k else rs[:, 0, :]
                rlink(nc.vector.tensor_reduce(best[k], prob, AX_X, ALU.max))
                rlink(nc.vector.tensor_tensor(a[0], prob, over(best[k]), ALU.is_ge))
                rlink(nc.vector.tensor_tensor(a[1], a[0], fall, ALU.mult))
                rlink(nc.vector.tensor_reduce(pos, a[1], AX_X, ALU.max))
                rlink(nc.vector.tensor_tensor(a[2], a[1], over(pos), ALU.is_equal))
                hot.append(a[2])
                if k == 0:
                    rlink(nc.vector.scalar_tensor_tensor(out=a[3], in0=a[2], scalar=-2.0, in1=prob, op0=ALU.mult,
                                                         op1=ALU.add))
                    prob = a[3]
            nc.vector.tensor_tensor(rs[:, 4, :], best[1], best[0], ALU.subtract).then_inc(rt_exp_in, 1)
            dve.wait_ge(rt_exp, 2)
            rlink(nc.vector.tensor_scalar(rs[:, 0, :], rs[:, 5, :], 1.0, None, ALU.add))
            rlink(nc.vector.reciprocal(rs[:, 1, :], rs[:, 0, :]))
            dve.wait_ge(gate_ok, 1)
            rlink(nc.vector.tensor_scalar(rs[:, 2, :], rs[:, 1, :], gates_t[:, 1:2], 0.5, ALU.mult, ALU.mult))
            rlink(nc.vector.tensor_tensor(rs[:, 7, :], rs[:, 2, :], rs[:, 5, :], ALU.mult))
            rlink(nc.vector.tensor_tensor(rt[:, 13, :, :], hot[0], over(rs[:, 2, :]), ALU.mult))
            rlink(nc.vector.tensor_tensor(rt[:, 14, :, :], hot[1], over(rs[:, 7, :]), ALU.mult))
            nc.vector.tensor_tensor(w_tok[:, :, :], rt[:, 13, :, :], rt[:, 14, :, :], ALU.add).then_inc(w_ok, 1)
            dve.wait_ge(w_ok, 1)

            def expert_slot(i, n):
                if is_slot(i, n):
                    need(dve, th_ok, i, XPER, n + 1)
                    need(dve, hid_ok, i, XPER, n - 1)
                    nc.vector.scalar_tensor_tensor(out=gt[n % 2][:, :], in0=th[n % 2][:, :], scalar=1.0,
                                                   in1=scores[n % 2][:, 0:512], op0=ALU.add,
                                                   op1=ALU.mult).then_inc(gt_ok, 1)
                    need(dve, gt_ok, i, XPER, n + 1)
                    need(dve, u_mm, i, XPER, n + 1)
                    need(dve, d_mm, i, XPER, n - 1)
                    nc.vector.tensor_tensor(hid[n % 2][:, :], gt[n % 2][:, :], scores[n % 2][:, 512:1024],
                                            ALU.mult).then_inc(hid_ok, 1)
                m = n - 2
                if is_slot(i, m) and m % FC == FC - 1:
                    e, half, _ = expert_of(m)
                    need(dve, d_mm, i, XPER, m + 1)
                    for k in range(QT):
                        t = half * QT + k
                        need(dve, y_ok, i, 2 * T, T * (e - 1) + t + 1)
                        nc.vector.scalar_tensor_tensor(
                            out=x1[:, t, :], in0=(turned, attn_o)[half][:, k * D:(k + 1) * D],
                            scalar=w_tok[:, t, bass.ds(i * 2 + e, 1)], in1=x1[:, t, :], op0=ALU.mult,
                            op1=ALU.add).then_inc(y_ok, 1)

            run_expert_slots(dve, expert_slot)

        @block.tensor
        def _(pe):
            pe.wait_ge(ident_h_ok, 1)
            pe.wait_ge(z_ok, 1)
            nc.tensor.transpose(turned[:, 0:B * C], z[0:B * C, T, :], ident[0:B * C, 0:B * C]).then_inc(zT_ok, 1)
            for b, bank in enumerate((proj_qk, proj_v)):
                for t in range(QT):
                    pe.wait_ge(z_ok, 1 + b * QT + t + 1)
                    last = nc.tensor.transpose(bank[:, t * P:(t + 1) * P], z[:, b * QT + t, :], ident[:, :])
                last.then_inc(zT_ok, 1)
            pe.wait_ge(ident_h_ok, 2)
            pe.wait_ge(mask_ok, 1)

            def project(i, u, t, out_ap, c0, cols):
                first = B * N + (u % B) * C if t == 0 else (u % B) * N + (t - 1) * P
                toks = slice(first, first + P)
                w = bass.ds(i * W3 + ((u // B) * W3 + c0), cols)
                nc.tensor.matmul(out_ap, lnT_hi[:, toks], wqkv_hi[:, w], start=True, stop=False)
                nc.tensor.matmul(out_ap, lnT_hi[:, toks], wqkv_lo[:, w], start=False, stop=False)
                return nc.tensor.matmul(out_ap, lnT_lo[:, toks], wqkv_hi[:, w], start=False, stop=True)

            def proj_v_free(i, u, s):
                jobs = sorted([(a, 0, t) for t, a in enumerate(V_SLOT)] + [(a, 1, t) for t, a in enumerate(T_SLOT)])
                k = jobs.index(s)
                v, (_, kind, t) = (u, jobs[k - 1]) if k else (u - 1, jobs[-1])
                need(pe, (vlo_ok, qkst_ok)[kind], i, TP, TILES * v + t + 1)

            def times_values(i, k, cols, o, vh, vl, wait, start, stop):
                hi, lo = p_hi[k % SPLIT], p_lo[k % SPLIT]
                if wait:
                    need(pe, phi_ok, i, KP, k + 1)
                nc.tensor.matmul(o, hi[:, cols], vh, start=start, stop=False, skip_group_check=True)
                nc.tensor.matmul(o, hi[:, cols], vl, start=False, stop=False, skip_group_check=True)
                if wait:
                    need(pe, plo_ok, i, KP, k + 1)
                return nc.tensor.matmul(o, lo[:, cols], vh, start=False, stop=stop, skip_group_check=True)

            def slot(i, n):
                if (n - 3) % HG == 0 and is_item(i, n - 4):
                    u = (n - 4) // UNIT
                    if (n - 4) % UNIT == HG - 1:
                        need(pe, vbd_ok, i, 16 * HG * B, 16 * HG * (u + 1))
                    times_values(i, KSTEPS * ((n - 3) // HG) - 1, slice(0, P), attn_o[:, 0:GC], v_bd[u % B][:, 0, :],
                                 v_bd[u % B][:, 1, :], True, False, True).then_inc(pv_ok, 1)
                if is_item(i, n):
                    u, qt, h = n // UNIT, (n % UNIT) // HG, n % HG
                    b = u % B
                    if n % UNIT == 0:
                        need(pe, qkst_ok, i, TP, TILES * (u + 1))
                        need(pe, ksw_ok, i, 32 * B, 32 * (u + 1))
                    need(pe, exp_ok, i, PER, n - 1)
                    q = q_st[b][:, h, qt * P:(qt + 1) * P]
                    s = scores[n % 2]
                    nc.tensor.matmul(s[:, 0:N], q, k_st[b][:, h, 0:N], start=True, stop=False)
                    nc.tensor.matmul(s[:, N:KEYS], q, k_st[b][:, h, N:KEYS], start=True, stop=False)
                    nc.tensor.matmul(s[:, 0:N], q, k_sw[b][:, h, 0:N], start=False, stop=True)
                    nc.tensor.matmul(s[:, N:KEYS], q, k_sw[b][:, h, N:KEYS], start=False, stop=False)
                    nc.tensor.matmul(s[:, N:KEYS], ones_row[:, :], mask_row[:, b * C:(b + 1) * C], start=False,
                                     stop=True).then_inc(s_ok, 1)
                if is_item(i, n - 1):
                    m = n - 1
                    k = KSTEPS * (m // HG) + m % HG
                    need(pe, exp_ok, i, PER, m + 1)
                    need(pe, raw_ok, i, KP, k)
                    for c in range(QT):
                        last = nc.tensor.transpose(turned[:, c * P:(c + 1) * P],
                                                   probs[(m // HG) % 2][:, m % HG, c * P:(c + 1) * P], ident[:, :])
                    last.then_inc(pT_ok, 1)
                for u, t, tau in tiles_at(i, n, QK_SLOT, 0):
                    need(pe, wlo_ok, i, 1, u // B + 1)
                    if isinstance(i, int) and i == 0 and u < B:
                        pe.wait_ge(lnlo_ok, (2 if u == 0 else 3) if t else 1)
                    need(pe, norm_ok, i, TP, tau)
                    _, c0 = rows_cols(t)
                    project(i, u, t, proj_qk[:, c0:512], c0, 2 * GC - c0).then_inc(qk_mm, 1)
                for u, t, tau in tiles_at(i, n, V_SLOT, 0):
                    proj_v_free(i, u, (V_SLOT[t], 0, t))
                    project(i, u, t, proj_v[:, 0:GC], 2 * GC, GC).then_inc(v_mm, 1)
                for u, t, tau in tiles_at(i, n, T_SLOT, 0):
                    proj_v_free(i, u, (T_SLOT[t], 1, t))
                    need(pe, qklo_ok, i, TP, tau + 1)
                    _, c0 = rows_cols(t)
                    tr = proj_v[:, :].bitcast(F16)
                    for j in range(c0 // DH, 8):
                        last = nc.tensor.transpose(tr[:, j * P:(j + 1) * P], qk_hl[tau % 2][:, j, :, :], ident_h[:, :])
                    last.then_inc(qkT_ok, 1)
                if is_item(i, n - 3):
                    m = n - 3
                    u, h = m // UNIT, m % HG
                    if m % UNIT == 0:
                        need(pe, vlo_ok, i, TP, TILES * (u + 1))
                    if h == 0:
                        need(pe, o_ok, i, GP, m // HG)
                    k = KSTEPS * (m // HG) + h
                    for c in range(QT):
                        vh, vl = (v_hl[u % B][:, part, c, h * DH:(h + 1) * DH] for part in range(2))
                        last = times_values(i, k, slice(c * P, (c + 1) * P), attn_o[:, h * DH:(h + 1) * DH], vh, vl,
                                            c == 0, h == 0 and c == 0, False)
                    last.then_inc(pv_ok, 1)
                if n % HG == 0 and is_item(i, n - 1):
                    g = (n - 1) // HG
                    need(pe, pack_ok, i, GP, g + 1)
                    need(pe, raw_ok, i, KP, KSTEPS * g + HG)
                    nc.tensor.transpose(turned[:, 0:P], probs_c[g % 2][:, :], ident[:, :]).then_inc(pT_ok, 1)

            run_slots(pe, slot)

            def turn(t):
                if t < 2:
                    pe.wait_ge(o_ok, NG * T)
                else:
                    pe.wait_ge(oTa_ok, t - 1)
                    pe.wait_ge(oTv_ok, t - 1)
                for c in range(H // 2):
                    last = nc.tensor.transpose(scores[t % 2][:, c * P:(c + 1) * P],
                                               o_sb[:, t * INNER + c * P:t * INNER + (c + 1) * P], ident[:, :])
                last.then_inc(oT_mm, 1)

            turn(0)
            pe.wait_ge(rest_in, 16 * 5)
            for t in range(T):
                if t + 1 < T:
                    turn(t + 1)
                pe.wait_ge(oTa_ok, t + 1)
                pe.wait_ge(oTv_ok, t + 1)
                if t >= 2:
                    pe.wait_ge(x1_ok, t - 1)
                y = (proj_qk, proj_v)[t % 2][:, 0:D]
                for c in range(H // 2):
                    last = nc.tensor.matmul(y, oT[t % 2][:, c * P:(c + 1) * P], wout[:, c, :], start=(c == 0),
                                            stop=(c == H // 2 - 1))
                last.then_inc(y_mm, 1)
            for b in range(B):
                for t in range(QT):
                    pe.wait_ge(z2_ok, b * QT + t + 1)
                    last = nc.tensor.transpose((turned, attn_o)[b][:, t * P:(t + 1) * P], z[:, b * QT + t, :], ident[:, :])
                last.then_inc(z2T_ok, 1)
            for t in range(T):
                pe.wait_ge(x2lo_ok, t // QT + 1)
                if t == 0:
                    pe.wait_ge(wr_ok, 2)
                    pe.wait_ge(x2T_ok, 1)
                o = turned[:, t * 2 * E:(t + 1) * 2 * E]
                r = wr_hl[:, :, :].rearrange("p k e -> p (k e)")
                nc.tensor.matmul(o, x2T_hi[:, t * P:(t + 1) * P], r, start=True, stop=False)
                nc.tensor.matmul(o, x2T_lo[:, t * P:(t + 1) * P], r, start=False, stop=True).then_inc(logit_ok, 1)
            pe.wait_ge(moe_in, 48)

            def expert_slot(i, n):
                if is_slot(i, n):
                    e, half, c = expert_of(n)
                    toks = slice(half * N, (half + 1) * N)
                    if n % 4 == 0:
                        need(pe, wsp_lo, i, 4, 2 * e + 2)
                    if isinstance(i, int) and i == 0 and n < 4:
                        pe.wait_ge(x2lo_ok, B)
                    need(pe, hid_ok, i, XPER, n - 1)
                    for k, done in enumerate((g_mm, u_mm)):
                        o = scores[n % 2][:, k * 512:(k + 1) * 512]
                        w = slice(k * F + c * P, k * F + (c + 1) * P)
                        nc.tensor.matmul(o, wgu_hi[e % 2][:, w], x2T_hi[:, toks], start=True, stop=False)
                        nc.tensor.matmul(o, wgu_hi[e % 2][:, w], x2T_lo[:, toks], start=False, stop=False)
                        nc.tensor.matmul(o, wgu_lo[e % 2][:, w], x2T_hi[:, toks], start=False,
                                         stop=True).then_inc(done, 1)
                m = n - 1
                if is_slot(i, m):
                    e, half, c = expert_of(m)
                    need(pe, hid_ok, i, XPER, m + 1)
                    if c == 0:
                        need(pe, y_ok, i, 2 * T, T * (e - 1) + (half + 1) * QT)
                        if isinstance(i, int) and i == 0 and m < 4:
                            pe.wait_ge(w_ok, 1)
                    for k in range(QT):
                        last = nc.tensor.matmul((turned, attn_o)[half][:, k * D:(k + 1) * D],
                                                hid[m % 2][:, k * P:(k + 1) * P],
                                                wd[:, bass.ds(i * (2 * FC * D) + (e * FC + c) * D, D)],
                                                start=(c == 0 and k == 0), stop=(c == FC - 1), skip_group_check=True)
                    last.then_inc(d_mm, 1)

            run_expert_slots(pe, expert_slot)


_INS = ['x', 'ctx_1024', 'mask_BxS2_bf1', 'g_xattn', 'g_ffn', 'L0_xattn_ln_x_g', 'L0_xattn_ln_x_b', 'L0_xattn_ln_l_g',
        'L0_xattn_ln_l_b', 'L0_xattn_qn_g', 'L0_xattn_kn_g', 'L0_xattn_Wq', 'L0_xattn_Wkv', 'L0_xattn_Wout',
        'L0_xattn_bout', 'L0_ffn_kernel_router_DE', 'L0_ffn_kernel_gating_EDF', 'L0_ffn_kernel_up_EDF',
        'L0_ffn_kernel_down_EFD']
_OUTS = [((2, 512, 128), 'float32')]


def kernel(**inputs):
    import numpy as _np
    import concourse.bacc as _bacc
    from concourse import mybir as _mybir
    from concourse.bass_utils import run_bass_kernel_spmd as _run

    nc = _bacc.Bacc("TRN2", target_bir_lowering=False, num_devices=1)
    arrays, args = {}, []
    for name in _INS:
        a = _np.ascontiguousarray(inputs[name])
        arrays[f"in_{name}_dram"] = a
        args.append(nc.dram_tensor(f"in_{name}_dram", a.shape, _mybir.dt.from_np(a.dtype), kind="ExternalInput").ap())
    for k, (shape, dtype) in enumerate(_OUTS):
        dt = _mybir.dt.from_np(_np.dtype(dtype))
        args.append(nc.dram_tensor(f"out_{k}_dram", shape, dt, kind="ExternalOutput").ap())
    flamingo_gated_block(nc, *args)
    r = _run(nc, [arrays], core_ids=[0])
    got = tuple(r.results[0][f"out_{k}_dram"] for k in range(len(_OUTS)))
    return got[0]
```

```python
from contextlib import ExitStack

import concourse.bass as bass
from concourse import mybir

P = 128
F32 = mybir.dt.float32
F32R = mybir.dt.float32r
F16 = mybir.dt.float16
BF16 = mybir.dt.bfloat16
U8 = mybir.dt.uint8
ALU = mybir.AluOpType
ACT = mybir.ActivationFunctionType
AX_X = mybir.AxisListType.X

LN_EPS = 1e-5
RMS_EPS = 1e-8
V_SCALE = 32.0
MASKED = 1e30


def flamingo_gated_block(nc, x, ctx_in, mask, g_xattn, g_ffn, ln_x_g, ln_x_b, ln_l_g, ln_l_b, qn_g, kn_g,
                         Wq, Wkv, Wout, bout, router, w_gate, w_up, w_down, out):
    B, N, D = x.shape
    C = ctx_in.shape[1]
    DH = qn_g.shape[0]
    INNER = Wq.shape[1]
    H = INNER // DH
    HG = 4
    NG = H // HG
    GC = HG * DH
    QT = N // P
    T = B * QT
    KEYS = N + C
    UNIT = QT * HG
    UNITS = B * NG
    ITEMS = UNITS * UNIT
    PER = B * UNIT
    KSTEPS = HG + 1
    TILES = QT + 1
    E, _, F = w_gate.shape
    FC = F // P
    W3 = 3 * GC

    with ExitStack() as ctx:
        def sb(name, shape, dt):
            return ctx.enter_context(nc.sbuf_tensor(name, shape, dt))

        def ps(name, shape, dt):
            return ctx.enter_context(nc.psum_tensor(name, shape, dt))

        def sem(name):
            return ctx.enter_context(nc.semaphore(name))

        scores = [ps(f"scores{k}", [P, 1024], F32) for k in range(2)]
        turned = ps("turned", [P, 512], F32)
        attn_o = ps("attn_o", [P, 512], F32)
        proj_qk = ps("proj_qk", [P, 512], F32)
        proj_v = ps("proj_v", [P, 512], F32)

        x_sb = sb("x_sb", [P, T, D], F32)
        ctx_sb = sb("ctx_sb", [B * C, D], F32)
        gains = sb("gains", [P, 4], F32)
        head_gains = sb("head_gains", [P, 2, DH], F32)
        head_gain = sb("head_gain", [P, DH], F32)
        bout_b = sb("bout_b", [P, D], F32)
        gates = sb("gates", [P, 2], F32)
        gates_t = sb("gates_t", [P, 2], F32)
        mask_u8 = sb("mask_u8", [1, B * C], U8)
        mask_row = sb("mask_row", [1, B * C], BF16)
        ones_row = sb("ones_row", [1, P], BF16)
        ident = sb("ident", [P, P], F32)
        ident_h = sb("ident_h", [P, P], F16)
        falling = sb("falling", [P, E], F32)
        wqkv = sb("wqkv", [P, NG * W3], F32)
        wqkv_hi = sb("wqkv_hi", [P, NG * W3], F32R)
        wqkv_lo = sb("wqkv_lo", [P, NG * W3], F32R)
        wout = sb("wout", [P, H // 2, D], F32)
        wr = sb("wr", [P, E], F32)
        wr_hl = sb("wr_hl", [P, 2, E], F32R)
        wg = sb("wg", [P, E * F], F32)
        wu = sb("wu", [P, E * F], F32)
        wd = sb("wd", [P, E * FC * D], F32)

        stats = sb("stats", [P, T + 1, 6], F32)
        moments = sb("moments", [P, T + 1, 2], F32)
        ln_v = sb("ln_v", [P, 8, QT], F32)
        ln_l = sb("ln_l", [P, 8, QT], F32)
        ln_e = sb("ln_e", [P, 8, QT], F32)
        ln_t = sb("ln_t", [P, 8, 3, QT], F32)
        ln_r = sb("ln_r", [P, 8, QT], F32)
        ln_s = sb("ln_s", [P, T], F32)
        z = sb("z", [P, T + 1, D], F32)
        lnT = sb("lnT", [P, B * N + B * C], F32)
        LNW = B * N + (B - 1) * C + P
        lnT_hi = sb("lnT_hi", [P, LNW], F32R)
        lnT_lo = sb("lnT_lo", [P, LNW], F32R)

        squares = [sb(f"squares{k}", [P, 512], F32) for k in range(2)]
        sumsq = sb("sumsq", [P, 2, 8], F32)
        meansq = sb("meansq", [P, 2, 8], F32)
        rms_l = sb("rms_l", [P, 2, 8], F32)
        rms_e = sb("rms_e", [P, 2, 8], F32)
        rms_t = sb("rms_t", [P, 2, 3, 8], F32)
        rms_r = sb("rms_r", [P, 2, 8], F32)
        qk = [sb(f"qk{k}", [P, 512], F32) for k in range(2)]
        qk_hl = [sb(f"qk_hl{k}", [P, 8, 2, DH], F16) for k in range(2)]
        v_ctx = [sb(f"v_ctx{k}", [C, HG, 2, DH], F16) for k in range(B)]
        q_st = [sb(f"q_st{k}", [P, HG, N], F16) for k in range(B)]
        k_st = [sb(f"k_st{k}", [P, HG, KEYS], F16) for k in range(B)]
        k_sw = [sb(f"k_sw{k}", [P, HG, KEYS], F16) for k in range(B)]
        v_hl = [sb(f"v_hl{k}", [P, 2, QT, GC], F16) for k in range(B)]
        v_bd = [sb(f"v_bd{k}", [P, 2, GC], F16) for k in range(B)]

        NM, SUMS, RAW, SPLIT = 4, 4, 4, 4
        neg_max = sb("neg_max", [P, NM], F32)
        sums = sb("sums", [P, SUMS, HG], F32)
        sums_s = sb("sums_s", [P, 2, HG], F32)
        inv_sums = sb("inv_sums", [P, 2, HG], F32)
        probs = [sb(f"probs{k}", [P, HG, KEYS], F32) for k in range(2)]
        probs_c = [sb(f"probs_c{k}", [P, HG * C], F32) for k in range(2)]
        p_raw = [sb(f"p_raw{k}", [P, 512], F32) for k in range(RAW)]
        p_hi = [sb(f"p_hi{k}", [P, 512], F16) for k in range(SPLIT)]
        p_lo = [sb(f"p_lo{k}", [P, 512], F16) for k in range(SPLIT)]
        o_sb = sb("o_sb", [P, T * INNER], F32)

        oT = [q_st[k][:, :, :].rearrange("p h n -> p (h n)").bitcast(F32) for k in range(2)]
        spare = [probs[k][:, :, :].rearrange("p h n -> p (h n)") for k in range(2)]
        x1 = spare[0][:, 0:T * D].rearrange("p (t d) -> p t d", t=T)
        x1_t = spare[0][:, T * D:(T + 2) * D].rearrange("p (t d) -> p t d", t=2)
        x2T_hi = lnT_hi
        x2T_lo = lnT_lo
        x2T = lnT
        rt = k_st[0][:, :, :].rearrange("p h n -> p (h n)").bitcast(F32)[:, 0:16 * T * E].rearrange(
            "p (s t e) -> p s t e", s=16, t=T)
        rs = sb("rs", [P, 8, T], F32)
        w_tok = sb("w_tok", [P, T, E], F32)
        wgu_hi = [wqkv_hi[:, 2 * F * k:2 * F * (k + 1)] for k in range(2)]
        wgu_lo = [wqkv_lo[:, 2 * F * k:2 * F * (k + 1)] for k in range(2)]
        th = [p_raw[k] for k in range(2)]
        gt = [p_raw[2 + k] for k in range(2)]
        hid = [spare[1][:, 512 * k:512 * (k + 1)] for k in range(2)]

        x_in, ctx_inn, gains_in = sem("x_in"), sem("ctx_inn"), sem("gains_in")
        x_in2 = sem("x_in2")
        w0_in, w_in, rest_in, moe_in = sem("w0_in"), sem("w_in"), sem("rest_in"), sem("moe_in")
        const_z, const_ok, ident_h_ok = sem("const_z"), sem("const_ok"), sem("ident_h_ok")
        mask_ok, mask_f = sem("mask_ok"), sem("mask_f")
        head_gain_ok = sem("head_gain_ok")
        whi_ok, wlo_ok = sem("whi_ok"), sem("wlo_ok")
        bn_ok, var_ok, lnl_ok, lne_ok, newton = sem("bn_ok"), sem("var_ok"), sem("lnl_ok"), sem("lne_ok"), sem("newton")
        z_ok, zT_ok, lnT_ok, lnhi_ok, lnlo_ok = sem("z_ok"), sem("zT_ok"), sem("lnT_ok"), sem("lnhi_ok"), sem("lnlo_ok")
        qk_mm, sq_ok, ss_ok, ms_ok, rl_ok, re_ok = (sem(n) for n in
                                                   ("qk_mm", "sq_ok", "ss_ok", "ms_ok", "rl_ok", "re_ok"))
        rms_step, norm_ok, gain_ok, qkhi_ok, qklo_ok = (sem(n) for n in
                                                        ("rms_step", "norm_ok", "gain_ok", "qkhi_ok", "qklo_ok"))
        qkT_ok, qkst_ok, v_mm, vhi_ok, vlo_ok = (sem(n) for n in ("qkT_ok", "qkst_ok", "v_mm", "vhi_ok", "vlo_ok"))
        ksw_ok, vbd_ok = sem("ksw_ok"), sem("vbd_ok")
        s_ok, max_ok, exp_ok, pT_ok, raw_ok, phi_ok, plo_ok, pv_ok = (sem(n) for n in (
            "s_ok", "max_ok", "exp_ok", "pT_ok", "raw_ok", "phi_ok", "plo_ok", "pv_ok"))
        pack_ok, den_ok, o_ok = sem("pack_ok"), sem("den_ok"), sem("o_ok")
        oT_mm, oTa_ok, oTv_ok, y_mm, x1t_ok, x1_ok = (sem(n) for n in
                                                      ("oT_mm", "oTa_ok", "oTv_ok", "y_mm", "x1t_ok", "x1_ok"))
        gates_in = sem("gates_in")
        gate_ok, wr_ok = sem("gate_ok"), sem("wr_ok")
        z2_ok, z2T_ok, x2T_ok, x2hi_ok, x2lo_ok, logit_ok = (sem(n) for n in (
            "z2_ok", "z2T_ok", "x2T_ok", "x2hi_ok", "x2lo_ok", "logit_ok"))
        rt_step, rt_exp_in, rt_exp, w_ok = sem("rt_step"), sem("rt_exp_in"), sem("rt_exp"), sem("w_ok")
        wsp_hi, wsp_lo, g_mm, u_mm, th_ok, gt_ok, hid_ok, d_mm, y_ok = (sem(n) for n in (
            "wsp_hi", "wsp_lo", "g_mm", "u_mm", "th_ok", "gt_ok", "hid_ok", "d_mm", "y_ok"))
        out_ok = sem("out_ok")

        def need(eng, s, i, per, c):
            if isinstance(i, int):
                if per * i + c > 0:
                    eng.wait_ge(s, per * i + c)
            else:
                eng.wait_ge(s, i * per + max(c, 1))

        FIRST = 9
        QK_SLOT = [-7, -4, -1, 2, 5]
        V_SLOT = [2, 5, 8, 11, 14]
        T_SLOT = [s + 7 for s in QK_SLOT]

        FIRST_QK = [s - UNIT + 3 for s in range(TILES)]
        first_shift = {id(QK_SLOT): FIRST_QK, id(T_SLOT): [s + 5 for s in FIRST_QK],
                       id(V_SLOT): [s + 7 for s in FIRST_QK]}

        WEIGHTS = [-6, -5, -4]
        BATCH1 = -8

        def is_first(i, u):
            return isinstance(i, int) and B * i + u == 0

        def qk_bank(i, u, t):
            return (scores[1][:, 512:1024], scores[0][:, 0:512], scores[0][:, 512:1024], scores[1][:, 0:512],
                    proj_qk[:, :])[t] if is_first(i, u) else proj_qk[:, :]

        def turn_bank(i, u, t):
            return ((attn_o, turned)[t % 2] if is_first(i, u) else proj_v)[:, :].bitcast(F16)

        def is_item(i, n):
            return not isinstance(i, int) or 0 <= PER * i + n < ITEMS

        def units_at(i, n):
            for u, s in ((n // UNIT + 1, n % UNIT), (n // UNIT + 2, n % UNIT - UNIT)):
                if s >= QK_SLOT[0] and (not isinstance(i, int) or 0 <= B * i + u < UNITS):
                    yield u, s

        def tiles_at(i, n, slots, lag):
            for u, s in units_at(i, n):
                for t, at in enumerate(slots):
                    if is_first(i, u):
                        at = first_shift[id(slots)][t] + UNIT
                    if at + lag == s:
                        yield u, t, TILES * u + t

        def run_slots(eng, slot):
            for n in range(FIRST_QK[0], FIRST):
                slot(0, n)
            with eng.Fori(0, NG - 1) as i:
                for n in range(FIRST, FIRST + PER):
                    slot(i, n)
            for n in range(FIRST, PER + 8):
                slot(NG - 1, n)

        def rows_cols(t):
            return (C, GC) if t == 0 else (P, 0)

        def steps_of(i, n):
            k = KSTEPS * (n // HG) + n % HG
            if n % HG == 0 and is_item(i, n - 1):
                yield k - 1, True
            if is_item(i, n):
                yield k, False

        KP = KSTEPS * PER // HG
        TP = TILES * B
        GP = PER // HG

        CH_B0A, CH_CTX, CH_B0B, CH_B1A, CH_B1B, CH_2A, CH_2B = range(7)
        CHAIN_ROWS = [P, B * C, P, P, P, P, P]
        CHAIN_COLS = [QT, 1, QT, QT, QT, QT, QT]

        XPER = 2 * B * FC
        XFIRST = 6
        XSLOTS = E * B * FC

        def is_slot(i, n):
            return not isinstance(i, int) or 0 <= XPER * i + n < XSLOTS

        def run_expert_slots(eng, slot):
            for n in range(-2, XFIRST):
                slot(0, n)
            with eng.Fori(0, E // 2 - 1) as i:
                for n in range(XFIRST, XFIRST + XPER):
                    slot(i, n)
            for n in range(XFIRST, XPER + 4):
                slot(E // 2 - 1, n)

        def expert_of(n):
            return n // 4, (n % 4) // FC, n % FC

        block = ctx.enter_context(nc.Block())

        @block.sync
        def _(sp):
            x_v = x.rearrange("b (t p) d -> p (b t) d", p=P)
            sp.dma_start(x_sb[:, 0:QT, :], x_v[:, 0:QT, :]).then_inc(x_in, 16)
            wq_v = Wq.rearrange("d (g c) -> d g c", g=NG)
            wkv_v = Wkv.rearrange("d (k g c) -> d k g c", k=2, g=NG)
            w_v = wqkv[:, :].rearrange("p (g k c) -> p g k c", g=NG, k=3)
            for k, g in enumerate((ln_l_g, ln_l_b, ln_x_g, ln_x_b)):
                sp.dma_start(gains[:, k:k + 1], g.unsqueeze(1)).then_inc(gains_in, 16)
            sp.dma_start(w_v[:, 0, 0, :], wq_v[:, 0, :]).then_inc(w0_in, 16)
            sp.dma_start(w_v[:, 0, 1:3, :], wkv_v[:, :, 0, :]).then_inc(w0_in, 16)
            sp.dma_start(x_sb[:, QT:T, :], x_v[:, QT:T, :]).then_inc(x_in2, 16)
            sp.dma_start(head_gains[:, 0, :], qn_g.partition_broadcast(P)).then_inc(gains_in, 16)
            sp.dma_start(head_gains[:, 1, :], kn_g.partition_broadcast(P)).then_inc(gains_in, 16)
            sp.dma_start(mask_u8[:, :], mask.rearrange("b c -> (b c)").unsqueeze(0)).then_inc(gains_in, 16)
            sp.dma_start(w_v[:, 1:NG, 0, :], wq_v[:, 1:NG, :]).then_inc(w_in, 16)
            sp.dma_start(w_v[:, 1:NG, 1, :], wkv_v[:, 0, 1:NG, :]).then_inc(w_in, 16)
            sp.dma_start(w_v[:, 1:NG, 2, :], wkv_v[:, 1, 1:NG, :]).then_inc(w_in, 16)
            sp.dma_start(bout_b[:, :], bout.partition_broadcast(P)).then_inc(rest_in, 16)
            sp.dma_start(wr[:, :], router).then_inc(rest_in, 16)
            sp.dma_start(wout[:, :, :], Wout.rearrange("(c p) d -> p c d", p=P)).then_inc(rest_in, 16)
            sp.dma_start(wg[:, :].rearrange("p (e f) -> p e f", e=E), w_gate.rearrange("e d f -> d e f")).then_inc(moe_in, 16)
            sp.dma_start(wu[:, :].rearrange("p (e f) -> p e f", e=E), w_up.rearrange("e d f -> d e f")).then_inc(moe_in, 16)
            sp.dma_start(wd[:, :].rearrange("p (e c d) -> p e c d", e=E, c=FC),
                         w_down.rearrange("e (c p) d -> p e c d", p=P)).then_inc(moe_in, 16)

            def slot(i, n):
                for u, t, tau in tiles_at(i, n, V_SLOT, 1):
                    if t == 0:
                        if isinstance(i, int):
                            need(sp, vlo_ok, i, TP, tau + 1)
                        else:
                            need(sp, o_ok, i, GP, QT * (u - 1))
                        for h in range(HG):
                            sp.dma_start(
                                v_bd[u % B][C * h:C * (h + 1), :, DH * h:DH * (h + 1)],
                                v_ctx[u % B][:, h, :, :]).then_inc(vbd_ok, 16)
                for u, t, tau in tiles_at(i, n, T_SLOT, 1):
                    if t == TILES - 1:
                        need(sp, qkst_ok, i, TP, tau + 1)
                        sp.dma_start(k_sw[u % B][0:DH, :, :], k_st[u % B][DH:P, :, :]).then_inc(ksw_ok, 16)
                        sp.dma_start(k_sw[u % B][DH:P, :, :], k_st[u % B][0:DH, :, :]).then_inc(ksw_ok, 16)

            sp.wait_ge(const_ok, 1)
            run_slots(sp, slot)
            out_v = out.rearrange("b (t p) d -> p (b t) d", p=P)
            for half in range(B):
                sp.wait_ge(y_ok, (E - 1) * B * QT + (half + 1) * QT)
                sp.dma_start(out_v[:, half * QT:(half + 1) * QT, :], x1[:, half * QT:(half + 1) * QT, :]).then_inc(out_ok, 16)
            sp.wait_ge(out_ok, 16 * B)

        @block.gpsimd
        def _(pool):
            nc.gpsimd.memset(ident[:, :], 0.0).then_inc(const_z, 1)
            nc.gpsimd.memset(ones_row[:, :], 1.0)
            for e in range(E):
                nc.gpsimd.memset(falling[:, e:e + 1], float(E - e))
            pool.wait_ge(const_z, 1)
            nc.gpsimd.affine_select(out=ident[:, :], in_=ident[:, :], compare_op=ALU.not_equal, fill=1.0, base=0,
                                    pattern=[[-1, P]], channel_multiplier=1).then_inc(ident_h_ok, 1)
            for part in (lnT_hi, lnT_lo):
                nc.gpsimd.memset(part[:, B * (N + C):LNW].bitcast(F32), 0.0)
            for k in range(2):
                nc.gpsimd.memset(qk_hl[k][:, :, :, :], 0.0)
            for k in range(B):
                last = nc.gpsimd.memset(v_bd[k][:, :, :], 0.0)
            last.then_inc(const_ok, 1)
            def weights_lo(g):
                pool.wait_ge(whi_ok, g + 1)
                cols = slice(g * W3, (g + 1) * W3)
                nc.gpsimd.tensor_tensor(wqkv_lo[:, cols], wqkv[:, cols], wqkv_hi[:, cols].bitcast(F32),
                                        ALU.subtract).then_inc(wlo_ok, 1)

            weights_lo(0)
            pool.wait_ge(head_gain_ok, 1)

            def slot(i, n):
                if isinstance(i, int) and i == 0 and n - 5 in WEIGHTS:
                    weights_lo(1 + WEIGHTS.index(n - 5))
                for u, t, tau in tiles_at(i, n, QK_SLOT, 3):
                    if t:
                        need(pool, norm_ok, i, TP, tau + 1)
                        q = qk[tau % 2][:, 0:GC].rearrange("p (h d) -> p h d", d=DH)
                        nc.gpsimd.tensor_tensor(q, q, head_gain[:, :].unsqueeze(1).broadcast_to([P, HG, DH]),
                                                ALU.mult).then_inc(gain_ok, 1)
                for u, t, tau in [x for lag in (4, 5) for x in tiles_at(i, n, QK_SLOT, lag)
                                  if is_first(i, x[0]) == (lag == 4)]:
                    rows, c0 = rows_cols(t)
                    need(pool, qkhi_ok, i, TP, tau + 1)
                    hl = qk_hl[tau % 2]
                    nc.gpsimd.tensor_tensor(
                        hl[0:rows, c0 // DH:8, 1, :], qk[tau % 2][0:rows, c0:512].rearrange("p (h d) -> p h d", d=DH),
                        hl[0:rows, c0 // DH:8, 0, :], ALU.subtract).then_inc(qklo_ok, 1)
                for k, is_ctx in steps_of(i, n - 3):
                    w = P if is_ctx else 512
                    need(pool, phi_ok, i, KP, k + 1)
                    need(pool, pv_ok, i, KP, k + 1 - SPLIT)
                    nc.gpsimd.tensor_tensor(p_lo[k % SPLIT][:, 0:w], p_raw[k % RAW][:, 0:w], p_hi[k % SPLIT][:, 0:w],
                                            ALU.subtract).then_inc(plo_ok, 1)

            run_slots(pool, slot)

            def expert_slot(i, n):
                e, half, c = expert_of(n + 2)
                if (n + 2) % 4 == 0 and is_slot(i, n + 2):
                    need(pool, wsp_hi, i, 4, 2 * e + 2)
                    need(pool, u_mm, i, XPER, 4 * (e - 1))
                    for k, w in enumerate((wg, wu)):
                        nc.gpsimd.tensor_tensor(wgu_lo[e % 2][:, k * F:(k + 1) * F], w[:, bass.ds(i * (2 * F) + e * F, F)],
                                                wgu_hi[e % 2][:, k * F:(k + 1) * F].bitcast(F32),
                                                ALU.subtract).then_inc(wsp_lo, 1)

            run_expert_slots(pool, expert_slot)

        @block.scalar
        def _(act):
            act.dma_start(gates[:, 0:1], g_xattn.partition_broadcast(P)).then_inc(gates_in, 16)
            act.dma_start(gates[:, 1:2], g_ffn.partition_broadcast(P)).then_inc(gates_in, 16)
            act.dma_start(ctx_sb[:, :], ctx_in.rearrange("b c d -> (b c) d")).then_inc(ctx_inn, 16)
            nc.scalar.preload_act_table_set("exp_and_others")
            act.wait_ge(gates_in, 32)
            nc.scalar.activation(gates_t[:, :], gates[:, :], ACT.Tanh).then_inc(gate_ok, 1)
            nc.scalar.preload_act_table_set("natural_log_exp_and_others")

            def rsqrt_start(c):
                r, n = CHAIN_ROWS[c], CHAIN_COLS[c]
                act.wait_ge(var_ok, c + 1)
                nc.scalar.activation(ln_l[0:r, c, 0:n], ln_v[0:r, c, 0:n], ACT.Ln).then_inc(lnl_ok, 1)
                act.wait_ge(lnl_ok, c + 1)
                nc.scalar.activation(ln_e[0:r, c, 0:n], ln_l[0:r, c, 0:n], ACT.Exp, scale=-0.5).then_inc(lne_ok, 1)

            def weights_hi(g):
                act.wait_ge(w0_in if g == 0 else w_in, 32 if g == 0 else 48)
                nc.scalar.copy(wqkv_hi[:, g * W3:(g + 1) * W3], wqkv[:, g * W3:(g + 1) * W3]).then_inc(whi_ok, 1)

            rsqrt_start(CH_B0A)
            rsqrt_start(CH_CTX)
            weights_hi(0)
            rsqrt_start(CH_B0B)
            rsqrt_start(CH_B1A)
            act.wait_ge(gains_in, 16 * 7)

            def with_gain(k, bank, cols, g):
                act.wait_ge(zT_ok, k + 1)
                w = cols.stop - cols.start
                nc.scalar.activation(lnT[:, cols], bank[:, 0:w], ACT.Identity, scale=gains[:, g:g + 1],
                                     bias=gains[:, g + 1:g + 2]).then_inc(lnT_ok, 1)

            with_gain(0, turned, slice(B * N, B * N + B * C), 2)
            with_gain(1, proj_qk, slice(0, N), 0)
            rsqrt_start(CH_B1B)

            def raw(i, k, w):
                need(act, pT_ok, i, KP, k + 1)
                need(act, plo_ok, i, KP, k + 1 - RAW)
                nc.scalar.copy(p_raw[k % RAW][:, 0:w], turned[:, 0:w]).then_inc(raw_ok, 1)

            def slot(i, n):
                if isinstance(i, int) and i == 0:
                    if n == BATCH1:
                        with_gain(2, turned, slice(N, B * N), 0)
                    if n in WEIGHTS:
                        weights_hi(1 + WEIGHTS.index(n))
                rms = list(tiles_at(i, n, QK_SLOT, 2))
                m = n - 1
                if is_item(i, m):
                    g = m // HG
                    need(act, max_ok, i, PER, m + 1)
                    need(act, pT_ok, i, KP, KSTEPS * (g - 1))
                    need(act, o_ok, i, GP, g - SUMS + 1)
                    nc.scalar.activation(probs[g % 2][:, m % HG, :], scores[m % 2][:, 0:KEYS], ACT.Exp,
                                         bias=neg_max[:, m % NM:m % NM + 1],
                                         accum_out=sums[:, g % SUMS, m % HG:m % HG + 1]).then_inc(exp_ok, 1)
                for u, t, tau in rms:
                    rows, c0 = rows_cols(t)
                    need(act, ms_ok, i, TP, tau + 1)
                    nc.scalar.activation(rms_l[0:rows, tau % 2, c0 // DH:8], meansq[0:rows, tau % 2, c0 // DH:8],
                                         ACT.Ln).then_inc(rl_ok, 1)
                for u, t, tau in rms:
                    rows, c0 = rows_cols(t)
                    need(act, rl_ok, i, TP, tau + 1)
                    nc.scalar.activation(rms_e[0:rows, tau % 2, c0 // DH:8], rms_l[0:rows, tau % 2, c0 // DH:8],
                                         ACT.Exp, scale=-0.5).then_inc(re_ok, 1)
                steps = list(steps_of(i, n - 2))
                if steps and steps[0][1]:
                    raw(i, steps[0][0], P)
                for u, t, tau in tiles_at(i, n, V_SLOT, 0):
                    rows, _ = rows_cols(t)
                    need(act, v_mm, i, TP, tau + 1)
                    if t == 0:
                        need(act, vbd_ok, i, 16 * HG * B, 16 * HG * (u - 1))
                        o = v_ctx[u % B][:, :, 0, :]
                        p = proj_v[0:C, 0:GC].rearrange("p (h d) -> p h d", d=DH)
                    else:
                        need(act, pv_ok, i, KP, KSTEPS * QT * (u - 1) - 1)
                        o = v_hl[u % B][:, 0, t - 1, :]
                        p = proj_v[:, 0:GC]
                    nc.scalar.activation(o, p, ACT.Copy, scale=V_SCALE).then_inc(vhi_ok, 1)
                for u, t, tau in tiles_at(i, n, QK_SLOT, 1):
                    rows, c0 = rows_cols(t)
                    need(act, qk_mm, i, TP, tau + 1)
                    need(act, ss_ok, i, TP, tau - 1)
                    nc.scalar.activation(squares[tau % 2][0:rows, c0:512], qk_bank(i, u, t)[0:rows, c0:512],
                                         ACT.Square).then_inc(sq_ok, 1)
                for u, t, tau in tiles_at(i, n, T_SLOT, 1):
                    need(act, qkT_ok, i, TP, tau + 1)
                    need(act, s_ok, i, PER, UNIT * (u - 1))
                    tr = turn_bank(i, u, t)
                    if t == 0:
                        nc.scalar.copy(k_st[u % B][:, :, N:KEYS],
                                       tr[:, 512:1024].rearrange("p (h c) -> p h c", c=P)[:, :, 0:C]).then_inc(qkst_ok, 1)
                    else:
                        cols = slice((t - 1) * P, t * P)
                        nc.scalar.copy(q_st[u % B][:, :, cols], tr[:, 0:512].rearrange("p (h c) -> p h c", c=P))
                        nc.scalar.copy(k_st[u % B][:, :, cols],
                                       tr[:, 512:1024].rearrange("p (h c) -> p h c", c=P)).then_inc(qkst_ok, 1)
                if steps and not steps[-1][1]:
                    raw(i, steps[-1][0], 512)

            run_slots(act, slot)

            for t in range(T):
                act.wait_ge(oT_mm, t + 1)
                if t >= 2:
                    act.wait_ge(y_mm, t - 1)
                nc.scalar.copy(oT[t % 2][:, 0:512], scores[t % 2][:, 0:512]).then_inc(oTa_ok, 1)
            rsqrt_start(CH_2A)
            rsqrt_start(CH_2B)
            for b in range(B):
                act.wait_ge(z2T_ok, b + 1)
                nc.scalar.copy(x2T[:, b * N:(b + 1) * N], (turned, attn_o)[b][:, :]).then_inc(x2T_ok, 1)
                act.wait_ge(x2T_ok, b + 1)
                nc.scalar.copy(x2T_hi[:, b * N:(b + 1) * N], x2T[:, b * N:(b + 1) * N]).then_inc(x2hi_ok, 1)
            act.wait_ge(rt_exp_in, 1)
            nc.scalar.activation(rt[:, 1, :, :], rt[:, 0, :, :], ACT.Exp).then_inc(rt_exp, 1)
            act.wait_ge(rt_exp_in, 2)
            nc.scalar.activation(rs[:, 5, :], rs[:, 4, :], ACT.Exp).then_inc(rt_exp, 1)
            act.wait_ge(moe_in, 48)

            def expert_slot(i, n):
                e, half, c = expert_of(n + 2)
                if (n + 2) % 4 == 0 and is_slot(i, n + 2):
                    need(act, u_mm, i, XPER, 4 * (e - 1))
                    for k, w in enumerate((wg, wu)):
                        nc.scalar.copy(wgu_hi[e % 2][:, k * F:(k + 1) * F],
                                       w[:, bass.ds(i * (2 * F) + e * F, F)]).then_inc(wsp_hi, 1)
                if is_slot(i, n):
                    need(act, g_mm, i, XPER, n + 1)
                    need(act, gt_ok, i, XPER, n - 1)
                    nc.scalar.activation(th[n % 2][:, :], scores[n % 2][:, 0:512], ACT.Tanh, scale=0.5).then_inc(th_ok, 1)

            run_expert_slots(act, expert_slot)

        @block.vector
        def _(dve):
            def norm_stats(k, rows, src):
                nc.vector.bn_stats(stats[0:rows, k, :], src).then_inc(bn_ok, 1)

            def norm_moments(k, rows, done):
                dve.wait_ge(bn_ok, done)
                return nc.vector.bn_aggr(moments[0:rows, k, :], stats[0:rows, k, :])

            step = [0]

            def link(ins):
                step[0] += 1
                ins.then_inc(newton, 1)
                dve.wait_ge(newton, step[0])

            def rsqrt_finish(c):
                r, n = CHAIN_ROWS[c], CHAIN_COLS[c]
                v, e = ln_v[0:r, c, 0:n], ln_e[0:r, c, 0:n]
                a = [ln_t[0:r, c, k, 0:n] for k in range(3)]
                dve.wait_ge(lne_ok, c + 1)
                link(nc.vector.tensor_tensor(a[0], e, e, ALU.mult))
                link(nc.vector.tensor_tensor(a[1], a[0], v, ALU.mult))
                link(nc.vector.tensor_scalar(a[2], a[1], -0.5, 1.5, ALU.mult, ALU.add))
                link(nc.vector.tensor_tensor(ln_r[0:r, c, 0:n], a[2], e, ALU.mult))

            def first_norm(b, c):
                tiles = range(b * QT, (b + 1) * QT)
                dve.wait_ge(x_in if b == 0 else x_in2, 16)
                done = bn[0]
                for t in tiles:
                    norm_stats(t, P, x_sb[:, t, :])
                    bn[0] += 1
                for k, t in enumerate(tiles):
                    last = norm_moments(t, P, done + k + 1)
                link(last)
                nc.vector.tensor_scalar(ln_v[:, c, :], moments[:, b * QT:(b + 1) * QT, 1], LN_EPS, None,
                                        ALU.add).then_inc(var_ok, 1)

            def second_norm(b, c1, c2):
                var = moments[:, b * QT:(b + 1) * QT, 1]
                link(nc.vector.tensor_tensor(ln_t[:, c2, 0, :], ln_r[:, c1, :], ln_r[:, c1, :], ALU.mult))
                link(nc.vector.tensor_tensor(ln_t[:, c2, 1, :], ln_t[:, c2, 0, :], var, ALU.mult))
                nc.vector.tensor_scalar(ln_v[:, c2, :], ln_t[:, c2, 1, :], LN_EPS, None, ALU.add).then_inc(var_ok, 1)

            def normalise(b, c1, c2):
                link(nc.vector.tensor_tensor(ln_s[:, b * QT:(b + 1) * QT], ln_r[:, c1, :], ln_r[:, c2, :], ALU.mult))
                for t in range(b * QT, (b + 1) * QT):
                    nc.vector.tensor_scalar(z[:, t, :], x_sb[:, t, :], moments[:, t, 0:1], ln_s[:, t:t + 1],
                                            ALU.subtract, ALU.mult).then_inc(z_ok, 1)

            def split_ln(k, cols):
                dve.wait_ge(lnT_ok, k + 1)
                nc.vector.tensor_copy(lnT_hi[:, cols], lnT[:, cols]).then_inc(lnhi_ok, 1)
                dve.wait_ge(lnhi_ok, k + 1)
                nc.vector.tensor_tensor(lnT_lo[:, cols], lnT[:, cols], lnT_hi[:, cols].bitcast(F32),
                                        ALU.subtract).then_inc(lnlo_ok, 1)

            bn = [0]
            first_norm(0, CH_B0A)
            dve.wait_ge(ctx_inn, 16)
            norm_stats(T, B * C, ctx_sb[:, :])
            bn[0] += 1
            link(norm_moments(T, B * C, bn[0]))
            nc.vector.tensor_scalar(ln_v[0:B * C, CH_CTX, 0:1], moments[0:B * C, T, 1:2], LN_EPS, None,
                                    ALU.add).then_inc(var_ok, 1)
            rsqrt_finish(CH_B0A)
            second_norm(0, CH_B0A, CH_B0B)
            rsqrt_finish(CH_CTX)
            nc.vector.tensor_scalar(z[0:B * C, T, :], ctx_sb[:, :], moments[0:B * C, T, 0:1], ln_r[0:B * C, CH_CTX, 0:1],
                                    ALU.subtract, ALU.mult).then_inc(z_ok, 1)
            first_norm(1, CH_B1A)
            rsqrt_finish(CH_B0B)
            normalise(0, CH_B0A, CH_B0B)
            rsqrt_finish(CH_B1A)
            second_norm(1, CH_B1A, CH_B1B)
            dve.wait_ge(ident_h_ok, 1)
            nc.vector.tensor_copy(ident_h[:, :], ident[:, :]).then_inc(ident_h_ok, 1)
            dve.wait_ge(gains_in, 16 * 7)
            nc.vector.scalar_tensor_tensor(out=head_gain[:, :], in0=head_gains[:, 0, :], scalar=DH ** -0.5,
                                           in1=head_gains[:, 1, :], op0=ALU.mult, op1=ALU.mult).then_inc(head_gain_ok, 1)
            nc.vector.tensor_scalar(mask_row[:, :], mask_u8[:, :], 1.0, MASKED, ALU.subtract, ALU.mult).then_inc(mask_ok, 1)
            dve.wait_ge(const_ok, 1)
            split_ln(0, slice(B * N, B * N + B * C))
            split_ln(1, slice(0, N))
            rsqrt_finish(CH_B1B)
            normalise(1, CH_B1A, CH_B1B)

            def newton_step(i, n, k):
                for u, t, tau in tiles_at(i, n, QK_SLOT, 2):
                    rows, c0 = rows_cols(t)
                    h0 = c0 // DH
                    e = rms_e[0:rows, tau % 2, h0:8]
                    a = [rms_t[0:rows, tau % 2, j, h0:8] for j in range(2)]
                    if k == 0:
                        need(dve, re_ok, i, TP, tau + 1)
                        nc.vector.tensor_tensor(a[0], e, meansq[0:rows, tau % 2, h0:8], ALU.mult).then_inc(rms_step, 1)
                    elif k == 1:
                        need(dve, rms_step, i, 3 * TP, 3 * tau + 1)
                        nc.vector.scalar_tensor_tensor(out=a[1], in0=a[0], scalar=-0.5, in1=e, op0=ALU.mult,
                                                       op1=ALU.mult).then_inc(rms_step, 1)
                    else:
                        need(dve, rms_step, i, 3 * TP, 3 * tau + 2)
                        nc.vector.scalar_tensor_tensor(out=rms_r[0:rows, tau % 2, h0:8], in0=a[1], scalar=1.5, in1=e,
                                                       op0=ALU.add, op1=ALU.mult).then_inc(rms_step, 1)

            def slot(i, n):
                if isinstance(i, int) and n == BATCH1:
                    split_ln(2, slice(N, B * N))
                if n % HG == 1 and is_item(i, n - 9):
                    g = (n - 9) // HG
                    need(dve, pv_ok, i, KP, KSTEPS * (g + 1))
                    need(dve, den_ok, i, 2 * GP, 2 * g + 2)
                    if g % QT == QT - 1 and (not isinstance(i, int) or B * i + g // QT + 2 < UNITS):
                        need(dve, vlo_ok, i, TP, TILES * (g // QT + 2) + 1)
                    u, qt = g // QT, g % QT
                    t = (u % B) * QT + qt
                    o = o_sb[:, bass.ds(i * GC + (t * INNER + (u // B) * GC), GC)].rearrange("p (h d) -> p h d", d=DH)
                    nc.vector.tensor_tensor(o, attn_o[:, 0:GC].rearrange("p (h d) -> p h d", d=DH),
                                            inv_sums[:, g % 2, :].unsqueeze(2).broadcast_to([P, HG, DH]),
                                            ALU.mult).then_inc(o_ok, 1)
                if is_item(i, n):
                    need(dve, s_ok, i, PER, n + 1)
                    need(dve, exp_ok, i, PER, n + 1 - NM)
                    nc.vector.tensor_reduce(neg_max[:, n % NM:n % NM + 1], scores[n % 2][:, 0:KEYS], AX_X, ALU.max,
                                            negate=True).then_inc(max_ok, 1)
                for k, is_ctx in steps_of(i, n - 3):
                    w = P if is_ctx else 512
                    need(dve, raw_ok, i, KP, k + 1)
                    need(dve, pv_ok, i, KP, k + 1 - SPLIT)
                    nc.vector.tensor_copy(p_hi[k % SPLIT][:, 0:w], p_raw[k % RAW][:, 0:w]).then_inc(phi_ok, 1)
                newton_step(i, n, 0)
                if n % HG == 1 and is_item(i, n - 2):
                    g = (n - 2) // HG
                    need(dve, exp_ok, i, PER, n - 1)
                    need(dve, pT_ok, i, KP, KSTEPS * (g - 1))
                    nc.vector.tensor_copy(probs_c[g % 2][:, :].rearrange("p (h c) -> p h c", c=C),
                                          probs[g % 2][:, :, N:KEYS]).then_inc(pack_ok, 1)
                if n % HG == 2 and is_item(i, n - 3):
                    g = (n - 3) // HG
                    need(dve, exp_ok, i, PER, n - 2)
                    nc.vector.tensor_scalar(sums_s[:, g % 2, :], sums[:, g % SUMS, :], V_SCALE, None,
                                            ALU.mult).then_inc(den_ok, 1)
                newton_step(i, n, 1)
                for u, t, tau in tiles_at(i, n, V_SLOT, 0):
                    need(dve, vhi_ok, i, TP, tau + 1)
                    if t == 0:
                        hi, lo = v_ctx[u % B][:, :, 0, :], v_ctx[u % B][:, :, 1, :]
                        p = proj_v[0:C, 0:GC].rearrange("p (h d) -> p h d", d=DH)
                    else:
                        hi, lo = v_hl[u % B][:, 0, t - 1, :], v_hl[u % B][:, 1, t - 1, :]
                        p = proj_v[:, 0:GC]
                    nc.vector.scalar_tensor_tensor(out=lo, in0=p, scalar=V_SCALE, in1=hi, op0=ALU.mult,
                                                   op1=ALU.subtract).then_inc(vlo_ok, 1)
                newton_step(i, n, 2)
                if n % HG == 2 and is_item(i, n - 3):
                    g = (n - 3) // HG
                    need(dve, den_ok, i, 2 * GP, 2 * g + 1)
                    need(dve, o_ok, i, GP, g - 1)
                    nc.vector.reciprocal(inv_sums[:, g % 2, :], sums_s[:, g % 2, :]).then_inc(den_ok, 1)
                for u, t, tau in tiles_at(i, n, QK_SLOT, 2):
                    rows, c0 = rows_cols(t)
                    need(dve, rms_step, i, 3 * TP, 3 * tau + 3)
                    need(dve, qklo_ok, i, TP, tau - 1)
                    nc.vector.tensor_tensor(qk[tau % 2][0:rows, c0:512].rearrange("p (h d) -> p h d", d=DH),
                                            qk_bank(i, u, t)[0:rows, c0:512].rearrange("p (h d) -> p h d", d=DH),
                                            rms_r[0:rows, tau % 2, c0 // DH:8].unsqueeze(2).broadcast_to(
                                                [rows, 8 - c0 // DH, DH]), ALU.mult).then_inc(norm_ok, 1)
                for u, t, tau in tiles_at(i, n, QK_SLOT, 3):
                    rows, c0 = rows_cols(t)
                    if t:
                        need(dve, gain_ok, i, B * QT, QT * u + t)
                    else:
                        need(dve, norm_ok, i, TP, tau + 1)
                    need(dve, qkT_ok, i, TP, tau - 1)
                    nc.vector.tensor_copy(qk_hl[tau % 2][0:rows, c0 // DH:8, 0, :],
                                          qk[tau % 2][0:rows, c0:512].rearrange("p (h d) -> p h d", d=DH)).then_inc(qkhi_ok, 1)
                for u, t, tau in tiles_at(i, n, QK_SLOT, 1):
                    rows, c0 = rows_cols(t)
                    h0 = c0 // DH
                    need(dve, sq_ok, i, TP, tau + 1)
                    need(dve, norm_ok, i, TP, tau - 1)
                    nc.vector.tensor_reduce(sumsq[0:rows, tau % 2, h0:8],
                                            squares[tau % 2][0:rows, c0:512].rearrange("p (h d) -> p h d", d=DH),
                                            AX_X, ALU.add).then_inc(ss_ok, 1)
                    need(dve, ss_ok, i, TP, tau + 1)
                    nc.vector.tensor_scalar(meansq[0:rows, tau % 2, h0:8], sumsq[0:rows, tau % 2, h0:8], 1.0 / DH,
                                            RMS_EPS ** 2, ALU.mult, ALU.max).then_inc(ms_ok, 1)

            run_slots(dve, slot)

            def oT_half(t):
                dve.wait_ge(oT_mm, t + 1)
                if t >= 2:
                    dve.wait_ge(y_mm, t - 1)
                nc.vector.tensor_copy(oT[t % 2][:, 512:1024], scores[t % 2][:, 512:1024]).then_inc(oTv_ok, 1)

            dve.wait_ge(rest_in, 16 * 3)
            nc.vector.tensor_copy(wr_hl[:, 0, :], wr[:, :]).then_inc(wr_ok, 1)
            dve.wait_ge(wr_ok, 1)
            nc.vector.tensor_tensor(wr_hl[:, 1, :], wr[:, :], wr_hl[:, 0, :].bitcast(F32), ALU.subtract).then_inc(wr_ok, 1)
            dve.wait_ge(gate_ok, 1)
            oT_half(0)
            for t in range(T):
                if t + 1 < T:
                    oT_half(t + 1)
                dve.wait_ge(y_mm, t + 1)
                y = (proj_qk, proj_v)[t % 2][:, 0:D]
                link(nc.vector.tensor_tensor(x1_t[:, t % 2, :], y, bout_b[:, :], ALU.add))
                nc.vector.scalar_tensor_tensor(out=x1[:, t, :], in0=x1_t[:, t % 2, :], scalar=gates_t[:, 0:1],
                                               in1=x_sb[:, t, :], op0=ALU.mult, op1=ALU.add).then_inc(x1_ok, 1)
                dve.wait_ge(x1_ok, t + 1)
                norm_stats(t, P, x1[:, t, :])
                bn[0] += 1
                link(norm_moments(t, P, bn[0]))
                if t % QT == QT - 1:
                    b = t // QT
                    nc.vector.tensor_scalar(ln_v[:, CH_2A + b, :], moments[:, b * QT:(b + 1) * QT, 1], LN_EPS, None,
                                            ALU.add).then_inc(var_ok, 1)
            for b in range(B):
                rsqrt_finish(CH_2A + b)
                for t in range(b * QT, (b + 1) * QT):
                    nc.vector.tensor_scalar(z[:, t, :], x1[:, t, :], moments[:, t, 0:1],
                                            ln_r[:, CH_2A + b, t % QT:t % QT + 1], ALU.subtract,
                                            ALU.mult).then_inc(z2_ok, 1)
            for b in range(B):
                cols = slice(b * N, (b + 1) * N)
                dve.wait_ge(x2hi_ok, b + 1)
                nc.vector.tensor_tensor(x2T_lo[:, cols], x2T[:, cols], x2T_hi[:, cols].bitcast(F32),
                                        ALU.subtract).then_inc(x2lo_ok, 1)

            def over(v):
                return v.unsqueeze(2).broadcast_to([P, T, E])

            fall = falling[:, :].unsqueeze(1).broadcast_to([P, T, E])
            rstep = [0]

            def rlink(ins):
                rstep[0] += 1
                ins.then_inc(rt_step, 1)
                dve.wait_ge(rt_step, rstep[0])

            dve.wait_ge(logit_ok, T)
            lg = turned[:, 0:T * 2 * E].rearrange("p (t k e) -> p t k e", t=T, k=2)
            rlink(nc.vector.tensor_copy(rt[:, 2, :, :], lg[:, :, 0, :]))
            rlink(nc.vector.tensor_tensor(rt[:, 3, :, :], rt[:, 2, :, :], lg[:, :, 1, :], ALU.add))
            rlink(nc.vector.tensor_reduce(rs[:, 0, :], rt[:, 3, :, :], AX_X, ALU.max))
            nc.vector.tensor_tensor(rt[:, 0, :, :], rt[:, 3, :, :], over(rs[:, 0, :]), ALU.subtract).then_inc(rt_exp_in, 1)
            dve.wait_ge(rt_exp, 1)
            rlink(nc.vector.tensor_reduce(rs[:, 1, :], rt[:, 1, :, :], AX_X, ALU.add))
            rlink(nc.vector.reciprocal(rs[:, 2, :], rs[:, 1, :]))
            rlink(nc.vector.tensor_tensor(rt[:, 4, :, :], rt[:, 1, :, :], over(rs[:, 2, :]), ALU.mult))
            best = [rs[:, 3, :], rs[:, 6, :]]
            hot = []
            prob = rt[:, 4, :, :]
            for k in range(2):
                a = [rt[:, 5 + 4 * k + j, :, :] for j in range(4)]
                pos = rs[:, 7, :] if k else rs[:, 0, :]
                rlink(nc.vector.tensor_reduce(best[k], prob, AX_X, ALU.max))
                rlink(nc.vector.tensor_tensor(a[0], prob, over(best[k]), ALU.is_ge))
                rlink(nc.vector.tensor_tensor(a[1], a[0], fall, ALU.mult))
                rlink(nc.vector.tensor_reduce(pos, a[1], AX_X, ALU.max))
                rlink(nc.vector.tensor_tensor(a[2], a[1], over(pos), ALU.is_equal))
                hot.append(a[2])
                if k == 0:
                    rlink(nc.vector.scalar_tensor_tensor(out=a[3], in0=a[2], scalar=-2.0, in1=prob, op0=ALU.mult,
                                                         op1=ALU.add))
                    prob = a[3]
            nc.vector.tensor_tensor(rs[:, 4, :], best[1], best[0], ALU.subtract).then_inc(rt_exp_in, 1)
            dve.wait_ge(rt_exp, 2)
            rlink(nc.vector.tensor_scalar(rs[:, 0, :], rs[:, 5, :], 1.0, None, ALU.add))
            rlink(nc.vector.reciprocal(rs[:, 1, :], rs[:, 0, :]))
            dve.wait_ge(gate_ok, 1)
            rlink(nc.vector.tensor_scalar(rs[:, 2, :], rs[:, 1, :], gates_t[:, 1:2], 0.5, ALU.mult, ALU.mult))
            rlink(nc.vector.tensor_tensor(rs[:, 7, :], rs[:, 2, :], rs[:, 5, :], ALU.mult))
            rlink(nc.vector.tensor_tensor(rt[:, 13, :, :], hot[0], over(rs[:, 2, :]), ALU.mult))
            rlink(nc.vector.tensor_tensor(rt[:, 14, :, :], hot[1], over(rs[:, 7, :]), ALU.mult))
            nc.vector.tensor_tensor(w_tok[:, :, :], rt[:, 13, :, :], rt[:, 14, :, :], ALU.add).then_inc(w_ok, 1)
            dve.wait_ge(w_ok, 1)

            def expert_slot(i, n):
                if is_slot(i, n):
                    need(dve, th_ok, i, XPER, n + 1)
                    need(dve, hid_ok, i, XPER, n - 1)
                    nc.vector.scalar_tensor_tensor(out=gt[n % 2][:, :], in0=th[n % 2][:, :], scalar=1.0,
                                                   in1=scores[n % 2][:, 0:512], op0=ALU.add,
                                                   op1=ALU.mult).then_inc(gt_ok, 1)
                    need(dve, gt_ok, i, XPER, n + 1)
                    need(dve, u_mm, i, XPER, n + 1)
                    need(dve, d_mm, i, XPER, n - 1)
                    nc.vector.tensor_tensor(hid[n % 2][:, :], gt[n % 2][:, :], scores[n % 2][:, 512:1024],
                                            ALU.mult).then_inc(hid_ok, 1)
                m = n - 2
                if is_slot(i, m) and m % FC == FC - 1:
                    e, half, _ = expert_of(m)
                    need(dve, d_mm, i, XPER, m + 1)
                    for k in range(QT):
                        t = half * QT + k
                        need(dve, y_ok, i, 2 * T, T * (e - 1) + t + 1)
                        nc.vector.scalar_tensor_tensor(
                            out=x1[:, t, :], in0=(turned, attn_o)[half][:, k * D:(k + 1) * D],
                            scalar=w_tok[:, t, bass.ds(i * 2 + e, 1)], in1=x1[:, t, :], op0=ALU.mult,
                            op1=ALU.add).then_inc(y_ok, 1)

            run_expert_slots(dve, expert_slot)

        @block.tensor
        def _(pe):
            pe.wait_ge(ident_h_ok, 1)
            pe.wait_ge(z_ok, 1)
            nc.tensor.transpose(turned[:, 0:B * C], z[0:B * C, T, :], ident[0:B * C, 0:B * C]).then_inc(zT_ok, 1)
            def turn_rows(b, bank):
                for t in range(QT):
                    pe.wait_ge(z_ok, 1 + b * QT + t + 1)
                    last = nc.tensor.transpose(bank[:, t * P:(t + 1) * P], z[:, b * QT + t, :], ident[:, :])
                last.then_inc(zT_ok, 1)

            turn_rows(0, proj_qk)
            pe.wait_ge(ident_h_ok, 2)
            pe.wait_ge(mask_ok, 1)

            def project(i, u, t, out_ap, c0, cols):
                first = B * N + (u % B) * C if t == 0 else (u % B) * N + (t - 1) * P
                toks = slice(first, first + P)
                w = bass.ds(i * W3 + ((u // B) * W3 + c0), cols)
                nc.tensor.matmul(out_ap, lnT_hi[:, toks], wqkv_hi[:, w], start=True, stop=False)
                nc.tensor.matmul(out_ap, lnT_hi[:, toks], wqkv_lo[:, w], start=False, stop=False)
                return nc.tensor.matmul(out_ap, lnT_lo[:, toks], wqkv_hi[:, w], start=False, stop=True)

            def proj_v_free(i, u, s):
                jobs = sorted([(a, 0, t) for t, a in enumerate(V_SLOT)] + [(a, 1, t) for t, a in enumerate(T_SLOT)])
                k = jobs.index(s)
                v, (_, kind, t) = (u, jobs[k - 1]) if k else (u - 1, jobs[-1])
                need(pe, (vlo_ok, qkst_ok)[kind], i, TP, TILES * v + t + 1)

            def times_values(i, k, cols, o, vh, vl, wait, start, stop):
                hi, lo = p_hi[k % SPLIT], p_lo[k % SPLIT]
                if wait:
                    need(pe, phi_ok, i, KP, k + 1)
                nc.tensor.matmul(o, hi[:, cols], vh, start=start, stop=False, skip_group_check=True)
                nc.tensor.matmul(o, hi[:, cols], vl, start=False, stop=False, skip_group_check=True)
                if wait:
                    need(pe, plo_ok, i, KP, k + 1)
                return nc.tensor.matmul(o, lo[:, cols], vh, start=False, stop=stop, skip_group_check=True)

            def slot(i, n):
                if isinstance(i, int) and n == BATCH1:
                    pe.wait_ge(lnT_ok, 1)
                    turn_rows(1, turned)
                if (n - 5) % HG == 0 and is_item(i, n - 6):
                    u = (n - 6) // UNIT
                    if (n - 6) % UNIT == HG - 1:
                        need(pe, vbd_ok, i, 16 * HG * B, 16 * HG * (u + 1))
                    times_values(i, KSTEPS * ((n - 5) // HG) - 1, slice(0, P), attn_o[:, 0:GC], v_bd[u % B][:, 0, :],
                                 v_bd[u % B][:, 1, :], True, False, True).then_inc(pv_ok, 1)
                if is_item(i, n):
                    u, qt, h = n // UNIT, (n % UNIT) // HG, n % HG
                    b = u % B
                    if n % UNIT == 0:
                        need(pe, qkst_ok, i, TP, TILES * (u + 1))
                        need(pe, ksw_ok, i, 32 * B, 32 * (u + 1))
                    need(pe, exp_ok, i, PER, n - 1)
                    q = q_st[b][:, h, qt * P:(qt + 1) * P]
                    s = scores[n % 2]
                    nc.tensor.matmul(s[:, 0:N], q, k_st[b][:, h, 0:N], start=True, stop=False)
                    nc.tensor.matmul(s[:, N:KEYS], q, k_st[b][:, h, N:KEYS], start=True, stop=False)
                    nc.tensor.matmul(s[:, 0:N], q, k_sw[b][:, h, 0:N], start=False, stop=True)
                    nc.tensor.matmul(s[:, N:KEYS], q, k_sw[b][:, h, N:KEYS], start=False, stop=False)
                    nc.tensor.matmul(s[:, N:KEYS], ones_row[:, :], mask_row[:, b * C:(b + 1) * C], start=False,
                                     stop=True).then_inc(s_ok, 1)
                for u, t, tau in tiles_at(i, n, V_SLOT, 0):
                    if not is_first(i, u):
                        proj_v_free(i, u, (V_SLOT[t], 0, t))
                    elif t:
                        need(pe, vlo_ok, i, TP, tau)
                    project(i, u, t, proj_v[:, 0:GC], 2 * GC, GC).then_inc(v_mm, 1)
                if (n - 2) % HG == 0 and is_item(i, n - 3):
                    g = (n - 3) // HG
                    need(pe, pack_ok, i, GP, g + 1)
                    need(pe, raw_ok, i, KP, KSTEPS * g + HG)
                    nc.tensor.transpose(turned[:, 0:P], probs_c[g % 2][:, :], ident[:, :]).then_inc(pT_ok, 1)
                if is_item(i, n - 2):
                    m = n - 2
                    k = KSTEPS * (m // HG) + m % HG
                    need(pe, exp_ok, i, PER, m + 1)
                    need(pe, raw_ok, i, KP, k)
                    for c in range(QT):
                        last = nc.tensor.transpose(turned[:, c * P:(c + 1) * P],
                                                   probs[(m // HG) % 2][:, m % HG, c * P:(c + 1) * P], ident[:, :])
                    last.then_inc(pT_ok, 1)
                for u, t, tau in tiles_at(i, n, QK_SLOT, 0):
                    need(pe, wlo_ok, i, 1, u // B + 1)
                    if isinstance(i, int) and i == 0 and u < B:
                        pe.wait_ge(lnlo_ok, (2 if u == 0 else 3) if t else 1)
                        if u == 0 and t == TILES - 1:
                            pe.wait_ge(lnT_ok, 2)
                    if not is_first(i, u):
                        need(pe, norm_ok, i, TP, tau)
                    _, c0 = rows_cols(t)
                    project(i, u, t, qk_bank(i, u, t)[:, c0:512], c0, 2 * GC - c0).then_inc(qk_mm, 1)
                for u, t, tau in tiles_at(i, n, T_SLOT, 0):
                    if not is_first(i, u):
                        proj_v_free(i, u, (T_SLOT[t], 1, t))
                    elif t == 1:
                        pe.wait_ge(lnT_ok, 3)
                    elif t > 1:
                        need(pe, qkst_ok, i, TP, tau - 1)
                    need(pe, qklo_ok, i, TP, tau + 1)
                    _, c0 = rows_cols(t)
                    tr = turn_bank(i, u, t)
                    for j in range(c0 // DH, 8):
                        last = nc.tensor.transpose(tr[:, j * P:(j + 1) * P], qk_hl[tau % 2][:, j, :, :], ident_h[:, :])
                    last.then_inc(qkT_ok, 1)
                if is_item(i, n - 5):
                    m = n - 5
                    u, h = m // UNIT, m % HG
                    if m % UNIT == 0:
                        need(pe, vlo_ok, i, TP, TILES * (u + 1))
                    if h == 0:
                        need(pe, o_ok, i, GP, m // HG)
                    k = KSTEPS * (m // HG) + h
                    for c in range(QT):
                        vh, vl = (v_hl[u % B][:, part, c, h * DH:(h + 1) * DH] for part in range(2))
                        last = times_values(i, k, slice(c * P, (c + 1) * P), attn_o[:, h * DH:(h + 1) * DH], vh, vl,
                                            c == 0, h == 0 and c == 0, False)
                    last.then_inc(pv_ok, 1)

            run_slots(pe, slot)

            def turn(t):
                if t < 2:
                    pe.wait_ge(o_ok, NG * T)
                else:
                    pe.wait_ge(oTa_ok, t - 1)
                    pe.wait_ge(oTv_ok, t - 1)
                for c in range(H // 2):
                    last = nc.tensor.transpose(scores[t % 2][:, c * P:(c + 1) * P],
                                               o_sb[:, t * INNER + c * P:t * INNER + (c + 1) * P], ident[:, :])
                last.then_inc(oT_mm, 1)

            turn(0)
            pe.wait_ge(rest_in, 16 * 3)
            for t in range(T):
                if t + 1 < T:
                    turn(t + 1)
                pe.wait_ge(oTa_ok, t + 1)
                pe.wait_ge(oTv_ok, t + 1)
                if t >= 2:
                    pe.wait_ge(x1_ok, t - 1)
                y = (proj_qk, proj_v)[t % 2][:, 0:D]
                for c in range(H // 2):
                    last = nc.tensor.matmul(y, oT[t % 2][:, c * P:(c + 1) * P], wout[:, c, :], start=(c == 0),
                                            stop=(c == H // 2 - 1))
                last.then_inc(y_mm, 1)
            for b in range(B):
                for t in range(QT):
                    pe.wait_ge(z2_ok, b * QT + t + 1)
                    last = nc.tensor.transpose((turned, attn_o)[b][:, t * P:(t + 1) * P], z[:, b * QT + t, :], ident[:, :])
                last.then_inc(z2T_ok, 1)
            for t in range(T):
                pe.wait_ge(x2lo_ok, t // QT + 1)
                if t == 0:
                    pe.wait_ge(wr_ok, 2)
                    pe.wait_ge(x2T_ok, 1)
                o = turned[:, t * 2 * E:(t + 1) * 2 * E]
                r = wr_hl[:, :, :].rearrange("p k e -> p (k e)")
                nc.tensor.matmul(o, x2T_hi[:, t * P:(t + 1) * P], r, start=True, stop=False)
                nc.tensor.matmul(o, x2T_lo[:, t * P:(t + 1) * P], r, start=False, stop=True).then_inc(logit_ok, 1)
            pe.wait_ge(moe_in, 48)

            def expert_slot(i, n):
                if is_slot(i, n):
                    e, half, c = expert_of(n)
                    toks = slice(half * N, (half + 1) * N)
                    if n % 4 == 0:
                        need(pe, wsp_lo, i, 4, 2 * e + 2)
                    if isinstance(i, int) and i == 0 and n < 4:
                        pe.wait_ge(x2lo_ok, B)
                    need(pe, hid_ok, i, XPER, n - 1)
                    for k, done in enumerate((g_mm, u_mm)):
                        o = scores[n % 2][:, k * 512:(k + 1) * 512]
                        w = slice(k * F + c * P, k * F + (c + 1) * P)
                        nc.tensor.matmul(o, wgu_hi[e % 2][:, w], x2T_hi[:, toks], start=True, stop=False)
                        nc.tensor.matmul(o, wgu_hi[e % 2][:, w], x2T_lo[:, toks], start=False, stop=False)
                        nc.tensor.matmul(o, wgu_lo[e % 2][:, w], x2T_hi[:, toks], start=False,
                                         stop=True).then_inc(done, 1)
                m = n - 1
                if is_slot(i, m):
                    e, half, c = expert_of(m)
                    need(pe, hid_ok, i, XPER, m + 1)
                    if c == 0:
                        need(pe, y_ok, i, 2 * T, T * (e - 1) + (half + 1) * QT)
                        if isinstance(i, int) and i == 0 and m < 4:
                            pe.wait_ge(w_ok, 1)
                    for k in range(QT):
                        last = nc.tensor.matmul((turned, attn_o)[half][:, k * D:(k + 1) * D],
                                                hid[m % 2][:, k * P:(k + 1) * P],
                                                wd[:, bass.ds(i * (2 * FC * D) + (e * FC + c) * D, D)],
                                                start=(c == 0 and k == 0), stop=(c == FC - 1), skip_group_check=True)
                    last.then_inc(d_mm, 1)

            run_expert_slots(pe, expert_slot)


_INS = ['x', 'ctx_1024', 'mask_BxS2_bf1', 'g_xattn', 'g_ffn', 'L0_xattn_ln_x_g', 'L0_xattn_ln_x_b', 'L0_xattn_ln_l_g',
        'L0_xattn_ln_l_b', 'L0_xattn_qn_g', 'L0_xattn_kn_g', 'L0_xattn_Wq', 'L0_xattn_Wkv', 'L0_xattn_Wout',
        'L0_xattn_bout', 'L0_ffn_kernel_router_DE', 'L0_ffn_kernel_gating_EDF', 'L0_ffn_kernel_up_EDF',
        'L0_ffn_kernel_down_EFD']
_OUTS = [((2, 512, 128), 'float32')]


def kernel(**inputs):
    import numpy as _np
    import concourse.bacc as _bacc
    from concourse import mybir as _mybir
    from concourse.bass_utils import run_bass_kernel_spmd as _run

    nc = _bacc.Bacc("TRN2", target_bir_lowering=False, num_devices=1)
    arrays, args = {}, []
    for name in _INS:
        a = _np.ascontiguousarray(inputs[name])
        arrays[f"in_{name}_dram"] = a
        args.append(nc.dram_tensor(f"in_{name}_dram", a.shape, _mybir.dt.from_np(a.dtype), kind="ExternalInput").ap())
    for k, (shape, dtype) in enumerate(_OUTS):
        dt = _mybir.dt.from_np(_np.dtype(dtype))
        args.append(nc.dram_tensor(f"out_{k}_dram", shape, dt, kind="ExternalOutput").ap())
    flamingo_gated_block(nc, *args)
    r = _run(nc, [arrays], core_ids=[0])
    got = tuple(r.results[0][f"out_{k}_dram"] for k in range(len(_OUTS)))
    return got[0]
```

```python
from contextlib import ExitStack

import concourse.bass as bass
from concourse import mybir

P = 128
F32 = mybir.dt.float32
F32R = mybir.dt.float32r
F16 = mybir.dt.float16
BF16 = mybir.dt.bfloat16
U8 = mybir.dt.uint8
ALU = mybir.AluOpType
ACT = mybir.ActivationFunctionType
AX_X = mybir.AxisListType.X

LN_EPS = 1e-5
RMS_EPS = 1e-8
V_SCALE = 32.0
MASKED = 1e30


def flamingo_gated_block(nc, x, ctx_in, mask, g_xattn, g_ffn, ln_x_g, ln_x_b, ln_l_g, ln_l_b, qn_g, kn_g,
                         Wq, Wkv, Wout, bout, router, w_gate, w_up, w_down, out):
    B, N, D = x.shape
    C = ctx_in.shape[1]
    DH = qn_g.shape[0]
    INNER = Wq.shape[1]
    H = INNER // DH
    HG = 4
    NG = H // HG
    GC = HG * DH
    QT = N // P
    T = B * QT
    KEYS = N + C
    UNIT = QT * HG
    UNITS = B * NG
    ITEMS = UNITS * UNIT
    PER = B * UNIT
    KSTEPS = HG + 1
    TILES = QT + 1
    E, _, F = w_gate.shape
    FC = F // P
    W3 = 3 * GC

    with ExitStack() as ctx:
        def sb(name, shape, dt):
            return ctx.enter_context(nc.sbuf_tensor(name, shape, dt))

        def ps(name, shape, dt):
            return ctx.enter_context(nc.psum_tensor(name, shape, dt))

        def sem(name):
            return ctx.enter_context(nc.semaphore(name))

        scores = [ps(f"scores{k}", [P, 1024], F32) for k in range(2)]
        turned = ps("turned", [P, 512], F32)
        attn_o = ps("attn_o", [P, 512], F32)
        proj_qk = ps("proj_qk", [P, 512], F32)
        proj_v = ps("proj_v", [P, 512], F32)

        x_sb = sb("x_sb", [P, T, D], F32)
        ctx_sb = sb("ctx_sb", [B * C, D], F32)
        gains = sb("gains", [P, 4], F32)
        head_gains = sb("head_gains", [P, 2, DH], F32)
        head_gain = sb("head_gain", [P, DH], F32)
        bout_b = sb("bout_b", [P, D], F32)
        gates = sb("gates", [P, 2], F32)
        gates_t = sb("gates_t", [P, 2], F32)
        mask_u8 = sb("mask_u8", [1, B * C], U8)
        mask_row = sb("mask_row", [1, B * C], BF16)
        ones_row = sb("ones_row", [1, P], BF16)
        ident = sb("ident", [P, P], F32)
        ident_h = sb("ident_h", [P, P], F16)
        falling = sb("falling", [P, E], F32)
        wqkv = sb("wqkv", [P, NG * W3], F32)
        wqkv_hi = sb("wqkv_hi", [P, NG * W3], F32R)
        wqkv_lo = sb("wqkv_lo", [P, NG * W3], F32R)
        wout = sb("wout", [P, H // 2, D], F32)
        wr = sb("wr", [P, E], F32)
        wr_hl = sb("wr_hl", [P, 2, E], F32R)
        wg = sb("wg", [P, E * F], F32)
        wu = sb("wu", [P, E * F], F32)
        wd = sb("wd", [P, E * FC * D], F32)

        stats = sb("stats", [P, T + 1, 6], F32)
        moments = sb("moments", [P, T + 1, 2], F32)
        ln_v = sb("ln_v", [P, 8, QT], F32)
        ln_l = sb("ln_l", [P, 8, QT], F32)
        ln_e = sb("ln_e", [P, 8, QT], F32)
        ln_t = sb("ln_t", [P, 8, 3, QT], F32)
        ln_r = sb("ln_r", [P, 8, QT], F32)
        ln_s = sb("ln_s", [P, T], F32)
        z = sb("z", [P, T + 1, D], F32)
        lnT = sb("lnT", [P, B * N + B * C], F32)
        LNW = B * N + (B - 1) * C + P
        lnT_hi = sb("lnT_hi", [P, LNW], F32R)
        lnT_lo = sb("lnT_lo", [P, LNW], F32R)

        squares = [sb(f"squares{k}", [P, 512], F32) for k in range(2)]
        sumsq = sb("sumsq", [P, 2, 8], F32)
        meansq = sb("meansq", [P, 2, 8], F32)
        rms_l = sb("rms_l", [P, 2, 8], F32)
        rms_e = sb("rms_e", [P, 2, 8], F32)
        rms_t = sb("rms_t", [P, 2, 3, 8], F32)
        rms_r = sb("rms_r", [P, 2, 8], F32)
        qk = [sb(f"qk{k}", [P, 512], F32) for k in range(2)]
        qk_hl = [sb(f"qk_hl{k}", [P, 8, 2, DH], F16) for k in range(2)]
        v_ctx = [sb(f"v_ctx{k}", [C, HG, 2, DH], F16) for k in range(B)]
        q_st = [sb(f"q_st{k}", [P, HG, N], F16) for k in range(B)]
        k_st = [sb(f"k_st{k}", [P, HG, KEYS], F16) for k in range(B)]
        k_sw = [sb(f"k_sw{k}", [P, HG, KEYS], F16) for k in range(B)]
        v_hl = [sb(f"v_hl{k}", [P, 2, QT, GC], F16) for k in range(B)]
        v_bd = [sb(f"v_bd{k}", [P, 2, GC], F16) for k in range(B)]

        NM, SUMS, RAW, SPLIT = 4, 4, 4, 4
        neg_max = sb("neg_max", [P, NM], F32)
        sums = sb("sums", [P, SUMS, HG], F32)
        sums_s = sb("sums_s", [P, 2, HG], F32)
        inv_sums = sb("inv_sums", [P, 2, HG], F32)
        probs = [sb(f"probs{k}", [P, HG, KEYS], F32) for k in range(2)]
        probs_c = [sb(f"probs_c{k}", [P, HG * C], F32) for k in range(2)]
        p_raw = [sb(f"p_raw{k}", [P, 512], F32) for k in range(RAW)]
        p_hi = [sb(f"p_hi{k}", [P, 512], F16) for k in range(SPLIT)]
        p_lo = [sb(f"p_lo{k}", [P, 512], F16) for k in range(SPLIT)]
        o_sb = sb("o_sb", [P, T * INNER], F32)

        oT = [q_st[k][:, :, :].rearrange("p h n -> p (h n)").bitcast(F32) for k in range(2)]
        spare = [probs[k][:, :, :].rearrange("p h n -> p (h n)") for k in range(2)]
        x1 = v_hl[0][:, :, :, :].rearrange("p k t c -> p (k t c)").bitcast(F32).rearrange("p (t d) -> p t d", t=T)
        x1_t = k_sw[0][:, :, :].rearrange("p h n -> p (h n)").bitcast(F32)[:, 0:2 * D].rearrange(
            "p (t d) -> p t d", t=2)
        x2T_hi = lnT_hi
        x2T_lo = lnT_lo
        x2T = lnT
        rt = k_st[0][:, :, :].rearrange("p h n -> p (h n)").bitcast(F32)[:, 0:16 * T * E].rearrange(
            "p (s t e) -> p s t e", s=16, t=T)
        rs = sb("rs", [P, 8, T], F32)
        w_tok = sb("w_tok", [P, T, E], F32)
        wgu_hi = [wqkv_hi[:, 2 * F * k:2 * F * (k + 1)] for k in range(2)]
        wgu_lo = [wqkv_lo[:, 2 * F * k:2 * F * (k + 1)] for k in range(2)]
        th = [p_raw[k] for k in range(2)]
        gt = [p_raw[2 + k] for k in range(2)]
        hid = [spare[1][:, 512 * k:512 * (k + 1)] for k in range(2)]

        x_in, ctx_inn, gains_in = sem("x_in"), sem("ctx_inn"), sem("gains_in")
        x_in2 = sem("x_in2")
        w0_in, w_in, rest_in, moe_in = sem("w0_in"), sem("w_in"), sem("rest_in"), sem("moe_in")
        const_z, const_ok, ident_h_ok = sem("const_z"), sem("const_ok"), sem("ident_h_ok")
        mask_ok, mask_f = sem("mask_ok"), sem("mask_f")
        head_gain_ok = sem("head_gain_ok")
        whi_ok, wlo_ok = sem("whi_ok"), sem("wlo_ok")
        bn_ok, var_ok, lnl_ok, lne_ok, newton = sem("bn_ok"), sem("var_ok"), sem("lnl_ok"), sem("lne_ok"), sem("newton")
        z_ok, zT_ok, lnT_ok, lnhi_ok, lnlo_ok = sem("z_ok"), sem("zT_ok"), sem("lnT_ok"), sem("lnhi_ok"), sem("lnlo_ok")
        qk_mm, sq_ok, ss_ok, ms_ok, rl_ok, re_ok = (sem(n) for n in
                                                   ("qk_mm", "sq_ok", "ss_ok", "ms_ok", "rl_ok", "re_ok"))
        rms_step, norm_ok, gain_ok, qkhi_ok, qklo_ok = (sem(n) for n in
                                                        ("rms_step", "norm_ok", "gain_ok", "qkhi_ok", "qklo_ok"))
        qkT_ok, qkst_ok, v_mm, vhi_ok, vlo_ok = (sem(n) for n in ("qkT_ok", "qkst_ok", "v_mm", "vhi_ok", "vlo_ok"))
        ksw_ok, vbd_ok = sem("ksw_ok"), sem("vbd_ok")
        s_ok, max_ok, exp_ok, pT_ok, raw_ok, phi_ok, plo_ok, pv_ok = (sem(n) for n in (
            "s_ok", "max_ok", "exp_ok", "pT_ok", "raw_ok", "phi_ok", "plo_ok", "pv_ok"))
        pack_ok, den_ok, o_ok = sem("pack_ok"), sem("den_ok"), sem("o_ok")
        oT_mm, oTa_ok, y_mm, x1_ok = (sem(n) for n in ("oT_mm", "oTa_ok", "y_mm", "x1_ok"))
        gates_in = sem("gates_in")
        gate_ok, wr_ok = sem("gate_ok"), sem("wr_ok")
        z2_ok, z2T_ok, x2T_ok, x2hi_ok, x2lo_ok, logit_ok = (sem(n) for n in (
            "z2_ok", "z2T_ok", "x2T_ok", "x2hi_ok", "x2lo_ok", "logit_ok"))
        rt_step, rt_exp_in, rt_exp, w_ok = sem("rt_step"), sem("rt_exp_in"), sem("rt_exp"), sem("w_ok")
        wsp_hi, wsp_lo, g_mm, u_mm, th_ok, gt_ok, hid_ok, d_mm, y_ok = (sem(n) for n in (
            "wsp_hi", "wsp_lo", "g_mm", "u_mm", "th_ok", "gt_ok", "hid_ok", "d_mm", "y_ok"))
        out_ok = sem("out_ok")

        def need(eng, s, i, per, c):
            if isinstance(i, int):
                if per * i + c > 0:
                    eng.wait_ge(s, per * i + c)
            else:
                eng.wait_ge(s, i * per + max(c, 1))

        FIRST = 9
        QK_SLOT = [-7, -4, -1, 2, 5]
        V_SLOT = [2, 5, 8, 11, 14]
        T_SLOT = [s + 7 for s in QK_SLOT]

        FIRST_QK = [s - UNIT + 3 for s in range(TILES)]
        first_shift = {id(QK_SLOT): FIRST_QK, id(T_SLOT): [s + 5 for s in FIRST_QK],
                       id(V_SLOT): [s + 7 for s in FIRST_QK]}

        WEIGHTS = [-6, -5, -4]
        BATCH1 = -8

        def is_first(i, u):
            return isinstance(i, int) and B * i + u == 0

        def qk_bank(i, u, t):
            return (scores[1][:, 512:1024], scores[0][:, 0:512], scores[0][:, 512:1024], scores[1][:, 0:512],
                    proj_qk[:, :])[t] if is_first(i, u) else proj_qk[:, :]

        def turn_bank(i, u, t):
            return ((attn_o, turned)[t % 2] if is_first(i, u) else proj_v)[:, :].bitcast(F16)

        def is_item(i, n):
            return not isinstance(i, int) or 0 <= PER * i + n < ITEMS

        def units_at(i, n):
            for u, s in ((n // UNIT + 1, n % UNIT), (n // UNIT + 2, n % UNIT - UNIT)):
                if s >= QK_SLOT[0] and (not isinstance(i, int) or 0 <= B * i + u < UNITS):
                    yield u, s

        def tiles_at(i, n, slots, lag):
            for u, s in units_at(i, n):
                for t, at in enumerate(slots):
                    if is_first(i, u):
                        at = first_shift[id(slots)][t] + UNIT
                    if at + lag == s:
                        yield u, t, TILES * u + t

        def run_slots(eng, slot):
            for n in range(FIRST_QK[0], FIRST):
                slot(0, n)
            with eng.Fori(0, NG - 1) as i:
                for n in range(FIRST, FIRST + PER):
                    slot(i, n)
            for n in range(FIRST, PER + 8):
                slot(NG - 1, n)

        def rows_cols(t):
            return (C, GC) if t == 0 else (P, 0)

        def steps_of(i, n):
            k = KSTEPS * (n // HG) + n % HG
            if n % HG == 0 and is_item(i, n - 1):
                yield k - 1, True
            if is_item(i, n):
                yield k, False

        KP = KSTEPS * PER // HG
        TP = TILES * B
        GP = PER // HG

        CH_B0A, CH_CTX, CH_B0B, CH_B1A, CH_B1B, CH_2A, CH_2B = range(7)
        CHAIN_ROWS = [P, B * C, P, P, P, P, P]
        CHAIN_COLS = [QT, 1, QT, QT, QT, QT, QT]

        XPER = 2 * B * FC
        XFIRST = 6
        XSLOTS = E * B * FC

        def is_slot(i, n):
            return not isinstance(i, int) or 0 <= XPER * i + n < XSLOTS

        def run_expert_slots(eng, slot):
            for n in range(-2, XFIRST):
                slot(0, n)
            with eng.Fori(0, E // 2 - 1) as i:
                for n in range(XFIRST, XFIRST + XPER):
                    slot(i, n)
            for n in range(XFIRST, XPER + 4):
                slot(E // 2 - 1, n)

        def expert_of(n):
            return n // 4, (n % 4) // FC, n % FC

        HALF = INNER // 2
        OUT_SLOT = [22, 25, 28, 31]
        NORM_SLOT = OUT_SLOT[-1] + 4

        def turned_o(j):
            return proj_v[:, 0:HALF] if j < 2 * QT else scores[j % 4 // 2][:, j % 2 * 512:j % 2 * 512 + HALF]

        def oT_half(j):
            return oT[0 if j < 2 * QT else j // 2 % 2][:, j % 2 * HALF:(j % 2 + 1) * HALF]

        def y_bank(t):
            return (proj_qk if t < QT or t % 2 == 0 else proj_v)[:, 0:D]

        def out_step(i, n, lag):
            return [t for t in range(QT) if isinstance(i, int) and i == NG - 1 and n == OUT_SLOT[t] + lag]

        def last_slots(i, n, k):
            return isinstance(i, int) and i == NG - 1 and n == NORM_SLOT + k

        def logits(b):
            return (turned, proj_v)[b][:, 0:QT * 2 * E]

        block = ctx.enter_context(nc.Block())

        @block.sync
        def _(sp):
            x_v = x.rearrange("b (t p) d -> p (b t) d", p=P)
            sp.dma_start(x_sb[:, 0:QT, :], x_v[:, 0:QT, :]).then_inc(x_in, 16)
            wq_v = Wq.rearrange("d (g c) -> d g c", g=NG)
            wkv_v = Wkv.rearrange("d (k g c) -> d k g c", k=2, g=NG)
            w_v = wqkv[:, :].rearrange("p (g k c) -> p g k c", g=NG, k=3)
            for k, g in enumerate((ln_l_g, ln_l_b, ln_x_g, ln_x_b)):
                sp.dma_start(gains[:, k:k + 1], g.unsqueeze(1)).then_inc(gains_in, 16)
            sp.dma_start(w_v[:, 0, 0, :], wq_v[:, 0, :]).then_inc(w0_in, 16)
            sp.dma_start(w_v[:, 0, 1:3, :], wkv_v[:, :, 0, :]).then_inc(w0_in, 16)
            sp.dma_start(x_sb[:, QT:T, :], x_v[:, QT:T, :]).then_inc(x_in2, 16)
            sp.dma_start(head_gains[:, 0, :], qn_g.partition_broadcast(P)).then_inc(gains_in, 16)
            sp.dma_start(head_gains[:, 1, :], kn_g.partition_broadcast(P)).then_inc(gains_in, 16)
            sp.dma_start(mask_u8[:, :], mask.rearrange("b c -> (b c)").unsqueeze(0)).then_inc(gains_in, 16)
            sp.dma_start(w_v[:, 1:NG, 0, :], wq_v[:, 1:NG, :]).then_inc(w_in, 16)
            sp.dma_start(w_v[:, 1:NG, 1, :], wkv_v[:, 0, 1:NG, :]).then_inc(w_in, 16)
            sp.dma_start(w_v[:, 1:NG, 2, :], wkv_v[:, 1, 1:NG, :]).then_inc(w_in, 16)
            sp.dma_start(bout_b[:, :], bout.partition_broadcast(P)).then_inc(rest_in, 16)
            sp.dma_start(wr[:, :], router).then_inc(rest_in, 16)
            sp.dma_start(wout[:, :, :], Wout.rearrange("(c p) d -> p c d", p=P)).then_inc(rest_in, 16)
            sp.dma_start(wg[:, :].rearrange("p (e f) -> p e f", e=E), w_gate.rearrange("e d f -> d e f")).then_inc(moe_in, 16)
            sp.dma_start(wu[:, :].rearrange("p (e f) -> p e f", e=E), w_up.rearrange("e d f -> d e f")).then_inc(moe_in, 16)
            sp.dma_start(wd[:, :].rearrange("p (e c d) -> p e c d", e=E, c=FC),
                         w_down.rearrange("e (c p) d -> p e c d", p=P)).then_inc(moe_in, 16)

            def slot(i, n):
                for u, t, tau in tiles_at(i, n, V_SLOT, 1):
                    if t == 0:
                        if isinstance(i, int):
                            need(sp, vlo_ok, i, TP, tau + 1)
                        else:
                            need(sp, o_ok, i, GP, QT * (u - 1))
                        for h in range(HG):
                            sp.dma_start(
                                v_bd[u % B][C * h:C * (h + 1), :, DH * h:DH * (h + 1)],
                                v_ctx[u % B][:, h, :, :]).then_inc(vbd_ok, 16)
                for u, t, tau in tiles_at(i, n, T_SLOT, 1):
                    if t == TILES - 1:
                        need(sp, qkst_ok, i, TP, tau + 1)
                        sp.dma_start(k_sw[u % B][0:DH, :, :], k_st[u % B][DH:P, :, :]).then_inc(ksw_ok, 16)
                        sp.dma_start(k_sw[u % B][DH:P, :, :], k_st[u % B][0:DH, :, :]).then_inc(ksw_ok, 16)

            sp.wait_ge(const_ok, 1)
            run_slots(sp, slot)
            out_v = out.rearrange("b (t p) d -> p (b t) d", p=P)
            for half in range(B):
                sp.wait_ge(y_ok, (E - 1) * B * QT + (half + 1) * QT)
                sp.dma_start(out_v[:, half * QT:(half + 1) * QT, :], x1[:, half * QT:(half + 1) * QT, :]).then_inc(out_ok, 16)
            sp.wait_ge(out_ok, 16 * B)

        @block.gpsimd
        def _(pool):
            nc.gpsimd.memset(ident[:, :], 0.0).then_inc(const_z, 1)
            nc.gpsimd.memset(ones_row[:, :], 1.0)
            for e in range(E):
                nc.gpsimd.memset(falling[:, e:e + 1], float(E - e))
            pool.wait_ge(const_z, 1)
            nc.gpsimd.affine_select(out=ident[:, :], in_=ident[:, :], compare_op=ALU.not_equal, fill=1.0, base=0,
                                    pattern=[[-1, P]], channel_multiplier=1).then_inc(ident_h_ok, 1)
            for part in (lnT_hi, lnT_lo):
                nc.gpsimd.memset(part[:, B * (N + C):LNW].bitcast(F32), 0.0)
            for k in range(2):
                nc.gpsimd.memset(qk_hl[k][:, :, :, :], 0.0)
            for k in range(B):
                last = nc.gpsimd.memset(v_bd[k][:, :, :], 0.0)
            last.then_inc(const_ok, 1)
            def weights_lo(g):
                pool.wait_ge(whi_ok, g + 1)
                cols = slice(g * W3, (g + 1) * W3)
                nc.gpsimd.tensor_tensor(wqkv_lo[:, cols], wqkv[:, cols], wqkv_hi[:, cols].bitcast(F32),
                                        ALU.subtract).then_inc(wlo_ok, 1)

            weights_lo(0)
            pool.wait_ge(head_gain_ok, 1)

            def slot(i, n):
                if isinstance(i, int) and i == 0 and n - 5 in WEIGHTS:
                    weights_lo(1 + WEIGHTS.index(n - 5))
                for u, t, tau in tiles_at(i, n, QK_SLOT, 3):
                    if t:
                        need(pool, norm_ok, i, TP, tau + 1)
                        q = qk[tau % 2][:, 0:GC].rearrange("p (h d) -> p h d", d=DH)
                        nc.gpsimd.tensor_tensor(q, q, head_gain[:, :].unsqueeze(1).broadcast_to([P, HG, DH]),
                                                ALU.mult).then_inc(gain_ok, 1)
                for u, t, tau in [x for lag in (4, 5) for x in tiles_at(i, n, QK_SLOT, lag)
                                  if is_first(i, x[0]) == (lag == 4)]:
                    rows, c0 = rows_cols(t)
                    need(pool, qkhi_ok, i, TP, tau + 1)
                    hl = qk_hl[tau % 2]
                    nc.gpsimd.tensor_tensor(
                        hl[0:rows, c0 // DH:8, 1, :], qk[tau % 2][0:rows, c0:512].rearrange("p (h d) -> p h d", d=DH),
                        hl[0:rows, c0 // DH:8, 0, :], ALU.subtract).then_inc(qklo_ok, 1)
                for k, is_ctx in steps_of(i, n - 3):
                    w = P if is_ctx else 512
                    need(pool, phi_ok, i, KP, k + 1)
                    need(pool, pv_ok, i, KP, k + 1 - SPLIT)
                    nc.gpsimd.tensor_tensor(p_lo[k % SPLIT][:, 0:w], p_raw[k % RAW][:, 0:w], p_hi[k % SPLIT][:, 0:w],
                                            ALU.subtract).then_inc(plo_ok, 1)

            run_slots(pool, slot)

            def expert_slot(i, n):
                e, half, c = expert_of(n + 2)
                if (n + 2) % 4 == 0 and is_slot(i, n + 2):
                    need(pool, wsp_hi, i, 4, 2 * e + 2)
                    need(pool, u_mm, i, XPER, 4 * (e - 1))
                    for k, w in enumerate((wg, wu)):
                        nc.gpsimd.tensor_tensor(wgu_lo[e % 2][:, k * F:(k + 1) * F], w[:, bass.ds(i * (2 * F) + e * F, F)],
                                                wgu_hi[e % 2][:, k * F:(k + 1) * F].bitcast(F32),
                                                ALU.subtract).then_inc(wsp_lo, 1)

            run_expert_slots(pool, expert_slot)

        @block.scalar
        def _(act):
            act.dma_start(gates[:, 0:1], g_xattn.partition_broadcast(P)).then_inc(gates_in, 16)
            act.dma_start(gates[:, 1:2], g_ffn.partition_broadcast(P)).then_inc(gates_in, 16)
            act.dma_start(ctx_sb[:, :], ctx_in.rearrange("b c d -> (b c) d")).then_inc(ctx_inn, 16)
            nc.scalar.preload_act_table_set("exp_and_others")
            act.wait_ge(gates_in, 32)
            nc.scalar.activation(gates_t[:, :], gates[:, :], ACT.Tanh).then_inc(gate_ok, 1)
            nc.scalar.preload_act_table_set("natural_log_exp_and_others")

            def rsqrt_start(c):
                r, n = CHAIN_ROWS[c], CHAIN_COLS[c]
                act.wait_ge(var_ok, c + 1)
                nc.scalar.activation(ln_l[0:r, c, 0:n], ln_v[0:r, c, 0:n], ACT.Ln).then_inc(lnl_ok, 1)
                act.wait_ge(lnl_ok, c + 1)
                nc.scalar.activation(ln_e[0:r, c, 0:n], ln_l[0:r, c, 0:n], ACT.Exp, scale=-0.5).then_inc(lne_ok, 1)

            def weights_hi(g):
                act.wait_ge(w0_in if g == 0 else w_in, 32 if g == 0 else 48)
                nc.scalar.copy(wqkv_hi[:, g * W3:(g + 1) * W3], wqkv[:, g * W3:(g + 1) * W3]).then_inc(whi_ok, 1)

            rsqrt_start(CH_B0A)
            rsqrt_start(CH_CTX)
            weights_hi(0)
            rsqrt_start(CH_B0B)
            rsqrt_start(CH_B1A)
            act.wait_ge(gains_in, 16 * 7)

            def with_gain(k, bank, cols, g):
                act.wait_ge(zT_ok, k + 1)
                w = cols.stop - cols.start
                nc.scalar.activation(lnT[:, cols], bank[:, 0:w], ACT.Identity, scale=gains[:, g:g + 1],
                                     bias=gains[:, g + 1:g + 2]).then_inc(lnT_ok, 1)

            with_gain(0, turned, slice(B * N, B * N + B * C), 2)
            with_gain(1, proj_qk, slice(0, N), 0)
            rsqrt_start(CH_B1B)

            def evacuate(j):
                act.wait_ge(oT_mm, j + 1)
                used = j - 1 if j < 2 * QT + 2 else j - 3
                if used > 0:
                    act.wait_ge(y_mm, used)
                nc.scalar.copy(oT_half(j), turned_o(j)).then_inc(oTa_ok, 1)

            def second_rows(b):
                act.wait_ge(z2T_ok, b + 1)
                nc.scalar.copy(x2T[:, b * N:(b + 1) * N], (turned, attn_o)[b][:, :]).then_inc(x2T_ok, 1)
                act.wait_ge(x2T_ok, b + 1)
                nc.scalar.copy(x2T_hi[:, b * N:(b + 1) * N], x2T[:, b * N:(b + 1) * N]).then_inc(x2hi_ok, 1)

            def route_exp(b, k):
                tok = slice(b * QT, (b + 1) * QT)
                act.wait_ge(rt_exp_in, 2 * b + k + 1)
                o, a = (rs[:, 5, tok], rs[:, 4, tok]) if k else (rt[:, 1, tok, :], rt[:, 0, tok, :])
                nc.scalar.activation(o, a, ACT.Exp).then_inc(rt_exp, 1)

            def expert_weights_hi(i, e):
                need(act, u_mm, i, XPER, 4 * (e - 1))
                for k, w in enumerate((wg, wu)):
                    nc.scalar.copy(wgu_hi[e % 2][:, k * F:(k + 1) * F],
                                   w[:, bass.ds(i * (2 * F) + e * F, F)]).then_inc(wsp_hi, 1)

            def raw(i, k, w):
                need(act, pT_ok, i, KP, k + 1)
                need(act, plo_ok, i, KP, k + 1 - RAW)
                nc.scalar.copy(p_raw[k % RAW][:, 0:w], turned[:, 0:w]).then_inc(raw_ok, 1)

            def slot(i, n):
                if isinstance(i, int) and i == 0:
                    if n == BATCH1:
                        with_gain(2, turned, slice(N, B * N), 0)
                    if n in WEIGHTS:
                        weights_hi(1 + WEIGHTS.index(n))
                rms = list(tiles_at(i, n, QK_SLOT, 2))
                m = n - 1
                if is_item(i, m):
                    g = m // HG
                    need(act, max_ok, i, PER, m + 1)
                    need(act, pT_ok, i, KP, KSTEPS * (g - 1))
                    need(act, o_ok, i, GP, g - SUMS + 1)
                    nc.scalar.activation(probs[g % 2][:, m % HG, :], scores[m % 2][:, 0:KEYS], ACT.Exp,
                                         bias=neg_max[:, m % NM:m % NM + 1],
                                         accum_out=sums[:, g % SUMS, m % HG:m % HG + 1]).then_inc(exp_ok, 1)
                for u, t, tau in rms:
                    rows, c0 = rows_cols(t)
                    need(act, ms_ok, i, TP, tau + 1)
                    nc.scalar.activation(rms_l[0:rows, tau % 2, c0 // DH:8], meansq[0:rows, tau % 2, c0 // DH:8],
                                         ACT.Ln).then_inc(rl_ok, 1)
                for u, t, tau in rms:
                    rows, c0 = rows_cols(t)
                    need(act, rl_ok, i, TP, tau + 1)
                    nc.scalar.activation(rms_e[0:rows, tau % 2, c0 // DH:8], rms_l[0:rows, tau % 2, c0 // DH:8],
                                         ACT.Exp, scale=-0.5).then_inc(re_ok, 1)
                steps = list(steps_of(i, n - 2))
                if steps and steps[0][1]:
                    raw(i, steps[0][0], P)
                for u, t, tau in tiles_at(i, n, V_SLOT, 0):
                    rows, _ = rows_cols(t)
                    need(act, v_mm, i, TP, tau + 1)
                    if t == 0:
                        need(act, vbd_ok, i, 16 * HG * B, 16 * HG * (u - 1))
                        o = v_ctx[u % B][:, :, 0, :]
                        p = proj_v[0:C, 0:GC].rearrange("p (h d) -> p h d", d=DH)
                    else:
                        need(act, pv_ok, i, KP, KSTEPS * QT * (u - 1) - 1)
                        o = v_hl[u % B][:, 0, t - 1, :]
                        p = proj_v[:, 0:GC]
                    nc.scalar.activation(o, p, ACT.Copy, scale=V_SCALE).then_inc(vhi_ok, 1)
                for u, t, tau in tiles_at(i, n, QK_SLOT, 1):
                    rows, c0 = rows_cols(t)
                    need(act, qk_mm, i, TP, tau + 1)
                    need(act, ss_ok, i, TP, tau - 1)
                    nc.scalar.activation(squares[tau % 2][0:rows, c0:512], qk_bank(i, u, t)[0:rows, c0:512],
                                         ACT.Square).then_inc(sq_ok, 1)
                for u, t, tau in tiles_at(i, n, T_SLOT, 1):
                    need(act, qkT_ok, i, TP, tau + 1)
                    need(act, s_ok, i, PER, UNIT * (u - 1))
                    tr = turn_bank(i, u, t)
                    if t == 0:
                        nc.scalar.copy(k_st[u % B][:, :, N:KEYS],
                                       tr[:, 512:1024].rearrange("p (h c) -> p h c", c=P)[:, :, 0:C]).then_inc(qkst_ok, 1)
                    else:
                        cols = slice((t - 1) * P, t * P)
                        nc.scalar.copy(q_st[u % B][:, :, cols], tr[:, 0:512].rearrange("p (h c) -> p h c", c=P))
                        nc.scalar.copy(k_st[u % B][:, :, cols],
                                       tr[:, 512:1024].rearrange("p (h c) -> p h c", c=P)).then_inc(qkst_ok, 1)
                if steps and not steps[-1][1]:
                    raw(i, steps[-1][0], 512)
                for h in range(2):
                    for t in out_step(i, n, h):
                        evacuate(2 * t + h)
                if last_slots(i, n, 0):
                    rsqrt_start(CH_2A)

            run_slots(act, slot)

            act.wait_ge(moe_in, 48)
            expert_weights_hi(0, 0)
            for j in range(2 * QT, 2 * T):
                evacuate(j)
                if j == 2 * QT + 1:
                    second_rows(0)
                if j == 2 * QT + 5:
                    route_exp(0, 0)
            rsqrt_start(CH_2B)

            def expert_slot(i, n):
                e, half, c = expert_of(n + 2)
                if (n + 2) % 4 == 0 and is_slot(i, n + 2) and n != -2:
                    expert_weights_hi(i, e)
                if is_slot(i, n):
                    need(act, g_mm, i, XPER, n + 1)
                    need(act, gt_ok, i, XPER, n - 1)
                    nc.scalar.activation(th[n % 2][:, :], scores[n % 2][:, 0:512], ACT.Tanh, scale=0.5).then_inc(th_ok, 1)
                if isinstance(i, int) and i == 0 and n == 0:
                    second_rows(1)
                if isinstance(i, int) and i == 0 and n in (1, 3, 5):
                    route_exp((n - 1) // 2 if n < 5 else 1, (1, 0, 1)[n // 2])

            run_expert_slots(act, expert_slot)

        @block.vector
        def _(dve):
            def norm_stats(k, rows, src):
                nc.vector.bn_stats(stats[0:rows, k, :], src).then_inc(bn_ok, 1)

            def norm_moments(k, rows, done):
                dve.wait_ge(bn_ok, done)
                return nc.vector.bn_aggr(moments[0:rows, k, :], stats[0:rows, k, :])

            step = [0]

            def link(ins):
                step[0] += 1
                ins.then_inc(newton, 1)
                dve.wait_ge(newton, step[0])

            def rsqrt_finish(c):
                r, n = CHAIN_ROWS[c], CHAIN_COLS[c]
                v, e = ln_v[0:r, c, 0:n], ln_e[0:r, c, 0:n]
                a = [ln_t[0:r, c, k, 0:n] for k in range(3)]
                dve.wait_ge(lne_ok, c + 1)
                link(nc.vector.tensor_tensor(a[0], e, e, ALU.mult))
                link(nc.vector.tensor_tensor(a[1], a[0], v, ALU.mult))
                link(nc.vector.tensor_scalar(a[2], a[1], -0.5, 1.5, ALU.mult, ALU.add))
                link(nc.vector.tensor_tensor(ln_r[0:r, c, 0:n], a[2], e, ALU.mult))

            def first_norm(b, c):
                tiles = range(b * QT, (b + 1) * QT)
                dve.wait_ge(x_in if b == 0 else x_in2, 16)
                done = bn[0]
                for t in tiles:
                    norm_stats(t, P, x_sb[:, t, :])
                    bn[0] += 1
                for k, t in enumerate(tiles):
                    last = norm_moments(t, P, done + k + 1)
                link(last)
                nc.vector.tensor_scalar(ln_v[:, c, :], moments[:, b * QT:(b + 1) * QT, 1], LN_EPS, None,
                                        ALU.add).then_inc(var_ok, 1)

            def second_norm(b, c1, c2):
                var = moments[:, b * QT:(b + 1) * QT, 1]
                link(nc.vector.tensor_tensor(ln_t[:, c2, 0, :], ln_r[:, c1, :], ln_r[:, c1, :], ALU.mult))
                link(nc.vector.tensor_tensor(ln_t[:, c2, 1, :], ln_t[:, c2, 0, :], var, ALU.mult))
                nc.vector.tensor_scalar(ln_v[:, c2, :], ln_t[:, c2, 1, :], LN_EPS, None, ALU.add).then_inc(var_ok, 1)

            def normalise(b, c1, c2):
                link(nc.vector.tensor_tensor(ln_s[:, b * QT:(b + 1) * QT], ln_r[:, c1, :], ln_r[:, c2, :], ALU.mult))
                for t in range(b * QT, (b + 1) * QT):
                    nc.vector.tensor_scalar(z[:, t, :], x_sb[:, t, :], moments[:, t, 0:1], ln_s[:, t:t + 1],
                                            ALU.subtract, ALU.mult).then_inc(z_ok, 1)

            def split_ln(k, cols):
                dve.wait_ge(lnT_ok, k + 1)
                nc.vector.tensor_copy(lnT_hi[:, cols], lnT[:, cols]).then_inc(lnhi_ok, 1)
                dve.wait_ge(lnhi_ok, k + 1)
                nc.vector.tensor_tensor(lnT_lo[:, cols], lnT[:, cols], lnT_hi[:, cols].bitcast(F32),
                                        ALU.subtract).then_inc(lnlo_ok, 1)

            bn = [0]
            first_norm(0, CH_B0A)
            dve.wait_ge(ctx_inn, 16)
            norm_stats(T, B * C, ctx_sb[:, :])
            bn[0] += 1
            link(norm_moments(T, B * C, bn[0]))
            nc.vector.tensor_scalar(ln_v[0:B * C, CH_CTX, 0:1], moments[0:B * C, T, 1:2], LN_EPS, None,
                                    ALU.add).then_inc(var_ok, 1)
            rsqrt_finish(CH_B0A)
            second_norm(0, CH_B0A, CH_B0B)
            rsqrt_finish(CH_CTX)
            nc.vector.tensor_scalar(z[0:B * C, T, :], ctx_sb[:, :], moments[0:B * C, T, 0:1], ln_r[0:B * C, CH_CTX, 0:1],
                                    ALU.subtract, ALU.mult).then_inc(z_ok, 1)
            first_norm(1, CH_B1A)
            rsqrt_finish(CH_B0B)
            normalise(0, CH_B0A, CH_B0B)
            rsqrt_finish(CH_B1A)
            second_norm(1, CH_B1A, CH_B1B)
            dve.wait_ge(ident_h_ok, 1)
            nc.vector.tensor_copy(ident_h[:, :], ident[:, :]).then_inc(ident_h_ok, 1)
            dve.wait_ge(gains_in, 16 * 7)
            nc.vector.scalar_tensor_tensor(out=head_gain[:, :], in0=head_gains[:, 0, :], scalar=DH ** -0.5,
                                           in1=head_gains[:, 1, :], op0=ALU.mult, op1=ALU.mult).then_inc(head_gain_ok, 1)
            nc.vector.tensor_scalar(mask_row[:, :], mask_u8[:, :], 1.0, MASKED, ALU.subtract, ALU.mult).then_inc(mask_ok, 1)
            dve.wait_ge(const_ok, 1)
            split_ln(0, slice(B * N, B * N + B * C))
            split_ln(1, slice(0, N))
            rsqrt_finish(CH_B1B)
            normalise(1, CH_B1A, CH_B1B)

            def residual(t):
                dve.wait_ge(y_mm, 2 * t + 2)
                link(nc.vector.tensor_tensor(x1_t[:, t % 2, :], y_bank(t), bout_b[:, :], ALU.add))
                nc.vector.scalar_tensor_tensor(out=x1[:, t, :], in0=x1_t[:, t % 2, :], scalar=gates_t[:, 0:1],
                                               in1=x_sb[:, t, :], op0=ALU.mult, op1=ALU.add).then_inc(x1_ok, 1)
                dve.wait_ge(x1_ok, t + 1)
                norm_stats(t, P, x1[:, t, :])
                bn[0] += 1
                link(norm_moments(t, P, bn[0]))
                if t % QT == QT - 1:
                    b = t // QT
                    nc.vector.tensor_scalar(ln_v[:, CH_2A + b, :], moments[:, b * QT:(b + 1) * QT, 1], LN_EPS, None,
                                            ALU.add).then_inc(var_ok, 1)

            def second_z(b):
                for t in range(b * QT, (b + 1) * QT):
                    nc.vector.tensor_scalar(z[:, t, :], x1[:, t, :], moments[:, t, 0:1],
                                            ln_r[:, CH_2A + b, t % QT:t % QT + 1], ALU.subtract,
                                            ALU.mult).then_inc(z2_ok, 1)

            def second_lo(b):
                cols = slice(b * N, (b + 1) * N)
                dve.wait_ge(x2hi_ok, b + 1)
                nc.vector.tensor_tensor(x2T_lo[:, cols], x2T[:, cols], x2T_hi[:, cols].bitcast(F32),
                                        ALU.subtract).then_inc(x2lo_ok, 1)

            rstep = [0]

            def rlink(ins):
                rstep[0] += 1
                ins.then_inc(rt_step, 1)
                dve.wait_ge(rt_step, rstep[0])

            def route(b, phase):
                tok = slice(b * QT, (b + 1) * QT)
                fall = falling[:, :].unsqueeze(1).broadcast_to([P, QT, E])

                def r(k):
                    return rt[:, k, tok, :]

                def v(k):
                    return rs[:, k, tok]

                def over(k):
                    return v(k).unsqueeze(2).broadcast_to([P, QT, E])

                if phase == 0:
                    dve.wait_ge(logit_ok, QT * (b + 1))
                    rlink(nc.vector.tensor_reduce(r(3), logits(b).rearrange("p (t k e) -> p t e k", t=QT, k=2), AX_X,
                                                  ALU.add))
                    rlink(nc.vector.tensor_reduce(v(0), r(3), AX_X, ALU.max))
                    nc.vector.tensor_tensor(r(0), r(3), over(0), ALU.subtract).then_inc(rt_exp_in, 1)
                if phase == 1:
                    dve.wait_ge(rt_exp, 2 * b + 1)
                    rlink(nc.vector.tensor_reduce(v(1), r(1), AX_X, ALU.add))
                    rlink(nc.vector.reciprocal(v(2), v(1)))
                    rlink(nc.vector.tensor_tensor(r(4), r(1), over(2), ALU.mult))
                if phase in (1, 2):
                    second = phase - 1
                    prob, a, best, pos = r(8 if second else 4), 5 + 4 * second, 6 if second else 3, 7 if second else 0
                    rlink(nc.vector.tensor_reduce(v(best), prob, AX_X, ALU.max))
                    rlink(nc.vector.tensor_tensor(r(a), prob, over(best), ALU.is_ge))
                    rlink(nc.vector.tensor_tensor(r(a + 1), r(a), fall, ALU.mult))
                    rlink(nc.vector.tensor_reduce(v(pos), r(a + 1), AX_X, ALU.max))
                    rlink(nc.vector.tensor_tensor(r(a + 2), r(a + 1), over(pos), ALU.is_equal))
                    if second:
                        nc.vector.tensor_tensor(v(4), v(6), v(3), ALU.subtract).then_inc(rt_exp_in, 1)
                    else:
                        rlink(nc.vector.scalar_tensor_tensor(out=r(8), in0=r(7), scalar=-2.0, in1=prob, op0=ALU.mult,
                                                             op1=ALU.add))
                if phase == 3:
                    dve.wait_ge(rt_exp, 2 * b + 2)
                    rlink(nc.vector.tensor_scalar(v(0), v(5), 1.0, None, ALU.add))
                    rlink(nc.vector.reciprocal(v(1), v(0)))
                    rlink(nc.vector.tensor_scalar(v(2), v(1), gates_t[:, 1:2], 0.5, ALU.mult, ALU.mult))
                    rlink(nc.vector.tensor_tensor(v(7), v(2), v(5), ALU.mult))
                    rlink(nc.vector.tensor_tensor(r(13), r(7), over(2), ALU.mult))
                    rlink(nc.vector.tensor_tensor(r(14), r(11), over(7), ALU.mult))
                    nc.vector.tensor_tensor(w_tok[:, tok, :], r(13), r(14), ALU.add).then_inc(w_ok, 1)
                    dve.wait_ge(w_ok, b + 1)

            def newton_step(i, n, k):
                for u, t, tau in tiles_at(i, n, QK_SLOT, 2):
                    rows, c0 = rows_cols(t)
                    h0 = c0 // DH
                    e = rms_e[0:rows, tau % 2, h0:8]
                    a = [rms_t[0:rows, tau % 2, j, h0:8] for j in range(2)]
                    if k == 0:
                        need(dve, re_ok, i, TP, tau + 1)
                        nc.vector.tensor_tensor(a[0], e, meansq[0:rows, tau % 2, h0:8], ALU.mult).then_inc(rms_step, 1)
                    elif k == 1:
                        need(dve, rms_step, i, 3 * TP, 3 * tau + 1)
                        nc.vector.scalar_tensor_tensor(out=a[1], in0=a[0], scalar=-0.5, in1=e, op0=ALU.mult,
                                                       op1=ALU.mult).then_inc(rms_step, 1)
                    else:
                        need(dve, rms_step, i, 3 * TP, 3 * tau + 2)
                        nc.vector.scalar_tensor_tensor(out=rms_r[0:rows, tau % 2, h0:8], in0=a[1], scalar=1.5, in1=e,
                                                       op0=ALU.add, op1=ALU.mult).then_inc(rms_step, 1)

            def slot(i, n):
                if isinstance(i, int) and n == BATCH1:
                    split_ln(2, slice(N, B * N))
                if n % HG == 1 and is_item(i, n - 9):
                    g = (n - 9) // HG
                    need(dve, pv_ok, i, KP, KSTEPS * (g + 1))
                    need(dve, den_ok, i, 2 * GP, 2 * g + 2)
                    if g % QT == QT - 1 and (not isinstance(i, int) or B * i + g // QT + 2 < UNITS):
                        need(dve, vlo_ok, i, TP, TILES * (g // QT + 2) + 1)
                    u, qt = g // QT, g % QT
                    t = (u % B) * QT + qt
                    o = o_sb[:, bass.ds(i * GC + (t * INNER + (u // B) * GC), GC)].rearrange("p (h d) -> p h d", d=DH)
                    nc.vector.tensor_tensor(o, attn_o[:, 0:GC].rearrange("p (h d) -> p h d", d=DH),
                                            inv_sums[:, g % 2, :].unsqueeze(2).broadcast_to([P, HG, DH]),
                                            ALU.mult).then_inc(o_ok, 1)
                if is_item(i, n):
                    need(dve, s_ok, i, PER, n + 1)
                    need(dve, exp_ok, i, PER, n + 1 - NM)
                    nc.vector.tensor_reduce(neg_max[:, n % NM:n % NM + 1], scores[n % 2][:, 0:KEYS], AX_X, ALU.max,
                                            negate=True).then_inc(max_ok, 1)
                for k, is_ctx in steps_of(i, n - 3):
                    w = P if is_ctx else 512
                    need(dve, raw_ok, i, KP, k + 1)
                    need(dve, pv_ok, i, KP, k + 1 - SPLIT)
                    nc.vector.tensor_copy(p_hi[k % SPLIT][:, 0:w], p_raw[k % RAW][:, 0:w]).then_inc(phi_ok, 1)
                newton_step(i, n, 0)
                if n % HG == 1 and is_item(i, n - 2):
                    g = (n - 2) // HG
                    need(dve, exp_ok, i, PER, n - 1)
                    need(dve, pT_ok, i, KP, KSTEPS * (g - 1))
                    nc.vector.tensor_copy(probs_c[g % 2][:, :].rearrange("p (h c) -> p h c", c=C),
                                          probs[g % 2][:, :, N:KEYS]).then_inc(pack_ok, 1)
                if n % HG == 2 and is_item(i, n - 3):
                    g = (n - 3) // HG
                    need(dve, exp_ok, i, PER, n - 2)
                    nc.vector.tensor_scalar(sums_s[:, g % 2, :], sums[:, g % SUMS, :], V_SCALE, None,
                                            ALU.mult).then_inc(den_ok, 1)
                newton_step(i, n, 1)
                for u, t, tau in tiles_at(i, n, V_SLOT, 0):
                    need(dve, vhi_ok, i, TP, tau + 1)
                    if t == 0:
                        hi, lo = v_ctx[u % B][:, :, 0, :], v_ctx[u % B][:, :, 1, :]
                        p = proj_v[0:C, 0:GC].rearrange("p (h d) -> p h d", d=DH)
                    else:
                        hi, lo = v_hl[u % B][:, 0, t - 1, :], v_hl[u % B][:, 1, t - 1, :]
                        p = proj_v[:, 0:GC]
                    nc.vector.scalar_tensor_tensor(out=lo, in0=p, scalar=V_SCALE, in1=hi, op0=ALU.mult,
                                                   op1=ALU.subtract).then_inc(vlo_ok, 1)
                newton_step(i, n, 2)
                if n % HG == 2 and is_item(i, n - 3):
                    g = (n - 3) // HG
                    need(dve, den_ok, i, 2 * GP, 2 * g + 1)
                    need(dve, o_ok, i, GP, g - 1)
                    nc.vector.reciprocal(inv_sums[:, g % 2, :], sums_s[:, g % 2, :]).then_inc(den_ok, 1)
                for u, t, tau in tiles_at(i, n, QK_SLOT, 2):
                    rows, c0 = rows_cols(t)
                    need(dve, rms_step, i, 3 * TP, 3 * tau + 3)
                    need(dve, qklo_ok, i, TP, tau - 1)
                    nc.vector.tensor_tensor(qk[tau % 2][0:rows, c0:512].rearrange("p (h d) -> p h d", d=DH),
                                            qk_bank(i, u, t)[0:rows, c0:512].rearrange("p (h d) -> p h d", d=DH),
                                            rms_r[0:rows, tau % 2, c0 // DH:8].unsqueeze(2).broadcast_to(
                                                [rows, 8 - c0 // DH, DH]), ALU.mult).then_inc(norm_ok, 1)
                for u, t, tau in tiles_at(i, n, QK_SLOT, 3):
                    rows, c0 = rows_cols(t)
                    if t:
                        need(dve, gain_ok, i, B * QT, QT * u + t)
                    else:
                        need(dve, norm_ok, i, TP, tau + 1)
                    need(dve, qkT_ok, i, TP, tau - 1)
                    nc.vector.tensor_copy(qk_hl[tau % 2][0:rows, c0 // DH:8, 0, :],
                                          qk[tau % 2][0:rows, c0:512].rearrange("p (h d) -> p h d", d=DH)).then_inc(qkhi_ok, 1)
                for u, t, tau in tiles_at(i, n, QK_SLOT, 1):
                    rows, c0 = rows_cols(t)
                    h0 = c0 // DH
                    need(dve, sq_ok, i, TP, tau + 1)
                    need(dve, norm_ok, i, TP, tau - 1)
                    nc.vector.tensor_reduce(sumsq[0:rows, tau % 2, h0:8],
                                            squares[tau % 2][0:rows, c0:512].rearrange("p (h d) -> p h d", d=DH),
                                            AX_X, ALU.add).then_inc(ss_ok, 1)
                    need(dve, ss_ok, i, TP, tau + 1)
                    nc.vector.tensor_scalar(meansq[0:rows, tau % 2, h0:8], sumsq[0:rows, tau % 2, h0:8], 1.0 / DH,
                                            RMS_EPS ** 2, ALU.mult, ALU.max).then_inc(ms_ok, 1)
                if last_slots(i, n, 2):
                    rsqrt_finish(CH_2A)
                    second_z(0)
                for t in out_step(i, n, 0):
                    if t == 0:
                        dve.wait_ge(rest_in, 16 * 3)
                        nc.vector.tensor_copy(wr_hl[:, 0, :], wr[:, :]).then_inc(wr_ok, 1)
                        dve.wait_ge(wr_ok, 1)
                        nc.vector.tensor_tensor(wr_hl[:, 1, :], wr[:, :], wr_hl[:, 0, :].bitcast(F32),
                                                ALU.subtract).then_inc(wr_ok, 1)
                        dve.wait_ge(gate_ok, 1)
                for t in out_step(i, n, 3):
                    residual(t)

            run_slots(dve, slot)

            second_lo(0)
            for t in range(QT, T):
                residual(t)
                if t < QT + 2:
                    route(0, t - QT)
            rsqrt_finish(CH_2B)
            second_z(1)

            def expert_slot(i, n):
                if is_slot(i, n):
                    need(dve, th_ok, i, XPER, n + 1)
                    need(dve, hid_ok, i, XPER, n - 1)
                    nc.vector.scalar_tensor_tensor(out=gt[n % 2][:, :], in0=th[n % 2][:, :], scalar=1.0,
                                                   in1=scores[n % 2][:, 0:512], op0=ALU.add,
                                                   op1=ALU.mult).then_inc(gt_ok, 1)
                    need(dve, gt_ok, i, XPER, n + 1)
                    need(dve, u_mm, i, XPER, n + 1)
                    need(dve, d_mm, i, XPER, n - 1)
                    nc.vector.tensor_tensor(hid[n % 2][:, :], gt[n % 2][:, :], scores[n % 2][:, 512:1024],
                                            ALU.mult).then_inc(hid_ok, 1)
                if isinstance(i, int) and i == 0 and 0 <= n <= 5:
                    if n == 0:
                        second_lo(1)
                    route((0, 0, 1, 1, 1, 1)[n], (2, 3, 0, 1, 2, 3)[n])
                m = n - 2
                if is_slot(i, m) and m % FC == FC - 1:
                    e, half, _ = expert_of(m)
                    need(dve, d_mm, i, XPER, m + 1)
                    for k in range(QT):
                        t = half * QT + k
                        need(dve, y_ok, i, 2 * T, T * (e - 1) + t + 1)
                        nc.vector.scalar_tensor_tensor(
                            out=x1[:, t, :], in0=(turned, attn_o)[half][:, k * D:(k + 1) * D],
                            scalar=w_tok[:, t, bass.ds(i * 2 + e, 1)], in1=x1[:, t, :], op0=ALU.mult,
                            op1=ALU.add).then_inc(y_ok, 1)

            run_expert_slots(dve, expert_slot)

        @block.tensor
        def _(pe):
            pe.wait_ge(ident_h_ok, 1)
            pe.wait_ge(z_ok, 1)
            nc.tensor.transpose(turned[:, 0:B * C], z[0:B * C, T, :], ident[0:B * C, 0:B * C]).then_inc(zT_ok, 1)
            def turn_rows(b, bank):
                for t in range(QT):
                    pe.wait_ge(z_ok, 1 + b * QT + t + 1)
                    last = nc.tensor.transpose(bank[:, t * P:(t + 1) * P], z[:, b * QT + t, :], ident[:, :])
                last.then_inc(zT_ok, 1)

            turn_rows(0, proj_qk)
            pe.wait_ge(ident_h_ok, 2)
            pe.wait_ge(mask_ok, 1)

            def project(i, u, t, out_ap, c0, cols):
                first = B * N + (u % B) * C if t == 0 else (u % B) * N + (t - 1) * P
                toks = slice(first, first + P)
                w = bass.ds(i * W3 + ((u // B) * W3 + c0), cols)
                nc.tensor.matmul(out_ap, lnT_hi[:, toks], wqkv_hi[:, w], start=True, stop=False)
                nc.tensor.matmul(out_ap, lnT_hi[:, toks], wqkv_lo[:, w], start=False, stop=False)
                return nc.tensor.matmul(out_ap, lnT_lo[:, toks], wqkv_hi[:, w], start=False, stop=True)

            def proj_v_free(i, u, s):
                jobs = sorted([(a, 0, t) for t, a in enumerate(V_SLOT)] + [(a, 1, t) for t, a in enumerate(T_SLOT)])
                k = jobs.index(s)
                v, (_, kind, t) = (u, jobs[k - 1]) if k else (u - 1, jobs[-1])
                need(pe, (vlo_ok, qkst_ok)[kind], i, TP, TILES * v + t + 1)

            def times_values(i, k, cols, o, vh, vl, wait, start, stop):
                hi, lo = p_hi[k % SPLIT], p_lo[k % SPLIT]
                if wait:
                    need(pe, phi_ok, i, KP, k + 1)
                nc.tensor.matmul(o, hi[:, cols], vh, start=start, stop=False, skip_group_check=True)
                nc.tensor.matmul(o, hi[:, cols], vl, start=False, stop=False, skip_group_check=True)
                if wait:
                    need(pe, plo_ok, i, KP, k + 1)
                return nc.tensor.matmul(o, lo[:, cols], vh, start=False, stop=stop, skip_group_check=True)

            def turn_o(j):
                t = j // 2
                if j == 0:
                    pe.wait_ge(o_ok, NG * T - QT)
                    pe.wait_ge(v_mm, TILES * UNITS)
                    pe.wait_ge(vlo_ok, TILES * UNITS)
                elif j < 2 * QT:
                    pe.wait_ge(oTa_ok, j)
                elif j == 2 * QT:
                    pe.wait_ge(o_ok, NG * T)
                    pe.wait_ge(exp_ok, ITEMS)
                elif j >= 2 * QT + 4:
                    pe.wait_ge(oTa_ok, j - 3)
                for c in range(H // 4):
                    first = t * INNER + (j % 2) * HALF + c * P
                    last = nc.tensor.transpose(turned_o(j)[:, c * P:(c + 1) * P], o_sb[:, first:first + P], ident[:, :])
                last.then_inc(oT_mm, 1)

            def project_o(j):
                t, h = j // 2, j % 2
                pe.wait_ge(oTa_ok, j + 1)
                if j == 0:
                    pe.wait_ge(rest_in, 16 * 3)
                    pe.wait_ge(norm_ok, TILES * UNITS)
                elif h == 0:
                    pe.wait_ge(x1_ok, t if t <= QT else t - 1)
                for c in range(H // 4):
                    last = nc.tensor.matmul(y_bank(t), oT_half(j)[:, c * P:(c + 1) * P], wout[:, h * (H // 4) + c, :],
                                            start=(h == 0 and c == 0), stop=(h == 1 and c == H // 4 - 1))
                last.then_inc(y_mm, 1)

            def turn_rows2(b):
                pe.wait_ge(raw_ok, NG * KP)
                for t in range(QT):
                    pe.wait_ge(z2_ok, b * QT + t + 1)
                    last = nc.tensor.transpose((turned, attn_o)[b][:, t * P:(t + 1) * P], z[:, b * QT + t, :], ident[:, :])
                last.then_inc(z2T_ok, 1)

            def router_logits(b):
                pe.wait_ge(x2lo_ok, b + 1)
                pe.wait_ge(wr_ok, 2)
                if b:
                    pe.wait_ge(x1_ok, T)
                r = wr_hl[:, :, :].rearrange("p k e -> p (k e)")
                for t in range(QT):
                    o = logits(b)[:, t * 2 * E:(t + 1) * 2 * E]
                    toks = slice((b * QT + t) * P, (b * QT + t + 1) * P)
                    nc.tensor.matmul(o, x2T_hi[:, toks], r, start=True, stop=False)
                    nc.tensor.matmul(o, x2T_lo[:, toks], r, start=False, stop=True).then_inc(logit_ok, 1)

            def slot(i, n):
                if isinstance(i, int) and n == BATCH1:
                    pe.wait_ge(lnT_ok, 1)
                    turn_rows(1, turned)
                if (n - 5) % HG == 0 and is_item(i, n - 6):
                    u = (n - 6) // UNIT
                    if (n - 6) % UNIT == HG - 1:
                        need(pe, vbd_ok, i, 16 * HG * B, 16 * HG * (u + 1))
                    times_values(i, KSTEPS * ((n - 5) // HG) - 1, slice(0, P), attn_o[:, 0:GC], v_bd[u % B][:, 0, :],
                                 v_bd[u % B][:, 1, :], True, False, True).then_inc(pv_ok, 1)
                if is_item(i, n):
                    u, qt, h = n // UNIT, (n % UNIT) // HG, n % HG
                    b = u % B
                    if n % UNIT == 0:
                        need(pe, qkst_ok, i, TP, TILES * (u + 1))
                        need(pe, ksw_ok, i, 32 * B, 32 * (u + 1))
                    need(pe, exp_ok, i, PER, n - 1)
                    q = q_st[b][:, h, qt * P:(qt + 1) * P]
                    s = scores[n % 2]
                    nc.tensor.matmul(s[:, 0:N], q, k_st[b][:, h, 0:N], start=True, stop=False)
                    nc.tensor.matmul(s[:, N:KEYS], q, k_st[b][:, h, N:KEYS], start=True, stop=False)
                    nc.tensor.matmul(s[:, 0:N], q, k_sw[b][:, h, 0:N], start=False, stop=True)
                    nc.tensor.matmul(s[:, N:KEYS], q, k_sw[b][:, h, N:KEYS], start=False, stop=False)
                    nc.tensor.matmul(s[:, N:KEYS], ones_row[:, :], mask_row[:, b * C:(b + 1) * C], start=False,
                                     stop=True).then_inc(s_ok, 1)
                for u, t, tau in tiles_at(i, n, V_SLOT, 0):
                    if not is_first(i, u):
                        proj_v_free(i, u, (V_SLOT[t], 0, t))
                    elif t:
                        need(pe, vlo_ok, i, TP, tau)
                    project(i, u, t, proj_v[:, 0:GC], 2 * GC, GC).then_inc(v_mm, 1)
                if (n - 2) % HG == 0 and is_item(i, n - 3):
                    g = (n - 3) // HG
                    need(pe, pack_ok, i, GP, g + 1)
                    need(pe, raw_ok, i, KP, KSTEPS * g + HG)
                    nc.tensor.transpose(turned[:, 0:P], probs_c[g % 2][:, :], ident[:, :]).then_inc(pT_ok, 1)
                if is_item(i, n - 2):
                    m = n - 2
                    k = KSTEPS * (m // HG) + m % HG
                    need(pe, exp_ok, i, PER, m + 1)
                    need(pe, raw_ok, i, KP, k)
                    for c in range(QT):
                        last = nc.tensor.transpose(turned[:, c * P:(c + 1) * P],
                                                   probs[(m // HG) % 2][:, m % HG, c * P:(c + 1) * P], ident[:, :])
                    last.then_inc(pT_ok, 1)
                for u, t, tau in tiles_at(i, n, QK_SLOT, 0):
                    need(pe, wlo_ok, i, 1, u // B + 1)
                    if isinstance(i, int) and i == 0 and u < B:
                        pe.wait_ge(lnlo_ok, (2 if u == 0 else 3) if t else 1)
                        if u == 0 and t == TILES - 1:
                            pe.wait_ge(lnT_ok, 2)
                    if not is_first(i, u):
                        need(pe, norm_ok, i, TP, tau)
                    _, c0 = rows_cols(t)
                    project(i, u, t, qk_bank(i, u, t)[:, c0:512], c0, 2 * GC - c0).then_inc(qk_mm, 1)
                for u, t, tau in tiles_at(i, n, T_SLOT, 0):
                    if not is_first(i, u):
                        proj_v_free(i, u, (T_SLOT[t], 1, t))
                    elif t == 1:
                        pe.wait_ge(lnT_ok, 3)
                    elif t > 1:
                        need(pe, qkst_ok, i, TP, tau - 1)
                    need(pe, qklo_ok, i, TP, tau + 1)
                    _, c0 = rows_cols(t)
                    tr = turn_bank(i, u, t)
                    for j in range(c0 // DH, 8):
                        last = nc.tensor.transpose(tr[:, j * P:(j + 1) * P], qk_hl[tau % 2][:, j, :, :], ident_h[:, :])
                    last.then_inc(qkT_ok, 1)
                for h in range(2):
                    for t in out_step(i, n, h + 1):
                        project_o(2 * t + h)
                    for t in out_step(i, n, h):
                        turn_o(2 * t + h)
                if is_item(i, n - 5):
                    m = n - 5
                    u, h = m // UNIT, m % HG
                    if m % UNIT == 0:
                        need(pe, vlo_ok, i, TP, TILES * (u + 1))
                    if h == 0:
                        need(pe, o_ok, i, GP, m // HG)
                    k = KSTEPS * (m // HG) + h
                    for c in range(QT):
                        vh, vl = (v_hl[u % B][:, part, c, h * DH:(h + 1) * DH] for part in range(2))
                        last = times_values(i, k, slice(c * P, (c + 1) * P), attn_o[:, h * DH:(h + 1) * DH], vh, vl,
                                            c == 0, h == 0 and c == 0, False)
                    last.then_inc(pv_ok, 1)

            run_slots(pe, slot)

            for h in range(2):
                turn_o(2 * QT + h)
            turn_rows2(0)
            for t in range(QT, T):
                if t + 1 < T:
                    for h in range(2):
                        turn_o(2 * t + 2 + h)
                for h in range(2):
                    project_o(2 * t + h)
                if t == QT:
                    router_logits(0)
            pe.wait_ge(moe_in, 48)

            def expert_slot(i, n):
                if isinstance(i, int) and i == 0 and n == 2:
                    router_logits(1)
                if is_slot(i, n):
                    e, half, c = expert_of(n)
                    toks = slice(half * N, (half + 1) * N)
                    if n % 4 == 0:
                        need(pe, wsp_lo, i, 4, 2 * e + 2)
                    if isinstance(i, int) and i == 0 and n < 4:
                        pe.wait_ge(x2lo_ok, half + 1)
                    need(pe, hid_ok, i, XPER, n - 1)
                    for k, done in enumerate((g_mm, u_mm)):
                        o = scores[n % 2][:, k * 512:(k + 1) * 512]
                        w = slice(k * F + c * P, k * F + (c + 1) * P)
                        nc.tensor.matmul(o, wgu_hi[e % 2][:, w], x2T_hi[:, toks], start=True, stop=False)
                        nc.tensor.matmul(o, wgu_hi[e % 2][:, w], x2T_lo[:, toks], start=False, stop=False)
                        nc.tensor.matmul(o, wgu_lo[e % 2][:, w], x2T_hi[:, toks], start=False,
                                         stop=True).then_inc(done, 1)
                if isinstance(i, int) and i == 0 and n == 1:
                    turn_rows2(1)
                m = n - 1
                if is_slot(i, m):
                    e, half, c = expert_of(m)
                    need(pe, hid_ok, i, XPER, m + 1)
                    if c == 0:
                        need(pe, y_ok, i, 2 * T, T * (e - 1) + (half + 1) * QT)
                        if isinstance(i, int) and i == 0 and m < 4:
                            pe.wait_ge(rt_step, 1)
                    for k in range(QT):
                        last = nc.tensor.matmul((turned, attn_o)[half][:, k * D:(k + 1) * D],
                                                hid[m % 2][:, k * P:(k + 1) * P],
                                                wd[:, bass.ds(i * (2 * FC * D) + (e * FC + c) * D, D)],
                                                start=(c == 0 and k == 0), stop=(c == FC - 1), skip_group_check=True)
                    last.then_inc(d_mm, 1)

            run_expert_slots(pe, expert_slot)


_INS = ['x', 'ctx_1024', 'mask_BxS2_bf1', 'g_xattn', 'g_ffn', 'L0_xattn_ln_x_g', 'L0_xattn_ln_x_b', 'L0_xattn_ln_l_g',
        'L0_xattn_ln_l_b', 'L0_xattn_qn_g', 'L0_xattn_kn_g', 'L0_xattn_Wq', 'L0_xattn_Wkv', 'L0_xattn_Wout',
        'L0_xattn_bout', 'L0_ffn_kernel_router_DE', 'L0_ffn_kernel_gating_EDF', 'L0_ffn_kernel_up_EDF',
        'L0_ffn_kernel_down_EFD']
_OUTS = [((2, 512, 128), 'float32')]


def kernel(**inputs):
    import numpy as _np
    import concourse.bacc as _bacc
    from concourse import mybir as _mybir
    from concourse.bass_utils import run_bass_kernel_spmd as _run

    nc = _bacc.Bacc("TRN2", target_bir_lowering=False, num_devices=1)
    arrays, args = {}, []
    for name in _INS:
        a = _np.ascontiguousarray(inputs[name])
        arrays[f"in_{name}_dram"] = a
        args.append(nc.dram_tensor(f"in_{name}_dram", a.shape, _mybir.dt.from_np(a.dtype), kind="ExternalInput").ap())
    for k, (shape, dtype) in enumerate(_OUTS):
        dt = _mybir.dt.from_np(_np.dtype(dtype))
        args.append(nc.dram_tensor(f"out_{k}_dram", shape, dt, kind="ExternalOutput").ap())
    flamingo_gated_block(nc, *args)
    r = _run(nc, [arrays], core_ids=[0])
    got = tuple(r.results[0][f"out_{k}_dram"] for k in range(len(_OUTS)))
    return got[0]
```
